# Optimizing a Trainium2 kernel written in Bass

```python
import numpy as np
import jax
import jax.numpy as jnp

def _softmax(x, axis=-1):
    return jax.nn.softmax(x, axis=axis)

def _gelu(x):
    return jax.nn.gelu(x, approximate=True)

def _silu(x):
    return jax.nn.silu(x)

def _sigmoid(x):
    return jax.nn.sigmoid(x)

def _layernorm(x, axis=-1, eps=1e-05):
    m = jnp.mean(x, axis=axis, keepdims=True)
    v = jnp.var(x, axis=axis, keepdims=True)
    return (x - m) / jnp.sqrt(v + eps)

def _scatter_add(tgt, idx, src, axis=0):
    return tgt.at[idx].add(src)

def _segment_sum(src, seg, n):
    return jax.ops.segment_sum(src, seg, n)
kernel_name = 'mk_seq_preln_d1_jaxref_r4_ae8c2d'

def setup_inputs(seed: int=0):
    np.random.seed(seed)
    _w = jnp.asarray

    def _L0_attn_setup():
        import jax, jax.numpy as jnp
        import numpy as np
        B, N, DIM, H = (2, 512, 256, 16)
        DH = DIM // H
        SCALE = DH ** (-0.5)

        def _rotary_emb(n, d, dtype):
            inv_freq = 1.0 / 10000.0 ** (jnp.arange(0, d, 2, dtype=jnp.float32) / d)
            freqs = jnp.outer(jnp.arange(n, dtype=jnp.float32), inv_freq)
            return jnp.concatenate([freqs, freqs], axis=-1).astype(dtype)

        def _rotate_half(x):
            x1, x2 = jnp.split(x, 2, axis=-1)
            return jnp.concatenate([-x2, x1], axis=-1)

        def _apply_rotary(freqs, t):
            return t * jnp.cos(freqs) + _rotate_half(t) * jnp.sin(freqs)
        key = jax.random.key(seed)
        ks = jax.random.split(key, 4)
        x = jax.random.normal(ks[0], (B, N, DIM), dtype=jnp.float32)
        Wq = jax.random.normal(ks[1], (DIM, DIM), dtype=jnp.float32) * DIM ** (-0.5)
        Wkv = jax.random.normal(ks[2], (DIM, DIM), dtype=jnp.float32) * DIM ** (-0.5)
        Wout = jax.random.normal(ks[3], (DIM, DIM), dtype=jnp.float32) * DIM ** (-0.5)
        bout = jnp.zeros((DIM,), dtype=jnp.float32)
        return {'x': x, 'Wq': Wq, 'Wkv': Wkv, 'Wout': Wout, 'bout': bout}
    _L0_attn_in = _L0_attn_setup()

    def _L0_ffn_setup():
        import jax, jax.numpy as jnp
        import numpy as np
        B, S, D = (4, 1024, 256)
        DD = 4 * D
        N_EXPERTS = 8
        CAPACITY = 1.0
        LN_EPS = 1e-05
        key = jax.random.key(seed)
        ks = jax.random.split(key, 8)
        s1 = 1.0 / np.sqrt(D)
        s2 = 1.0 / np.sqrt(DD)
        return {'x': jax.random.normal(ks[0], (B, S, D), jnp.float32), 'gate_w': jax.random.normal(ks[1], (N_EXPERTS, D), jnp.float32) * 0.02, 'ln_w': jnp.ones((D,), jnp.float32), 'ln_b': jnp.zeros((D,), jnp.float32), 'fc1s': jax.random.normal(ks[2], (N_EXPERTS, DD, D), jnp.float32) * s1, 'b1s': jax.random.normal(ks[3], (N_EXPERTS, DD), jnp.float32) * s1, 'fc2s': jax.random.normal(ks[4], (N_EXPERTS, D, DD), jnp.float32) * s2, 'b2s': jax.random.normal(ks[5], (N_EXPERTS, D), jnp.float32) * s2}
    _L0_ffn_in = _L0_ffn_setup()
    _d = {'L0_attn_x': _L0_attn_in['x'], 'L0_attn_Wq': _L0_attn_in['Wq'], 'L0_attn_Wkv': _L0_attn_in['Wkv'], 'L0_attn_Wout': _L0_attn_in['Wout'], 'L0_attn_bout': _L0_attn_in['bout'], 'L0_ffn_gate_w': _L0_ffn_in['gate_w'], 'L0_ffn_ln_w': _L0_ffn_in['ln_w'], 'L0_ffn_ln_b': _L0_ffn_in['ln_b'], 'L0_ffn_fc1s': _L0_ffn_in['fc1s'], 'L0_ffn_b1s': _L0_ffn_in['b1s'], 'L0_ffn_fc2s': _L0_ffn_in['fc2s'], 'L0_ffn_b2s': _L0_ffn_in['b2s']}
    _x0 = _d['L0_attn_x']
    _d['L0_attn_x'] = jax.random.normal(jax.random.fold_in(jax.random.key(seed), 1), (8, 1024, 256), dtype=_x0.dtype)
    del _x0
    return _d

def reference(L0_attn_x, L0_attn_Wq, L0_attn_Wkv, L0_attn_Wout, L0_attn_bout, L0_ffn_gate_w, L0_ffn_ln_w, L0_ffn_ln_b, L0_ffn_fc1s, L0_ffn_b1s, L0_ffn_fc2s, L0_ffn_b2s):

    def _L0_attn_ref(x, Wq, Wkv, Wout, bout):
        import jax, jax.numpy as jnp
        import numpy as np
        B, N, DIM, H = (2, 512, 256, 16)
        DH = DIM // H
        SCALE = DH ** (-0.5)

        def _rotary_emb(n, d, dtype):
            inv_freq = 1.0 / 10000.0 ** (jnp.arange(0, d, 2, dtype=jnp.float32) / d)
            freqs = jnp.outer(jnp.arange(n, dtype=jnp.float32), inv_freq)
            return jnp.concatenate([freqs, freqs], axis=-1).astype(dtype)

        def _rotate_half(x):
            x1, x2 = jnp.split(x, 2, axis=-1)
            return jnp.concatenate([-x2, x1], axis=-1)

        def _apply_rotary(freqs, t):
            return t * jnp.cos(freqs) + _rotate_half(t) * jnp.sin(freqs)
        b, n, dim = x.shape
        q = x @ Wq
        kv = x @ Wkv
        split = lambda t: t.reshape(b, n, H, DH).transpose(0, 2, 1, 3).reshape(b * H, n, DH)
        q, kv = (split(q), split(kv))
        freqs = _rotary_emb(n, DH, x.dtype)[None]
        q = _apply_rotary(freqs, q)
        kv = _apply_rotary(freqs, kv)
        q = q * SCALE
        att = jnp.einsum('bmd,bnd->bmn', q, kv)
        attn = jax.nn.softmax(att, axis=-1)
        out = jnp.einsum('bij,bjd->bid', attn, kv)
        out = out.reshape(b, H, n, DH).transpose(0, 2, 1, 3).reshape(b, n, dim)
        return out @ Wout + bout

    def _L0_ffn_ref(x, gate_w, ln_w, ln_b, fc1s, b1s, fc2s, b2s):
        import jax, jax.numpy as jnp
        import numpy as np
        B, S, D = (4, 1024, 256)
        DD = 4 * D
        N_EXPERTS = 8
        CAPACITY = 1.0
        LN_EPS = 1e-05
        og_shape = x.shape
        d = og_shape[-1]
        xf = x.reshape(-1, d)
        bs = xf.shape[0]
        n = gate_w.shape[0]
        k = int(bs * CAPACITY) // n
        scores = jax.nn.softmax(xf @ gate_w.T, axis=-1)
        vals, idx = jax.lax.top_k(scores.T, k)
        kept_w = vals.T
        kept_idx = idx.T
        flat_idx = kept_idx.reshape(-1)
        y = xf[flat_idx].reshape(k, n, d)
        mu = y.mean(-1, keepdims=True)
        var = ((y - mu) ** 2).mean(-1, keepdims=True)
        y = (y - mu) * jax.lax.rsqrt(var + LN_EPS) * ln_w + ln_b
        h = jnp.einsum('knd,nfd->knf', y, fc1s) + b1s
        h = jax.nn.gelu(h, approximate=True)
        out = jnp.einsum('knf,ndf->knd', h, fc2s) + b2s
        out = out * kept_w[..., None]
        xf = xf.at[flat_idx].add(out.reshape(k * n, d))
        return xf.reshape(og_shape)
    x = L0_attn_x
    x = x + _L0_attn_ref(_layernorm(x, axis=-1), L0_attn_Wq, L0_attn_Wkv, L0_attn_Wout, L0_attn_bout)
    x = x + _L0_ffn_ref(_layernorm(x, axis=-1), L0_ffn_gate_w, L0_ffn_ln_w, L0_ffn_ln_b, L0_ffn_fc1s, L0_ffn_b1s, L0_ffn_fc2s, L0_ffn_b2s)
    return x

_drawn_inputs = setup_inputs


def setup_inputs(seed=0):
    import zlib

    import numpy as np

    out = dict(_drawn_inputs(seed))
    spreads = {'L0_attn_bout': (0.0, 0.1), 'L0_ffn_ln_w': (1.0, 0.6), 'L0_ffn_ln_b': (0.0, 0.8)}
    factors = {'L0_ffn_b1s': 8.0, 'L0_ffn_b2s': 8.0}
    for name, (base, spread) in spreads.items():
        noise = np.random.default_rng([zlib.crc32(name.encode()), seed]).standard_normal(out[name].shape)
        drawn = base * np.exp(spread * noise) if base else spread * noise
        out[name] = jnp.asarray(drawn.astype(out[name].dtype))
    for name, factor in factors.items():
        out[name] = (out[name] * factor).astype(out[name].dtype)
    return out
```

```python
from contextlib import ExitStack

import numpy as np

import concourse.bass as bass
from concourse import mybir

F32 = mybir.dt.float32
BF16 = mybir.dt.bfloat16
I32 = mybir.dt.int32
U32 = mybir.dt.uint32
ALU = mybir.AluOpType
ACT = mybir.ActivationFunctionType
AX = mybir.AxisListType

P = 128
B, N, D = 8, 1024, 256
H, DH = 16, 16
TILES = N // P
TOK = B * N
DC = D // P
HALF = DH // 2
PAIRS = H // 2
NP = B * PAIRS
PARTS = 3
EPS = 1e-5
E, FF = 8, 1024
K = TOK // E
FC = FF // P
ROW = D + E


class Alloc:

    def __init__(self, nc, ctx):
        self.nc, self.ctx = nc, ctx

    def sb(self, name, shape, dt=F32):
        return self.ctx.enter_context(self.nc.sbuf_tensor(name, shape, dt))

    def ps(self, name, shape, dt=F32):
        return self.ctx.enter_context(self.nc.psum_tensor(name, shape, dt))

    def sem(self, name):
        return self.ctx.enter_context(self.nc.semaphore(name))


def project(nc, x, w_qkv, rot_cos, rot_sin, ident_d, parts_dram, v_dram):
    SEQS = 2
    with ExitStack() as ctx:
        a = Alloc(nc, ctx)
        ident = a.sb("p_ident", [P, P])
        w = a.sb("p_w", [P, DC, 2 * D])
        cosb = a.sb("p_cos", [P, TILES, DH])
        sinb = a.sb("p_sin", [P, TILES, DH])
        xb = a.sb("p_x", [P, SEQS, TILES, D])
        stats = a.sb("p_stats", [P, SEQS, TILES, 6])
        mv = a.sb("p_mv", [P, SEQS, TILES, 2])
        veps = a.sb("p_veps", [P, SEQS, TILES])
        rstd = a.sb("p_rstd", [P, SEQS, TILES])
        mhalf = a.sb("p_mhalf", [P, TILES])
        epsb = a.sb("p_epsb", [P, TILES])
        ahead = a.sb("p_ahead", [P, 1])
        xn = a.sb("p_xn", [P, 2, D])
        xnT = a.sb("p_xnT", [P, 2, DC, P])
        qkv = a.sb("p_qkv", [P, 2, 2 * D])
        t_cos = a.sb("p_tcos", [P, 2, 2 * D])
        t_sin = a.sb("p_tsin", [P, 2 * D])
        rot = a.sb("p_rot", [P, 2, 2 * D])
        vaug = a.sb("p_vaug", [P, SEQS, PAIRS, TILES, 2, 2 * DH])
        parts = a.sb("p_parts", [P, SEQS, 4, PARTS, N], BF16)
        rest = a.sb("p_rest", [P, 2, 4, P])
        ps_xT = a.ps("p_ps_xT", [P, 2, 4, P])
        ps_q = a.ps("p_ps_q", [P, 2, 4 * P])
        ps_rT = a.ps("p_ps_rT", [P, 2, 4, P])

        consts_in = a.sem("p_consts_in")
        x_in = [a.sem(f"p_x_in{s}") for s in range(SEQS)]
        parts_out = [a.sem(f"p_parts_out{s}") for s in range(SEQS)]
        v_out = [a.sem(f"p_v_out{s}") for s in range(SEQS)]
        ones_set = a.sem("p_ones_set")
        stats_done = a.sem("p_stats_done")
        mv_done = a.sem("p_mv_done")
        veps_done = a.sem("p_veps_done")
        rstd_done = a.sem("p_rstd_done")
        xn_done = a.sem("p_xn_done")
        xT_done = a.sem("p_xT_done")
        xnT_done = a.sem("p_xnT_done")
        q_done = a.sem("p_q_done")
        qkv_done = a.sem("p_qkv_done")
        cos_done = a.sem("p_cos_done")
        sin_done = a.sem("p_sin_done")
        rot_done = a.sem("p_rot_done")
        vaug_done = a.sem("p_vaug_done")
        rT_done = a.sem("p_rT_done")
        part1_done = a.sem("p_part1_done")
        rest_done = a.sem("p_rest_done")
        part2_done = a.sem("p_part2_done")
        part3_done = a.sem("p_part3_done")
        block = ctx.enter_context(nc.Block())

        x_v = x.rearrange("b (i p) d -> b p i d", p=P)
        PASSES = B // SEQS

        STEP = SEQS * TILES

        def freed(it, j):
            return it * STEP + max(j - 1, 0)

        @block.sync
        def _(sp):
            def store(it, s):
                done = it * STEP + (s + 1) * TILES
                sp.wait_ge(part1_done, done)
                sp.wait_ge(part2_done, done)
                sp.wait_ge(part3_done, done)
                for c in range(4):
                    kind, chunk = c // 2, c % 2
                    for part in range(PARTS):
                        sp.dma_start(
                            parts_dram[bass.ds((it * SEQS + s) * H + chunk * 8, 8), kind, part],
                            parts[:, s, c, part]).then_inc(parts_out[s], 16)
                sp.wait_ge(vaug_done, done)
                sp.dma_start(v_dram[bass.ds(it * SEQS + s, 1)].rearrange("o r p n -> p (o r) n"),
                             vaug[:, s].rearrange("p r i h e -> p r (i h e)")).then_inc(v_out[s], 16)

            sp.dma_start(w[:], w_qkv.rearrange("(c p) n -> p c n", p=P)).then_inc(consts_in, 16)
            sp.dma_start(ident[:], ident_d).then_inc(consts_in, 16)
            sp.dma_start(cosb[:], rot_cos).then_inc(consts_in, 16)
            sp.dma_start(sinb[:], rot_sin).then_inc(consts_in, 16)
            for s in range(SEQS):
                sp.dma_start(xb[:, s], x_v[s]).then_inc(x_in[s], 16)
            with sp.Fori(0, PASSES - 1) as it:
                for s in range(SEQS):
                    sp.wait_ge(xn_done, it * STEP + (s + 1) * TILES)
                    sp.dma_start(xb[:, s], x_v[bass.ds((it + 1) * SEQS + s, 1)].rearrange("o p i d -> p (o i) d")
                                 ).then_inc(x_in[s], 16)
                for s in range(SEQS):
                    store(it, s)
            for s in range(SEQS):
                store(PASSES - 1, s)
            for s in range(SEQS):
                sp.wait_ge(parts_out[s], 16 * 4 * PARTS * PASSES)
                sp.wait_ge(v_out[s], 16 * PASSES)

        @block.vector
        def _(dve):
            def normalise(it, j):
                s, i = j // TILES, j % TILES
                dve.wait_ge(rstd_done, it * SEQS + s + 1)
                dve.wait_ge(xT_done, freed(it, j))
                nc.vector.tensor_scalar(xn[:, j % 2], xb[:, s, i], mv[:, s, i, 0:1], rstd[:, s, i:i + 1],
                                        ALU.subtract, ALU.mult).then_inc(xn_done, 1)

            def cos_product(it, j):
                i = j % TILES
                dve.wait_ge(qkv_done, it * STEP + j + 1)
                dve.wait_ge(rot_done, freed(it, j))
                nc.vector.tensor_tensor(t_cos[:, j % 2].rearrange("p (h d) -> p h d", d=DH),
                                        qkv[:, j % 2].rearrange("p (h d) -> p h d", d=DH),
                                        cosb[:, i:i + 1, :].to_broadcast([P, 2 * H, DH]),
                                        ALU.mult).then_inc(cos_done, 1)

            def cut(it, j):
                s, i = j // TILES, j % TILES
                cols = slice(i * P, (i + 1) * P)
                dve.wait_ge(part1_done, it * STEP + j + 1)
                dve.wait_ge(part3_done, freed(it, j))
                nc.vector.tensor_tensor(rest[:, j % 2], ps_rT[:, j % 2], parts[:, s, :, 0, cols],
                                        ALU.subtract).then_inc(rest_done, 1)
                dve.wait_ge(rest_done, it * STEP + j + 1)
                nc.vector.tensor_copy(parts[:, s, :, 1, cols], rest[:, j % 2]).then_inc(part2_done, 1)
                dve.wait_ge(part2_done, it * STEP + j + 1)
                nc.vector.tensor_tensor(parts[:, s, :, 2, cols], rest[:, j % 2], parts[:, s, :, 1, cols],
                                        ALU.subtract).then_inc(part3_done, 1)

            dve.wait_ge(consts_in, 64)
            nc.vector.memset(mhalf[:], -0.5).then_inc(ones_set, 1)
            nc.vector.memset(epsb[:], EPS).then_inc(ones_set, 1)
            nc.vector.memset(vaug[:], 1.0).then_inc(ones_set, 1)
            with dve.Fori(0, PASSES) as it:
                for s in range(SEQS):
                    dve.wait_ge(x_in[s], 16 * (it + 1))
                    for i in range(TILES):
                        nc.vector.bn_stats(stats[:, s, i], xb[:, s, i]).then_inc(stats_done, 1)
                    dve.wait_ge(stats_done, (it * SEQS + s + 1) * (TILES + 1) - 1)
                    nc.vector.memset(ahead[:], 0.0).then_inc(stats_done, 1)
                    for i in range(TILES):
                        nc.vector.bn_aggr(mv[:, s, i], stats[:, s, i]).then_inc(mv_done, 1)
                for j in range(STEP + 5):
                    if j < STEP:
                        normalise(it, j)
                    if 2 <= j < STEP + 2:
                        cos_product(it, j - 2)
                    if j >= 5:
                        cut(it, j - 5)

        @block.gpsimd
        def _(pool):
            pool.wait_ge(consts_in, 64)
            pool.wait_ge(ones_set, 3)
            with pool.Fori(0, PASSES) as it:
                for s in range(SEQS):
                    pool.wait_ge(mv_done, it * STEP + (s + 1) * TILES)
                    nc.gpsimd.tensor_tensor(veps[:, s], mv[:, s, :, 1], epsb[:], ALU.add).then_inc(veps_done, 1)
                    pool.wait_ge(veps_done, it * SEQS + s + 1)
                    nc.gpsimd.tensor_tensor(rstd[:, s], veps[:, s], mhalf[:], ALU.pow).then_inc(rstd_done, 1)
                for j in range(STEP):
                    s, i = j // TILES, j % TILES
                    n = it * STEP + j
                    src = qkv[:, j % 2].rearrange("p (h d) -> p h d", d=DH)
                    ts = t_sin[:].rearrange("p (h d) -> p h d", d=DH)
                    pool.wait_ge(qkv_done, n + 1)
                    pool.wait_ge(rot_done, n)
                    for k in range(2):
                        nc.gpsimd.tensor_tensor(
                            ts[:, :, k * HALF:(k + 1) * HALF], src[:, :, (1 - k) * HALF:(2 - k) * HALF],
                            sinb[:, i:i + 1, k * HALF:(k + 1) * HALF].to_broadcast([P, 2 * H, HALF]),
                            ALU.mult).then_inc(sin_done, 1)
                    pool.wait_ge(cos_done, n + 1)
                    pool.wait_ge(sin_done, 2 * (n + 1))
                    pool.wait_ge(rT_done, freed(it, j))
                    pool.wait_ge(vaug_done, freed(it, j))
                    nc.gpsimd.tensor_tensor(rot[:, j % 2], t_cos[:, j % 2], t_sin[:], ALU.add).then_inc(rot_done, 1)

        @block.scalar
        def _(act):
            act.wait_ge(ones_set, 3)
            with act.Fori(0, PASSES) as it:
                for j in range(STEP + 4):
                    if j < STEP:
                        act.wait_ge(xT_done, it * STEP + j + 1)
                        act.wait_ge(q_done, freed(it, j))
                        nc.scalar.copy(xnT[:, j % 2], ps_xT[:, j % 2, 0:DC]).then_inc(xnT_done, 1)
                    if 1 <= j <= STEP:
                        act.wait_ge(q_done, it * STEP + j)
                        act.wait_ge(rot_done, freed(it, j - 1))
                        nc.scalar.copy(qkv[:, (j - 1) % 2], ps_q[:, (j - 1) % 2]).then_inc(qkv_done, 1)
                    if j >= 4:
                        k = j - 4
                        s, i = k // TILES, k % TILES
                        if i == 0:
                            act.wait_ge(parts_out[s], 16 * 4 * PARTS * it)
                            act.wait_ge(v_out[s], 16 * it)
                        act.wait_ge(rT_done, it * STEP + k + 1)
                        act.wait_ge(rest_done, freed(it, k))
                        nc.scalar.copy(parts[:, s, :, 0, i * P:(i + 1) * P], ps_rT[:, k % 2]).then_inc(part1_done, 1)
                        nc.scalar.copy(vaug[:, s, :, i, :, 0:DH],
                                       rot[:, k % 2, D:2 * D].rearrange("p (r h d) -> p r h d", h=2, d=DH)
                                       ).then_inc(vaug_done, 1)

        @block.tensor
        def _(pe):
            pe.wait_ge(consts_in, 64)
            with pe.Fori(0, PASSES) as it:
                for j in range(STEP + 4):
                    if j < STEP:
                        pe.wait_ge(xn_done, it * STEP + j + 1)
                        pe.wait_ge(xnT_done, freed(it, j))
                        for c in range(DC):
                            mm = nc.tensor.transpose(ps_xT[:, j % 2, c], xn[:, j % 2, c * P:(c + 1) * P], ident[:])
                        mm.then_inc(xT_done, 1)
                    if 1 <= j <= STEP:
                        k = j - 1
                        pe.wait_ge(xnT_done, it * STEP + k + 1)
                        pe.wait_ge(qkv_done, freed(it, k))
                        for c in range(DC):
                            mm = nc.tensor.matmul(ps_q[:, k % 2], xnT[:, k % 2, c], w[:, c],
                                                  start=(c == 0), stop=(c == DC - 1))
                        mm.then_inc(q_done, 1)
                    if j >= 4:
                        k = j - 4
                        pe.wait_ge(rot_done, it * STEP + k + 1)
                        pe.wait_ge(rest_done, freed(it, k))
                        for c in range(4):
                            mm = nc.tensor.transpose(ps_rT[:, k % 2, c], rot[:, k % 2, c * P:(c + 1) * P], ident[:])
                        mm.then_inc(rT_done, 1)


SLOTS = ((0, 0), (1, 1), (0, 1), (1, 0), (2, 0), (0, 2))
SLOT_ROW = ([0, 16, 32, 48, 64, 80], [64, 80, 96, 112, 0, 16])
MAX_ROW = (96, 32)
MAX_PARTS = 2


def slot_runs(h, kind):
    runs = []
    for row, of in zip(SLOT_ROW[h], SLOTS):
        part = of[kind]
        if runs and runs[-1][0] + runs[-1][2] * DH == row and runs[-1][1] + runs[-1][2] == part:
            runs[-1][2] += 1
        else:
            runs.append([row, part, 1])
    return runs


CHUNK = 512
QUARTER = N // 4


def attend(nc, parts_dram, v_dram, o_dram, ident_d):
    NG = 2 * TILES
    with ExitStack() as ctx:
        a = Alloc(nc, ctx)
        identb = a.sb("a_identb", [P, P], BF16)
        identf = a.sb("a_identf", [P, P])
        qb = a.sb("a_q", [P, 3, 2, N], BF16)
        kb = a.sb("a_k", [P, 3, 2, N], BF16)
        vb = a.sb("a_v", [P, 3, TILES, 2, 2 * DH])
        prob = a.sb("a_prob", [P, 4, N])
        mx = a.sb("a_mx", [P, TILES, 2, 2])
        nm = a.sb("a_nm", [P, TILES, 2])
        nsplit = a.sb("a_nsplit", [P, 2, MAX_PARTS, TILES], BF16)
        zero = a.sb("a_zero", [P, TILES, 2])
        mrow = a.sb("a_mrow", [2 * MAX_PARTS * TILES, P], BF16)
        oraw = a.sb("a_oraw", [P, 2, QUARTER])
        sm = a.ps("a_sm", [P, 2, 2, CHUNK])
        st = a.ps("a_st", [P, 3, CHUNK])
        pv = a.ps("a_pv", [P, CHUNK])

        set_up = a.sem("a_set_up")
        ident_in = a.sem("a_ident_in")
        identb_set = a.sem("a_identb_set")
        qk_in = [a.sem(f"a_qk_in{i}") for i in range(3)]
        v_in = [a.sem(f"a_v_in{i}") for i in range(3)]
        m_in = a.sem("a_m_in")
        o_out = [a.sem(f"a_o_out{i}") for i in range(2)]
        sm_done = a.sem("a_sm_done")
        max_done = a.sem("a_max_done")
        nm_done = a.sem("a_nm_done")
        n1_done = a.sem("a_n1_done")
        n2_done = a.sem("a_n2_done")
        mT_done = a.sem("a_mT_done")
        mrow_done = a.sem("a_mrow_done")
        st_done = a.sem("a_st_done")
        exp_done = a.sem("a_exp_done")
        pv_done = a.sem("a_pv_done")
        evac_done = a.sem("a_evac_done")
        block = ctx.enter_context(nc.Block())
        QK_LOADS = sum(len(slot_runs(h, kind)) for h in range(2) for kind in range(2))
        UNITS = 2 * NG
        AHEAD = NG + NG // 2
        turned = pv[0:2 * MAX_PARTS * TILES, QUARTER:QUARTER + P // 2].bitcast(BF16)

        class Pair:

            def __init__(self, k, c, p=None):
                self.k, self.c, self.p = k, c, p
                self.n = k * 3 + c
                self.buf = c % 3
                self.turn = k + c // 3

            def plus(self, d):
                return Pair(self.k, self.c + d, None if self.p is None else self.p + d)

            def exists(self):
                return self.p is None or self.p < NP

            def first(self):
                return self.p == 0

        def pairs(eng, body):
            body(Pair(0, 0, 0))
            with eng.Fori(0, (NP - 4) // 3) as k:
                for c in range(1, 4):
                    body(Pair(k, c))
            for p in range(NP - 3, NP):
                body(Pair(0, p, p))

        @block.sync
        def _(sp):
            def load(q):
                if not (q.p is not None and q.p < 3):
                    sp.wait_ge(st_done, (q.n - 2) * UNITS)
                for h in range(2):
                    for kind, buf in ((0, qb), (1, kb)):
                        for row, part, parts in slot_runs(h, kind):
                            sp.dma_start(buf[row:row + parts * DH, q.buf, h, :],
                                         parts_dram[bass.ds(q.n * 2 + h, 1), kind, part:part + parts]
                                         .rearrange("o s d n -> (o s d) n")).then_inc(qk_in[q.buf], 16)
                if not (q.p is not None and q.p < 3):
                    sp.wait_ge(pv_done, (q.n - 2) * NG)
                sp.dma_start(vb[:, q.buf].rearrange("p i h e -> p (i h e)"),
                             v_dram[bass.ds(q.n, 1)].rearrange("o p n -> (o p) n")).then_inc(v_in[q.buf], 16)

            def store(q, h):
                sp.wait_ge(evac_done, q.n * 2 + h + 1)
                sp.dma_start(o_dram[bass.ds(q.n, 1), h].rearrange("o c r n -> (o c r) n"), oraw[:, h]
                             ).then_inc(o_out[h], 16)

            def max_rows(q):
                sp.wait_ge(mrow_done, q.n + 1)
                rows = MAX_PARTS * TILES
                for h in range(2):
                    sp.dma_start(qb[MAX_ROW[h]:MAX_ROW[h] + MAX_PARTS, q.buf, h, :].rearrange("r (t c) -> r t c", c=P),
                                 mrow[h * rows:(h + 1) * rows, :]).then_inc(m_in, 16)

            def body(q):
                if not q.first() and q.plus(2).exists():
                    load(q.plus(2))
                if not q.first():
                    store(q.plus(-1), 1)
                store(q, 0)
                if q.plus(1).exists():
                    max_rows(q.plus(1))

            sp.dma_start(identf[:], ident_d).then_inc(ident_in, 16)
            sp.wait_ge(set_up, 4)
            for p in range(3):
                load(Pair(0, p, p))
            max_rows(Pair(0, 0, 0))
            pairs(sp, body)
            store(Pair(0, NP - 1, NP - 1), 1)
            for h in range(2):
                sp.wait_ge(o_out[h], 16 * NP)

        @block.tensor
        def _(pe):
            def scores(q, g, ic):
                h, jt = g // TILES, g % TILES
                u = g * 2 + ic
                slot = (q.c * UNITS + u) % 3
                if g == 0 and ic == 0:
                    pe.wait_ge(m_in, (q.n + 1) * 32)
                if not (q.first() and u < 3):
                    pe.wait_ge(exp_done, q.n * UNITS + (u - 2))
                nc.tensor.matmul(st[:, slot], kb[:, q.buf, h, jt * P:(jt + 1) * P],
                                 qb[:, q.buf, h, ic * CHUNK:(ic + 1) * CHUNK],
                                 start=True, stop=True).then_inc(st_done, 1)

            def values(q, g):
                h, jt = g // TILES, g % TILES
                if g == 0:
                    pe.wait_ge(v_in[q.buf], (q.turn + 1) * 16)
                if jt == 0 and not (q.first() and g == 0):
                    pe.wait_ge(evac_done, q.n * 2 + h)
                if jt == 0 and not (h == 1 and not q.plus(1).exists()):
                    pe.wait_ge(mrow_done, q.n + 1 + h)
                pe.wait_ge(exp_done, q.n * UNITS + 2 * g + 2)
                for c in range(4):
                    mm = nc.tensor.matmul(pv[32 * c:32 * c + 32, 0:QUARTER], vb[:, q.buf, jt, h, :],
                                          prob[:, g % 4, c * QUARTER:(c + 1) * QUARTER],
                                          start=(jt == 0), stop=(jt == TILES - 1))
                mm.then_inc(pv_done, 1)

            def maxima(q, v, slot):
                qt, kc = v // 2, v % 2
                if v == 0:
                    pe.wait_ge(qk_in[q.buf], (q.turn + 1) * 16 * QK_LOADS)
                for h in range(2):
                    rows = slice(64 * h, 64 * h + 64)
                    mm = nc.tensor.matmul(sm[:, slot, h], qb[rows, q.buf, h, qt * P:(qt + 1) * P],
                                          kb[rows, q.buf, h, kc * CHUNK:(kc + 1) * CHUNK], start=True, stop=True)
                mm.then_inc(sm_done, 1)

            def turn_maxima(q):
                pe.wait_ge(n2_done, q.n + 1)
                nc.tensor.transpose(turned, nsplit[:].rearrange("p h s t -> p (h s t)"), identb[:]).then_inc(mT_done, 1)

            def body(q):
                seen = q.n * NG + AHEAD
                for g in range(NG):
                    scores(q, g, 0)
                    if g >= 2:
                        values(q, g - 2)
                        if g - 2 == TILES - 1 and q.plus(1).exists():
                            turn_maxima(q.plus(1))
                    elif not q.first():
                        values(q.plus(-1), NG + g - 2)
                    scores(q, g, 1)
                    ahead = q.plus(1) if g < NG // 2 else q.plus(2)
                    if ahead.exists():
                        pe.wait_ge(max_done, seen + g - 1)
                        maxima(ahead, (g + NG // 2) % NG, g % 2)

            pe.wait_ge(set_up, 4)
            pe.wait_ge(identb_set, 1)
            q0, q1 = Pair(0, 0, 0), Pair(0, 1, 1)
            for v in range(NG):
                if v >= 2:
                    pe.wait_ge(max_done, v - 1)
                maxima(q0, v, v % 2)
            turn_maxima(q0)
            for v in range(NG // 2):
                pe.wait_ge(max_done, NG + v - 1)
                maxima(q1, v, v % 2)
            pairs(pe, body)
            last = Pair(0, NP - 1, NP - 1)
            values(last, NG - 2)
            values(last, NG - 1)

        @block.vector
        def _(dve):
            def reduce(q, v, s, slot):
                qt, kc = v // 2, v % 2
                if v == 0 and not q.first():
                    dve.wait_ge(nm_done, q.n)
                dve.wait_ge(sm_done, s + 1)
                nc.vector.tensor_reduce(mx[:, qt, kc, :], sm[:, slot], AX.X, ALU.max,
                                        negate=True).then_inc(max_done, 1)
                if v == NG - 1:
                    if not q.first():
                        dve.wait_ge(n2_done, q.n)
                    dve.wait_ge(max_done, (q.n + 1) * NG)
                    nc.vector.tensor_tensor(nm[:], mx[:, :, 0], mx[:, :, 1], ALU.min).then_inc(nm_done, 1)

            def body(q):
                for g in range(NG):
                    ahead = q.plus(1) if g < NG // 2 else q.plus(2)
                    if ahead.exists():
                        reduce(ahead, (g + NG // 2) % NG, q.n * NG + AHEAD + g, g % 2)

            nc.vector.memset(qb[:].bitcast(U32), 0).then_inc(set_up, 1)
            nc.vector.memset(kb[:].bitcast(U32), 0).then_inc(set_up, 1)
            nc.vector.memset(zero[:], 0.0).then_inc(set_up, 1)
            dve.wait_ge(set_up, 3)
            nc.vector.memset(kb[MAX_ROW[0]:MAX_ROW[0] + MAX_PARTS, :, 0], 1.0).then_inc(identb_set, 1)
            nc.vector.memset(kb[MAX_ROW[1]:MAX_ROW[1] + MAX_PARTS, :, 1], 1.0).then_inc(set_up, 1)
            dve.wait_ge(ident_in, 16)
            nc.vector.tensor_copy(identb[:], identf[:]).then_inc(identb_set, 1)
            for v in range(NG):
                reduce(Pair(0, 0, 0), v, v, v % 2)
            for v in range(NG // 2):
                reduce(Pair(0, 1, 1), v, NG + v, v % 2)
            pairs(dve, body)

        @block.gpsimd
        def _(pool):
            def split(q):
                part = [nsplit[:, :, s, :].rearrange("p h t -> p t h") for s in range(MAX_PARTS)]
                pool.wait_ge(nm_done, q.n + 1)
                if not q.first():
                    pool.wait_ge(mT_done, q.n)
                nc.gpsimd.tensor_tensor(part[0], nm[:], zero[:], ALU.add).then_inc(n1_done, 1)
                pool.wait_ge(n1_done, q.n + 1)
                nc.gpsimd.tensor_tensor(part[1], nm[:], part[0], ALU.subtract).then_inc(n2_done, 1)

            pool.wait_ge(set_up, 4)
            pairs(pool, split)

        @block.scalar
        def _(act):
            def exp(q, g, ic):
                u = g * 2 + ic
                act.wait_ge(st_done, q.n * UNITS + u + 1)
                if ic == 0 and not (q.first() and g < 4):
                    act.wait_ge(pv_done, q.n * NG + g - 3)
                nc.scalar.activation(prob[:, g % 4, ic * CHUNK:(ic + 1) * CHUNK], st[:, (q.c * UNITS + u) % 3],
                                     ACT.Exp, scale=DH ** -0.5).then_inc(exp_done, 1)

            def evacuate(q, h):
                act.wait_ge(pv_done, q.n * NG + (h + 1) * TILES)
                if not q.first():
                    act.wait_ge(o_out[h], q.n * 16)
                nc.scalar.copy(oraw[:, h], pv[:, 0:QUARTER]).then_inc(evac_done, 1)

            def copy_max_rows(q):
                act.wait_ge(mT_done, q.n + 1)
                if not q.first():
                    act.wait_ge(m_in, q.n * 32)
                nc.scalar.copy(mrow[:], turned).then_inc(mrow_done, 1)

            def body(q):
                for g in range(NG):
                    exp(q, g, 0)
                    if g == 1 and not q.first():
                        evacuate(q.plus(-1), 1)
                    if g == 9:
                        if q.plus(1).exists():
                            act.wait_ge(mT_done, q.n + 2)
                        evacuate(q, 0)
                        if q.plus(1).exists():
                            copy_max_rows(q.plus(1))
                    exp(q, g, 1)

            copy_max_rows(Pair(0, 0, 0))
            pairs(act, body)
            evacuate(Pair(0, NP - 1, NP - 1), 1)


def finish(nc, x, o_dram, rden_dram, w_out, b_out, w_gate, ident_d, table, out, gate):
    SEQS = 2
    STEP = SEQS * TILES
    PASSES = B // SEQS
    with ExitStack() as ctx:
        a = Alloc(nc, ctx)
        ident = a.sb("f_ident", [P, P])
        w = a.sb("f_w", [P, DC, D])
        wg = a.sb("f_wg", [P, DC, E])
        bo = a.sb("f_bo", [P, D])
        mhalf = a.sb("f_mhalf", [P, TILES])
        epsb = a.sb("f_epsb", [P, TILES])
        ahead = a.sb("f_ahead", [P, 1])
        den = a.sb("f_den", [P, SEQS, P])
        rden = a.sb("f_rden", [P, SEQS, P])
        num = a.sb("f_num", [P, SEQS, DC, N])
        rrep = a.sb("f_rrep", [P, SEQS, DC, N])
        xb = a.sb("f_x", [P, SEQS, TILES, D])
        x2 = a.sb("f_x2", [P, SEQS, TILES, D])
        xf = a.sb("f_xf", [P, SEQS, TILES, D])
        tab = a.sb("f_tab", [P, SEQS, TILES, ROW])
        stats = a.sb("f_stats", [P, SEQS, 2, TILES, 6])
        mv = a.sb("f_mv", [P, SEQS, 2, TILES, 2])
        veps = a.sb("f_veps", [P, SEQS, 2, TILES])
        rstd = a.sb("f_rstd", [P, SEQS, 2, TILES])
        xfT = a.sb("f_xfT", [P, 2, DC, P])
        lmax = a.sb("f_lmax", [P, TILES])
        lcen = a.sb("f_lcen", [P, TILES, E])
        lexp = a.sb("f_lexp", [P, TILES, E])
        lsum = a.sb("f_lsum", [P, TILES])
        lrec = a.sb("f_lrec", [P, TILES])
        ps_y = a.ps("f_ps_y", [P, 2, 512])
        ps_xT = a.ps("f_ps_xT", [P, 2, 4, P])
        ps_l = a.ps("f_ps_l", [P, 2, 512])

        consts_in = a.sem("f_consts_in")
        set_up = a.sem("f_set_up")
        den_in = [a.sem(f"f_den_in{s}") for s in range(SEQS)]
        num_in = [a.sem(f"f_num_in{s}") for s in range(SEQS)]
        rrep_in = [a.sem(f"f_rrep_in{s}") for s in range(SEQS)]
        x_in = [a.sem(f"f_x_in{s}") for s in range(SEQS)]
        rden_out = a.sem("f_rden_out")
        out_out = [a.sem(f"f_out_out{s}") for s in range(SEQS)]
        tab_out = [a.sem(f"f_tab_out{s}") for s in range(SEQS)]
        rden_done = a.sem("f_rden_done")
        onorm_done = a.sem("f_onorm_done")
        xb_done = a.sem("f_xb_done")
        y_done = a.sem("f_y_done")
        x2_done = a.sem("f_x2_done")
        stats_done = a.sem("f_stats_done")
        mv_done = a.sem("f_mv_done")
        veps_done = a.sem("f_veps_done")
        rstd_done = a.sem("f_rstd_done")
        xf_done = a.sem("f_xf_done")
        xT_done = a.sem("f_xT_done")
        xfT_done = a.sem("f_xfT_done")
        logits_done = a.sem("f_logits_done")
        yn_done = a.sem("f_yn_done")
        base_done = a.sem("f_base_done")
        lmax_done = a.sem("f_lmax_done")
        lcen_done = a.sem("f_lcen_done")
        lexp_done = a.sem("f_lexp_done")
        lsum_done = a.sem("f_lsum_done")
        lrec_done = a.sem("f_lrec_done")
        gate_done = a.sem("f_gate_done")
        scores_done = a.sem("f_scores_done")
        block = ctx.enter_context(nc.Block())

        x_v = x.rearrange("b (i p) d -> b p i d", p=P)
        out_v = out.rearrange("b (i p) d -> b p i d", p=P)
        table_v = table.rearrange("(b i p) e -> b p i e", p=P, i=TILES)
        HC = PAIRS // DC
        NUM_LOADS = DC * 4

        def root_count(it, s, k):
            return it * 2 * SEQS + k * SEQS + s + 1

        def mv_count(it, s, k):
            return root_count(it, s, k) * TILES

        def freed(it, j):
            return it * STEP + max(j - 1, 0)

        @block.sync
        def _(sp):
            def one(v):
                return bass.ds(v, 1)

            def load(it, s):
                b = it * SEQS + s
                sp.dma_start(den[:, s], o_dram[bass.ds(b * PAIRS, PAIRS), :, :, DH, :]
                             .rearrange("n h c (f x) -> (n h c) f x", f=2)).then_inc(den_in[s], 16)
                for ch in range(DC):
                    for c in range(4):
                        sp.dma_start(num[:, s, ch, c * QUARTER:(c + 1) * QUARTER],
                                     o_dram[bass.ds(b * PAIRS + ch * HC, HC), :, c, 0:DH, :]
                                     .rearrange("n h r x -> (n h) r x")).then_inc(num_in[s], 16)
                sp.dma_start(xb[:, s], x_v[one(b)].rearrange("o p i d -> p (o i) d")).then_inc(x_in[s], 16)
                sp.wait_ge(rden_done, b + 1)
                sp.dma_start(rden_dram[one(b)].rearrange("o r n -> (o r) n"), rden[:, s]).then_inc(rden_out, 16)
                sp.wait_ge(rden_out, 16 * (b + 1))
                for ch in range(DC):
                    sp.dma_start(rrep[:, s, ch],
                                 rden_dram[one(b), ch * 64:(ch + 1) * 64].rearrange("o (k q) n -> (o k) (q n)", q=TILES)
                                 .unsqueeze(1).to_broadcast([2 * HC, DH, N])).then_inc(rrep_in[s], 16)

            def store(it, s):
                b = it * SEQS + s
                sp.wait_ge(base_done, (b + 1) * TILES)
                sp.dma_start(out_v[one(b)].rearrange("o p i d -> p (o i) d"), x2[:, s]).then_inc(out_out[s], 16)
                sp.wait_ge(yn_done, (b + 1) * TILES)
                sp.wait_ge(scores_done, b + 1)
                sp.dma_start(table_v[one(b)].rearrange("o p i e -> p (o i) e"), tab[:, s]).then_inc(tab_out[s], 16)

            sp.dma_start(w[:], w_out.rearrange("(c p) n -> p c n", p=P)).then_inc(consts_in, 16)
            sp.dma_start(wg[:], w_gate).then_inc(consts_in, 16)
            sp.dma_start(ident[:], ident_d).then_inc(consts_in, 16)
            sp.dma_start(bo[:], b_out.rearrange("(o n) -> o n", o=1).to_broadcast([P, D])).then_inc(consts_in, 16)
            for s in range(SEQS):
                load(0, s)
            with sp.Fori(0, PASSES - 1) as it:
                for s in range(SEQS):
                    sp.wait_ge(y_done, (it * SEQS + s + 1) * TILES)
                    sp.wait_ge(x2_done, (it * SEQS + s + 1) * TILES)
                    load(it + 1, s)
                for s in range(SEQS):
                    store(it, s)
            for s in range(SEQS):
                store(PASSES - 1, s)
            for s in range(SEQS):
                sp.wait_ge(out_out[s], 16 * PASSES)
                sp.wait_ge(tab_out[s], 16 * PASSES)

        @block.gpsimd
        def _(pool):
            def inverse_root(b, s, k):
                pool.wait_ge(mv_done, mv_count(b, s, k))
                nc.gpsimd.tensor_tensor(veps[:, s, k], mv[:, s, k, :, 1], epsb[:], ALU.add).then_inc(veps_done, 1)
                pool.wait_ge(veps_done, root_count(b, s, k))
                nc.gpsimd.tensor_tensor(rstd[:, s, k], veps[:, s, k], mhalf[:], ALU.pow).then_inc(rstd_done, 1)

            pool.wait_ge(consts_in, 64)
            pool.wait_ge(set_up, 2)
            with pool.Fori(0, PASSES) as it:
                for s in range(SEQS):
                    b = it * SEQS + s
                    pool.wait_ge(num_in[s], 16 * NUM_LOADS * (it + 1))
                    pool.wait_ge(rrep_in[s], 16 * DC * (it + 1))
                    for ch in range(DC):
                        nc.gpsimd.tensor_tensor(num[:, s, ch], num[:, s, ch], rrep[:, s, ch],
                                                ALU.mult).then_inc(onorm_done, 1)
                    pool.wait_ge(x_in[s], 16 * (it + 1))
                    nc.gpsimd.tensor_tensor(xb[:, s], xb[:, s], bo[:].unsqueeze(1).to_broadcast([P, TILES, D]),
                                            ALU.add).then_inc(xb_done, 1)
                for k in range(2):
                    for s in range(SEQS):
                        inverse_root(it, s, k)
                for s in range(SEQS):
                    pool.wait_ge(xf_done, (it * SEQS + s + 1) * TILES)
                    for i in range(TILES):
                        nc.gpsimd.tensor_tensor(x2[:, s, i], x2[:, s, i], xf[:, s, i], ALU.add).then_inc(base_done, 1)

        @block.vector
        def _(dve):
            def residual(it, s):
                for i in range(TILES):
                    n = it * STEP + s * TILES + i
                    if i == 0:
                        dve.wait_ge(xb_done, it * SEQS + s + 1)
                        dve.wait_ge(out_out[s], 16 * it)
                    dve.wait_ge(y_done, n + 1)
                    nc.vector.tensor_tensor(x2[:, s, i], ps_y[:, i % 2, 0:D], xb[:, s, i], ALU.add).then_inc(x2_done, 1)
                    if i > 0:
                        dve.wait_ge(x2_done, n)
                        nc.vector.bn_stats(stats[:, s, 0, i - 1], x2[:, s, i - 1]).then_inc(stats_done, 1)
                dve.wait_ge(x2_done, n + 1)
                nc.vector.bn_stats(stats[:, s, 0, TILES - 1], x2[:, s, TILES - 1]).then_inc(stats_done, 1)
                aggregate(it, s, 0)

            def aggregate(it, s, k):
                dve.wait_ge(stats_done, root_count(it, s, k) * (TILES + 1) - 1)
                nc.vector.memset(ahead[:], 0.0).then_inc(stats_done, 1)
                for i in range(TILES):
                    nc.vector.bn_aggr(mv[:, s, k, i], stats[:, s, k, i]).then_inc(mv_done, 1)

            def normalise(it, s):
                dve.wait_ge(rstd_done, root_count(it, s, 0))
                for i in range(TILES):
                    n = it * STEP + s * TILES + i
                    nc.vector.tensor_scalar(xf[:, s, i], x2[:, s, i], mv[:, s, 0, i, 0:1], rstd[:, s, 0, i:i + 1],
                                            ALU.subtract, ALU.mult).then_inc(xf_done, 1)
                    if i > 0:
                        dve.wait_ge(xf_done, n)
                        nc.vector.bn_stats(stats[:, s, 1, i - 1], xf[:, s, i - 1]).then_inc(stats_done, 1)
                dve.wait_ge(xf_done, n + 1)
                nc.vector.bn_stats(stats[:, s, 1, TILES - 1], xf[:, s, TILES - 1]).then_inc(stats_done, 1)
                aggregate(it, s, 1)

            def rows(it, s):
                b = it * SEQS + s
                lg = ps_l[:, s, 0:TILES * E].rearrange("p (i e) -> p i e", e=E)
                dve.wait_ge(logits_done, (b + 1) * TILES)
                nc.vector.tensor_reduce(lmax[:], lg, AX.X, ALU.max).then_inc(lmax_done, 1)
                dve.wait_ge(lmax_done, b + 1)
                nc.vector.tensor_tensor(lcen[:], lg, lmax[:].unsqueeze(2).to_broadcast([P, TILES, E]),
                                        ALU.subtract).then_inc(lcen_done, 1)
                dve.wait_ge(rstd_done, root_count(it, s, 1))
                dve.wait_ge(tab_out[s], 16 * it)
                for i in range(TILES):
                    nc.vector.tensor_scalar(tab[:, s, i, 0:D], xf[:, s, i], mv[:, s, 1, i, 0:1], rstd[:, s, 1, i:i + 1],
                                            ALU.subtract, ALU.mult).then_inc(yn_done, 1)
                dve.wait_ge(lexp_done, b + 1)
                nc.vector.tensor_reduce(lsum[:], lexp[:], AX.X, ALU.add).then_inc(lsum_done, 1)
                dve.wait_ge(lsum_done, b + 1)
                nc.vector.reciprocal(lrec[:], lsum[:]).then_inc(lrec_done, 1)
                dve.wait_ge(lrec_done, b + 1)
                nc.vector.tensor_tensor(gate[:, bass.ds(b * TILES, TILES), :], lexp[:],
                                        lrec[:].unsqueeze(2).to_broadcast([P, TILES, E]), ALU.mult).then_inc(gate_done, 1)

            nc.vector.memset(mhalf[:], -0.5).then_inc(set_up, 1)
            nc.vector.memset(epsb[:], EPS).then_inc(set_up, 1)
            with dve.Fori(0, PASSES) as it:
                for s in range(SEQS):
                    dve.wait_ge(den_in[s], 16 * (it + 1))
                    dve.wait_ge(rden_out, 16 * (it * SEQS))
                    nc.vector.reciprocal(rden[:, s], den[:, s]).then_inc(rden_done, 1)
                for s in range(SEQS):
                    residual(it, s)
                for s in range(SEQS):
                    normalise(it, s)
                for s in range(SEQS):
                    rows(it, s)

        @block.scalar
        def _(act):
            with act.Fori(0, PASSES) as it:
                for s in range(SEQS):
                    for i in range(TILES):
                        n = it * STEP + s * TILES + i
                        act.wait_ge(xT_done, n + 1)
                        act.wait_ge(logits_done, freed(it, s * TILES + i))
                        nc.scalar.copy(xfT[:, i % 2], ps_xT[:, i % 2, 0:DC]).then_inc(xfT_done, 1)
                for s in range(SEQS):
                    b = it * SEQS + s
                    act.wait_ge(lcen_done, b + 1)
                    act.wait_ge(gate_done, b)
                    nc.scalar.activation(lexp[:], lcen[:], ACT.Exp).then_inc(lexp_done, 1)
                    act.wait_ge(gate_done, b + 1)
                    act.wait_ge(tab_out[s], 16 * it)
                    nc.scalar.copy(tab[:, s, :, D:ROW], gate[:, bass.ds(b * TILES, TILES), :]).then_inc(scores_done, 1)

        @block.tensor
        def _(pe):
            pe.wait_ge(consts_in, 64)
            with pe.Fori(0, PASSES) as it:
                for s in range(SEQS):
                    pe.wait_ge(onorm_done, DC * (it * SEQS + s + 1))
                    for i in range(TILES):
                        pe.wait_ge(x2_done, freed(it, s * TILES + i))
                        for ch in range(DC):
                            mm = nc.tensor.matmul(ps_y[:, i % 2, 0:D], num[:, s, ch, i * P:(i + 1) * P], w[:, ch],
                                                  start=(ch == 0), stop=(ch == DC - 1))
                        mm.then_inc(y_done, 1)
                for s in range(SEQS):
                    for i in range(TILES + 1):
                        n = it * STEP + s * TILES + i
                        if i < TILES:
                            pe.wait_ge(xf_done, n + 1)
                            pe.wait_ge(xfT_done, freed(it, s * TILES + i))
                            for c in range(DC):
                                mm = nc.tensor.transpose(ps_xT[:, i % 2, c], xf[:, s, i, c * P:(c + 1) * P], ident[:])
                            mm.then_inc(xT_done, 1)
                        if i > 0:
                            pe.wait_ge(xfT_done, n)
                            if i == 1:
                                pe.wait_ge(lcen_done, it * SEQS)
                            for c in range(DC):
                                mm = nc.tensor.matmul(ps_l[:, s, (i - 1) * E:i * E], xfT[:, (i - 1) % 2, c], wg[:, c],
                                                      start=(c == 0), stop=(c == DC - 1))
                            mm.then_inc(logits_done, 1)


ROUNDS = 15
LEVELS = 4


def choose(nc, gate, consts, places_hi, places_lo):
    GROUP = TOK // 16
    GC = GROUP // P
    with ExitStack() as ctx:
        a = Alloc(nc, ctx)
        ident = a.sb("c_ident", [P, P])
        same = a.sb("c_same", [P, P])
        before = a.sb("c_before", [P, P])
        bits = a.sb("c_bits", [P, ROUNDS, LEVELS], I32)
        by_group = a.sb("c_by_group", [P, GC, E, 16])
        score = a.sb("c_score", [P, GROUP])
        mark = a.sb("c_mark", [P, LEVELS, GROUP], BF16)
        zeros = a.sb("c_zeros", [P, GROUP])
        best = a.sb("c_best", [P, 1])
        cand = a.sb("c_cand", [P, LEVELS])
        held = a.sb("c_held", [P, LEVELS])
        count = a.sb("c_count", [P, LEVELS])
        above = a.sb("c_above", [P, GROUP])
        n_above = a.sb("c_n_above", [P, 1])
        equal = a.sb("c_equal", [P, GROUP])
        rank = a.sb("c_rank", [P, GROUP])
        need = a.sb("c_need", [P, 1])
        limit = a.sb("c_limit", [P, 1])
        taken = a.sb("c_taken", [P, GROUP])
        chosen = a.sb("c_chosen", [P, GROUP])
        place = a.sb("c_place", [P, GROUP])
        offset = a.sb("c_offset", [P, 1])
        marked = a.sb("c_marked", [P, GROUP])
        place_i = a.sb("c_place_i", [P, GROUP], I32)
        hi_i = a.sb("c_hi_i", [P, GROUP], I32)
        lo_i = a.sb("c_lo_i", [P, GROUP], I32)
        ps_t = a.ps("c_ps_t", [P, GC, P])
        ps_c = a.ps("c_ps_c", [P, 512])
        ps_p = a.ps("c_ps_p", [P, GC, P])

        consts_in = a.sem("c_consts_in")
        grouped = a.sem("c_grouped")
        turned = a.sem("c_turned")
        counted = a.sem("c_counted")
        totals = a.sem("c_totals")
        step = a.sem("c_step")
        block = ctx.enter_context(nc.Block())

        @block.sync
        def _(sp):
            for buf, name in ((ident, "ident"), (same, "same"), (before, "before"), (bits, "bits")):
                sp.dma_start(buf[:], consts[name]).then_inc(consts_in, 16)

        @block.tensor
        def _(pe):
            pe.wait_ge(consts_in, 64)
            pe.wait_ge(grouped, GC)
            for c in range(GC):
                mm = nc.tensor.transpose(ps_t[:, c], by_group[:, c].rearrange("p e g -> p (e g)"), ident[:])
            mm.then_inc(turned, 1)
            with pe.Fori(0, ROUNDS) as r:
                pe.wait_ge(counted, r + 1)
                nc.tensor.matmul(ps_c[:, 0:LEVELS], same[:], count[:], start=True, stop=True).then_inc(totals, 1)
            pe.wait_ge(counted, ROUNDS + 1)
            nc.tensor.matmul(ps_c[:, 0:1], same[:], n_above[:], start=True, stop=True).then_inc(totals, 1)
            pe.wait_ge(counted, ROUNDS + 2)
            nc.tensor.matmul(ps_c[:, 0:1], before[:], rank[:, GROUP - 1:GROUP], start=True, stop=True
                             ).then_inc(totals, 1)
            pe.wait_ge(counted, ROUNDS + 3)
            nc.tensor.matmul(ps_c[:, 0:1], before[:], place[:, GROUP - 1:GROUP], start=True, stop=True
                             ).then_inc(totals, 1)
            pe.wait_ge(counted, ROUNDS + 4)
            for c in range(GC):
                mm = nc.tensor.transpose(ps_p[:, c], marked[:, c * P:(c + 1) * P], ident[:])
            mm.then_inc(turned, 1)

        @block.vector
        def _(dve):
            for c in range(GC):
                nc.vector.tensor_copy(by_group[:, c], gate[:].rearrange("p (g c) e -> p c e g", c=GC)[:, c]
                                      ).then_inc(grouped, 1)
            nc.vector.memset(zeros[:], 0.0).then_inc(step, 1)
            nc.vector.memset(best[:], 0.0).then_inc(step, 1)
            dve.wait_ge(consts_in, 64)
            dve.wait_ge(turned, 1)
            nc.vector.tensor_copy(score[:], ps_t[:].rearrange("p c n -> p (c n)")).then_inc(step, 1)
            SET_UP, EACH = 3, LEVELS + 3
            with dve.Fori(0, ROUNDS) as r:
                done = r * EACH + SET_UP
                dve.wait_ge(step, done)
                nc.vector.tensor_tensor(cand[:].bitcast(I32), bits[:, bass.ds(r, 1), :].rearrange("p o l -> p (o l)"),
                                        best[:].bitcast(I32).to_broadcast([P, LEVELS]), ALU.bitwise_or).then_inc(step, 1)
                dve.wait_ge(step, done + 1)
                for v in range(LEVELS):
                    nc.vector.tensor_scalar(mark[:, v], score[:], cand[:, v:v + 1], 0.0, ALU.is_ge, ALU.add,
                                            accum_out=count[:, v:v + 1]).then_inc(step if v < LEVELS - 1 else counted, 1)
                dve.wait_ge(totals, r + 1)
                nc.vector.scalar_tensor_tensor(out=held[:], in0=ps_c[:, 0:LEVELS], scalar=float(K), in1=cand[:],
                                               op0=ALU.is_ge, op1=ALU.mult).then_inc(step, 1)
                dve.wait_ge(step, done + LEVELS + 1)
                nc.vector.tensor_reduce(best[:], held[:], AX.X, ALU.max).then_inc(step, 2)
            done = ROUNDS * EACH + SET_UP
            dve.wait_ge(step, done)
            nc.vector.tensor_scalar(above[:], score[:], best[:], 0.0, ALU.is_gt, ALU.add, accum_out=n_above[:]
                                    ).then_inc(counted, 1)
            nc.vector.tensor_scalar(equal[:], score[:], best[:], None, ALU.is_equal).then_inc(step, 1)
            dve.wait_ge(step, done + 1)
            nc.vector.tensor_tensor_scan(rank[:], equal[:], zeros[:], 0.0, ALU.add, ALU.add).then_inc(step, 1)
            dve.wait_ge(totals, ROUNDS + 1)
            nc.vector.tensor_scalar(need[:], ps_c[:, 0:1], -1.0, float(K), ALU.mult, ALU.add).then_inc(step, 1)
            dve.wait_ge(step, done + 3)
            nc.vector.tensor_copy(offset[:], need[:]).then_inc(counted, 1)
            dve.wait_ge(totals, ROUNDS + 2)
            nc.vector.tensor_tensor(limit[:], need[:], ps_c[:, 0:1], ALU.subtract).then_inc(step, 1)
            dve.wait_ge(step, done + 4)
            nc.vector.scalar_tensor_tensor(out=taken[:], in0=rank[:], scalar=limit[:], in1=equal[:],
                                           op0=ALU.is_le, op1=ALU.mult).then_inc(step, 1)
            dve.wait_ge(step, done + 5)
            dve.wait_ge(counted, ROUNDS + 2)
            nc.vector.tensor_tensor(chosen[:], taken[:], above[:], ALU.add).then_inc(step, 1)
            dve.wait_ge(step, done + 6)
            nc.vector.tensor_tensor_scan(place[:], chosen[:], zeros[:], 0.0, ALU.add, ALU.add).then_inc(counted, 1)
            dve.wait_ge(totals, ROUNDS + 3)
            nc.vector.tensor_copy(offset[:], ps_c[:, 0:1]).then_inc(step, 1)
            dve.wait_ge(step, done + 7)
            dve.wait_ge(counted, ROUNDS + 3)
            nc.vector.scalar_tensor_tensor(out=marked[:], in0=place[:], scalar=offset[:], in1=chosen[:],
                                           op0=ALU.add, op1=ALU.mult).then_inc(counted, 1)
            dve.wait_ge(turned, 2)
            nc.vector.tensor_scalar(place_i[:], ps_p[:].rearrange("p c n -> p (c n)"), -1.0, None, ALU.add
                                    ).then_inc(step, 1)
            dve.wait_ge(step, done + 8)
            nc.vector.tensor_scalar(hi_i[:], place_i[:], 7, None, ALU.arith_shift_right).then_inc(step, 1)
            nc.vector.tensor_scalar(lo_i[:], place_i[:], P - 1, None, ALU.bitwise_and).then_inc(step, 1)
            dve.wait_ge(step, done + 10)
            for to, of in ((places_hi, hi_i), (places_lo, lo_i)):
                for c in range(GC):
                    nc.vector.tensor_copy(to[:].rearrange("p e (g c) -> p c e g", c=GC)[:, c],
                                          of[:].rearrange("p (c e g) -> p c e g", c=GC, e=E)[:, c]).then_inc(step, 1)
            dve.wait_ge(step, done + 10 + 2 * GC)


def experts(nc, table, consts, fc1, fc2, b1, b2, ln_w, ln_b, places_hi, places_lo, out):
    TT = TOK // P
    KT = K // P
    HK = KT // 2
    WIDE = HK * P
    with ExitStack() as ctx:
        a = Alloc(nc, ctx)
        ident = a.sb("e_ident", [P, P])
        iota = a.sb("e_iota", [P, P])
        iota16 = a.sb("e_iota16", [P, P], BF16)
        tile_no = a.sb("e_tile_no", [P, TT, KT])
        row_no = a.sb("e_row_no", [P, 1])
        lnw = a.sb("e_lnw", [P, DC])
        lnb = a.sb("e_lnb", [P, DC])
        hi = a.sb("e_hi", [P, TT])
        lo = a.sb("e_lo", [P, TT])
        at_lo = a.sb("e_at_lo", [P, TT, P], BF16)
        at_hi = a.sb("e_at_hi", [P, TT, KT])
        number = a.sb("e_number", [P, TT, 2, KT], BF16)
        rows_p = a.sb("e_rows_p", [P, KT])
        idx = a.sb("e_idx", [P, 2, KT], U32)
        y = a.sb("e_y", [P, 2, KT, ROW])
        wk = a.sb("e_wk", [P, 2, KT])
        yT = a.sb("e_yT", [P, DC, K])
        w1 = a.sb("e_w1", [P, 2, DC, FF])
        w2 = a.sb("e_w2", [P, 2, FC, D])
        b1b = a.sb("e_b1b", [P, 2, FC])
        b2b = a.sb("e_b2b", [P, 2, D])
        hT = a.sb("e_hT", [P, FC, K])
        biased = a.sb("e_biased", [P, 2, D])
        ob = a.sb("e_ob", [P, KT, D])
        ahead = a.sb("e_ahead", [P, 1])
        ps_h = a.ps("e_ps_h", [P, 3, WIDE])
        ps_o = a.ps("e_ps_o", [P, 2, 512])
        ps_y = a.ps("e_ps_y", [P, 2, WIDE])
        ps_i = a.ps("e_ps_i", [P, 512])

        consts_in = a.sem("e_consts_in")
        w1_in = [a.sem(f"e_w1_in{k}") for k in range(2)]
        w2_in = [a.sem(f"e_w2_in{k}") for k in range(2)]
        gathered = [a.sem(f"e_gathered{k}") for k in range(2)]
        scattered = a.sem("e_scattered")
        iota_done = a.sem("e_iota_done")
        cur_done = a.sem("e_cur_done")
        at_hi_done = a.sem("e_at_hi_done")
        onehots_done = a.sem("e_onehots_done")
        listed = a.sem("e_listed")
        rows_p_done = a.sem("e_rows_p_done")
        idx_done = a.sem("e_idx_done")
        wk_done = a.sem("e_wk_done")
        turned = a.sem("e_turned")
        yT_done = a.sem("e_yT_done")
        h_done = a.sem("e_h_done")
        gelu_done = a.sem("e_gelu_done")
        o_done = a.sem("e_o_done")
        biased_done = a.sem("e_biased_done")
        ob_done = a.sem("e_ob_done")
        ahead_done = a.sem("e_ahead_done")
        block = ctx.enter_context(nc.Block())

        ONEHOTS = TT + 2
        GROUPS = 2 * DC
        HG = 2 * FC
        out_rows = out.rearrange("b n d -> (b n) d")

        def each(eng, step):
            with eng.Fori(0, E // 2 - 1) as it:
                for k in range(2):
                    step(it * 2 + k, k, True)
            step(E - 2, 0, True)
            step(E - 1, 1, False)

        @block.sync
        def _(sp):
            def load(e, k):
                sp.dma_start(w1[:, k], fc1[bass.ds(e, 1)].rearrange("o (c p) f -> p (o c) f", p=P)).then_inc(w1_in[k], 16)
                sp.dma_start(b1b[:, k], b1[bass.ds(e, 1)].rearrange("o p f -> (o p) f")).then_inc(w1_in[k], 16)
                if not isinstance(e, int):
                    sp.wait_ge(o_done, KT * (e - 1))
                    sp.wait_ge(biased_done, KT * (e - 1))
                sp.dma_start(w2[:, k], fc2[bass.ds(e, 1)].rearrange("o (c p) d -> p (o c) d", p=P)).then_inc(w2_in[k], 16)
                sp.dma_start(b2b[:, k], b2[bass.ds(e, 1)].to_broadcast([P, D])).then_inc(w2_in[k], 16)

            for buf, src in ((ident, consts["ident"]), (iota, consts["iota"]), (tile_no, consts["tile_no"]),
                             (row_no, consts["row_no"]), (lnw, ln_w), (lnb, ln_b)):
                sp.dma_start(buf[:], src).then_inc(consts_in, 16)
            for k in range(2):
                load(k, k)
            with sp.Fori(0, E // 2 - 1) as it:
                for k in range(2):
                    sp.wait_ge(h_done, HG * (it * 2 + k + 1))
                    sp.wait_ge(gelu_done, HG * (it * 2 + k + 1))
                    load(it * 2 + k + 2, k)
            sp.wait_ge(scattered, 16 * KT * E)

        @block.vector
        def _(dve):
            def onehots(e):
                dve.wait_ge(onehots_done, ONEHOTS * e)
                nc.vector.tensor_copy(hi[:], places_hi[:, bass.ds(e, 1)].rearrange("p o t -> p (o t)")).then_inc(cur_done, 1)
                nc.vector.tensor_copy(lo[:], places_lo[:, bass.ds(e, 1)].rearrange("p o t -> p (o t)")).then_inc(cur_done, 1)
                dve.wait_ge(cur_done, 2 * (e + 1))
                dve.wait_ge(listed, e)
                nc.vector.tensor_tensor(at_hi[:], hi[:].unsqueeze(2).to_broadcast([P, TT, KT]),
                                        iota[:, 0:KT].unsqueeze(1).to_broadcast([P, TT, KT]), ALU.is_equal
                                        ).then_inc(at_hi_done, 1)
                for t in range(TT):
                    nc.vector.tensor_scalar(at_lo[:, t], iota16[:], lo[:, t:t + 1], None, ALU.is_equal
                                            ).then_inc(onehots_done, 1)
                dve.wait_ge(at_hi_done, e + 1)
                nc.vector.tensor_tensor(number[:, :, 0], at_hi[:], tile_no[:], ALU.mult).then_inc(onehots_done, 1)
                nc.vector.tensor_scalar(number[:, :, 1], at_hi[:], row_no[:], None, ALU.mult).then_inc(onehots_done, 1)

            def indices(e, k):
                dve.wait_ge(listed, e + 1)
                dve.wait_ge(idx_done, e)
                nc.vector.tensor_copy(rows_p[:], ps_i[:, KT:2 * KT]).then_inc(rows_p_done, 1)
                dve.wait_ge(rows_p_done, e + 1)
                if not isinstance(e, int) or e >= 2:
                    dve.wait_ge(scattered, 16 * KT * (e - 1))
                nc.vector.scalar_tensor_tensor(out=idx[:, k], in0=ps_i[:, 0:KT], scalar=float(P), in1=rows_p[:],
                                               op0=ALU.mult, op1=ALU.add).then_inc(idx_done, 1)

            def affine(e, k):
                for h in range(2):
                    for c in range(DC):
                        g = h * DC + c
                        dve.wait_ge(turned, GROUPS * e + g + 1)
                        nc.vector.tensor_scalar(yT[:, c, h * WIDE:(h + 1) * WIDE], ps_y[:, g % 2],
                                                lnw[:, c:c + 1], lnb[:, c:c + 1], ALU.mult, ALU.add).then_inc(yT_done, 1)
                for h in range(2):
                    dve.wait_ge(gathered[h], 16 * HK * (e + 1))
                nc.vector.tensor_copy(wk[:, k], y[:, k, :, bass.ds(e + D, 1)].rearrange("p t o -> p (t o)")
                                      ).then_inc(wk_done, 1)

            def weigh(e, k):
                dve.wait_ge(w2_in[k], 32 * (e // 2 + 1) if isinstance(e, int) else (e - k) * 16 + 32)
                dve.wait_ge(wk_done, e + 1)
                for i in range(KT + 1):
                    if i < KT:
                        dve.wait_ge(o_done, KT * e + i + 1)
                        dve.wait_ge(ob_done, KT * e + max(i - 1, 0))
                        nc.vector.tensor_tensor(biased[:, i % 2], ps_o[:, i % 2, 0:D], b2b[:, k], ALU.add
                                                ).then_inc(biased_done, 1)
                    if i > 0:
                        dve.wait_ge(biased_done, KT * e + i)
                        dve.wait_ge(scattered, 16 * KT * e)
                        nc.vector.tensor_scalar(ob[:, i - 1], biased[:, (i - 1) % 2], wk[:, k, i - 1:i], None, ALU.mult
                                                ).then_inc(ob_done, 1)

            def step(e, k, more):
                if more:
                    onehots(e + 1)
                    indices(e + 1, 1 - k)
                weigh(e, k)
                if more:
                    affine(e + 1, 1 - k)

            dve.wait_ge(consts_in, 16 * 6)
            nc.vector.tensor_copy(iota16[:], iota[:]).then_inc(iota_done, 1)
            dve.wait_ge(iota_done, 1)
            onehots(0)
            indices(0, 0)
            affine(0, 0)
            each(dve, step)

        @block.gpsimd
        def _(pool):
            def carry_waits(n):
                pool.wait_ge(ahead_done, n)
                nc.gpsimd.tensor_tensor(ahead[:], row_no[:], row_no[:], ALU.add).then_inc(ahead_done, 1)

            def gather(e, k, first):
                pool.wait_ge(idx_done, e + 1)
                if not isinstance(e, int) or e >= 2:
                    pool.wait_ge(turned, GROUPS * (e - 1))
                    pool.wait_ge(wk_done, e - 1)
                carry_waits(first)
                for i in range(KT):
                    nc.gpsimd.indirect_dma_start(
                        out=y[:, k, i], out_offset=None, in_=table,
                        in_offset=bass.IndirectOffsetOnAxis(ap=idx[:, k, i:i + 1], axis=0)).then_inc(gathered[i // HK], 16)

            def step(e, k, more):
                if more:
                    gather(e + 1, 1 - k, (KT + 1) * e + 1)
                pool.wait_ge(scattered, 16 * KT * e)
                for i in range(KT):
                    pool.wait_ge(ob_done, KT * e + i + 1)
                    carry_waits((KT + 1) * e + 1 + more + i)
                    nc.gpsimd.indirect_dma_start(
                        out=out_rows, out_offset=bass.IndirectOffsetOnAxis(ap=idx[:, k, i:i + 1], axis=0),
                        in_=ob[:, i], in_offset=None, compute_op=ALU.add).then_inc(scattered, 16)

            pool.wait_ge(consts_in, 16 * 6)
            gather(0, 0, 0)
            each(pool, step)

        @block.scalar
        def _(act):
            def step(e, k, more):
                for g in range(HG):
                    h, f = g // FC, g % FC
                    act.wait_ge(h_done, HG * e + g + 1)
                    act.wait_ge(o_done, KT * e)
                    nc.scalar.activation(hT[:, f, h * WIDE:(h + 1) * WIDE], ps_h[:, g % 3], ACT.Gelu_apprx_tanh,
                                         bias=b1b[:, k, f:f + 1]).then_inc(gelu_done, 1)

            each(act, step)

        @block.tensor
        def _(pe):
            def list_tokens(e):
                pe.wait_ge(onehots_done, ONEHOTS * (e + 1))
                pe.wait_ge(idx_done, e)
                for t in range(TT):
                    mm = nc.tensor.matmul(ps_i[:, 0:2 * KT], at_lo[:, t], number[:, t].rearrange("p v k -> p (v k)"),
                                          start=(t == 0), stop=(t == TT - 1))
                mm.then_inc(listed, 1)

            def turn(e, k):
                for h in range(2):
                    pe.wait_ge(gathered[h], 16 * HK * (e + 1))
                    for c in range(DC):
                        g = h * DC + c
                        pe.wait_ge(yT_done, GROUPS * e + max(g - 1, 0))
                        for i in range(HK):
                            mm = nc.tensor.transpose(ps_y[:, g % 2, i * P:(i + 1) * P],
                                                     y[:, k, h * HK + i, c * P:(c + 1) * P], ident[:])
                        mm.then_inc(turned, 1)

            def step(e, k, more):
                pe.wait_ge(w1_in[k], 32 * (e // 2 + 1) if isinstance(e, int) else (e - k) * 16 + 32)
                for g in range(HG):
                    h, f = g // FC, g % FC
                    if f == 0:
                        pe.wait_ge(yT_done, GROUPS * e + DC * (h + 1))
                    pe.wait_ge(gelu_done, HG * e + max(g - 2, 0))
                    for c in range(DC):
                        mm = nc.tensor.matmul(ps_h[:, g % 3], w1[:, k, c, f * P:(f + 1) * P],
                                              yT[:, c, h * WIDE:(h + 1) * WIDE], start=(c == 0), stop=(c == DC - 1))
                    mm.then_inc(h_done, 1)
                if more:
                    list_tokens(e + 1)
                pe.wait_ge(w2_in[k], 32 * (e // 2 + 1) if isinstance(e, int) else (e - k) * 16 + 32)
                pe.wait_ge(gelu_done, HG * (e + 1))
                for i in range(KT):
                    pe.wait_ge(biased_done, KT * e + max(i - 1, 0))
                    for f in range(FC):
                        mm = nc.tensor.matmul(ps_o[:, i % 2, 0:D], hT[:, f, i * P:(i + 1) * P], w2[:, k, f],
                                              start=(f == 0), stop=(f == FC - 1))
                    mm.then_inc(o_done, 1)
                if more:
                    turn(e + 1, 1 - k)

            pe.wait_ge(consts_in, 16 * 6)
            list_tokens(0)
            turn(0, 0)
            each(pe, step)


def block_kernel(nc, t, out):
    parts = nc.dram_tensor("qkv_parts", (B * H, 2, PARTS, DH, N), BF16).ap()
    values = nc.dram_tensor("values", (B, PAIRS, P, TILES * 2 * 2 * DH), F32).ap()
    o = nc.dram_tensor("attended", (NP, 2, 4, 2 * DH, N // 4), F32).ap()
    rden = nc.dram_tensor("reciprocal_denominators", (B, P, P), F32).ap()
    table = nc.dram_tensor("token_table", (TOK, ROW), F32).ap()
    with ExitStack() as ctx:
        a = Alloc(nc, ctx)
        gate = a.sb("gate", [P, TOK // P, E])
        places_hi = a.sb("places_hi", [P, E, TOK // P])
        places_lo = a.sb("places_lo", [P, E, TOK // P])
        project(nc, t["x"], t["w_qkv"], t["rot_cos"], t["rot_sin"], t["ident"], parts, values)
        attend(nc, parts, values.rearrange("b r p n -> (b r) p n"), o, t["ident"])
        finish(nc, t["x"], o, rden, t["w_out"], t["b_out"], t["w_gate"], t["ident"], table, out, gate)
        choose(nc, gate, t, places_hi, places_lo)
        experts(nc, table, t, t["fc1"], t["fc2"], t["b1"], t["b2"], t["ln_w"], t["ln_b"], places_hi, places_lo, out)


def constants():
    i = np.arange(P)
    inv_freq = (1.0 / 10000.0 ** (np.arange(0, DH, 2, dtype=np.float32) / DH)).astype(np.float32)
    angle = np.outer(np.arange(N, dtype=np.float32), inv_freq).astype(np.float32)
    cos, sin = np.cos(angle), np.sin(angle)

    def by_tile(v):
        return v.reshape(TILES, P, DH).transpose(1, 0, 2)

    group = i // DH
    return {
        "ident": np.eye(P, dtype=np.float32),
        "rot_cos": by_tile(np.concatenate([cos, cos], -1)),
        "rot_sin": by_tile(np.concatenate([-sin, sin], -1)),
        "same": (group[:, None] == group[None]).astype(np.float32),
        "before": ((group[:, None] == group[None]) & (i[:, None] < i[None])).astype(np.float32),
        "bits": np.broadcast_to(np.array([[v << (2 * (ROUNDS - 1 - r)) for v in range(LEVELS)]
                                          for r in range(ROUNDS)], np.int32), (P, ROUNDS, LEVELS)),
        "iota": np.broadcast_to(i.astype(np.float32), (P, P)),
        "tile_no": np.broadcast_to(np.arange(TOK // P, dtype=np.float32)[None, :, None], (P, TOK // P, K // P)),
        "row_no": i.astype(np.float32)[:, None],
    }


def layout(L0_attn_x, L0_attn_Wq, L0_attn_Wkv, L0_attn_Wout, L0_attn_bout, L0_ffn_gate_w, L0_ffn_ln_w, L0_ffn_ln_b,
           L0_ffn_fc1s, L0_ffn_b1s, L0_ffn_fc2s, L0_ffn_b2s):
    return {
        "x": L0_attn_x,
        "w_qkv": np.concatenate([L0_attn_Wq, L0_attn_Wkv], axis=1),
        "w_out": L0_attn_Wout,
        "b_out": L0_attn_bout,
        "w_gate": L0_ffn_gate_w.T.reshape(DC, P, E).transpose(1, 0, 2),
        "ln_w": L0_ffn_ln_w.reshape(DC, P).T,
        "ln_b": L0_ffn_ln_b.reshape(DC, P).T,
        "fc1": L0_ffn_fc1s.transpose(0, 2, 1),
        "b1": L0_ffn_b1s.reshape(E, FC, P).transpose(0, 2, 1),
        "fc2": L0_ffn_fc2s.transpose(0, 2, 1),
        "b2": L0_ffn_b2s,
    }


def kernel(**inputs):
    import concourse.bacc as bacc
    from concourse.bass_utils import run_bass_kernel_spmd

    nc = bacc.Bacc("TRN2", target_bir_lowering=False, num_devices=1)
    arrays, aps = {}, {}
    for name, value in {**constants(), **layout(**{n: np.asarray(v) for n, v in inputs.items()})}.items():
        value = np.ascontiguousarray(value)
        arrays[f"in_{name}_dram"] = value
        aps[name] = nc.dram_tensor(f"in_{name}_dram", value.shape, mybir.dt.from_np(value.dtype),
                                   kind="ExternalInput").ap()
    out = nc.dram_tensor("out_0_dram", (B, N, D), F32, kind="ExternalOutput").ap()
    block_kernel(nc, aps, out)
    result = run_bass_kernel_spmd(nc, [arrays], core_ids=[0])
    return result.results[0]["out_0_dram"]
```

```python
from contextlib import ExitStack

import numpy as np

import concourse.bass as bass
from concourse import mybir

F32 = mybir.dt.float32
BF16 = mybir.dt.bfloat16
I32 = mybir.dt.int32
U32 = mybir.dt.uint32
ALU = mybir.AluOpType
ACT = mybir.ActivationFunctionType
AX = mybir.AxisListType

P = 128
B, N, D = 8, 1024, 256
H, DH = 16, 16
TILES = N // P
TOK = B * N
DC = D // P
HALF = DH // 2
PAIRS = H // 2
NP = B * PAIRS
PARTS = 3
EPS = 1e-5
E, FF = 8, 1024
K = TOK // E
FC = FF // P
ROW = D + E


class Alloc:

    def __init__(self, nc, ctx):
        self.nc, self.ctx = nc, ctx

    def sb(self, name, shape, dt=F32):
        return self.ctx.enter_context(self.nc.sbuf_tensor(name, shape, dt))

    def ps(self, name, shape, dt=F32):
        return self.ctx.enter_context(self.nc.psum_tensor(name, shape, dt))

    def sem(self, name):
        return self.ctx.enter_context(self.nc.semaphore(name))


def past(count, least=1):
    return not isinstance(count, int) or count >= least


class Flow:

    def __init__(self, step, passes):
        self.step, self.passes = step, passes

    def at(self, it, j, lag):
        turn = it if j >= lag else it - 1
        k = (j - lag) % self.step
        if isinstance(turn, int) and not 0 <= turn < self.passes:
            return None
        return turn, k, turn * self.step + k

    def run(self, eng, body, last_lag):
        for j in range(self.step):
            body(0, j)
        with eng.Fori(1, self.passes) as it:
            for j in range(self.step):
                body(it, j)
        for j in range(last_lag):
            body(self.passes, j)


def project(nc, x, w_qkv, rot_cos, rot_sin, ident_d, parts_dram, v_dram):
    SEQS = 2
    STEP = SEQS * TILES
    PASSES = B // SEQS
    GROUP = 4
    GROUPS = STEP // GROUP
    NORM, PROJ, TURN, BACK, CUT, LAST = 6, 7, 8, 10, 11, 12
    with ExitStack() as ctx:
        a = Alloc(nc, ctx)
        ident = a.sb("p_ident", [P, P])
        w = a.sb("p_w", [P, DC, 2 * D])
        cosb = a.sb("p_cos", [P, TILES, DH])
        sinb = a.sb("p_sin", [P, TILES, DH])
        xb = a.sb("p_x", [P, STEP, D])
        stats = a.sb("p_stats", [P, STEP, 6])
        mv = a.sb("p_mv", [P, STEP, 2])
        veps = a.sb("p_veps", [P, STEP])
        rstd = a.sb("p_rstd", [P, STEP])
        mhalf = a.sb("p_mhalf", [P, GROUP])
        epsb = a.sb("p_epsb", [P, GROUP])
        ahead = a.sb("p_ahead", [P, 1])
        xn = a.sb("p_xn", [P, 2, D])
        xnT = a.sb("p_xnT", [P, 2, DC, P])
        qkv = a.sb("p_qkv", [P, 2, 2 * D])
        t_cos = a.sb("p_tcos", [P, 2, 2 * D])
        t_sin = a.sb("p_tsin", [P, 2 * D])
        rot = a.sb("p_rot", [P, 2, 2 * D])
        vaug = a.sb("p_vaug", [P, SEQS, PAIRS, TILES, 2, 2 * DH])
        parts = a.sb("p_parts", [P, SEQS, 4, PARTS, N], BF16)
        rest = a.sb("p_rest", [P, 2, 4, P])
        ps_xT = a.ps("p_ps_xT", [P, 2, 4, P])
        ps_q = a.ps("p_ps_q", [P, 2, 4 * P])
        ps_rT = a.ps("p_ps_rT", [P, 2, 4, P])

        consts_in = a.sem("p_consts_in")
        x_in = [a.sem(f"p_x_in{g}") for g in range(GROUPS)]
        parts_out = [a.sem(f"p_parts_out{s}") for s in range(SEQS)]
        v_out = [a.sem(f"p_v_out{s}") for s in range(SEQS)]
        ones_set = a.sem("p_ones_set")
        stats_done = a.sem("p_stats_done")
        mv_done = a.sem("p_mv_done")
        veps_done = a.sem("p_veps_done")
        rstd_done = a.sem("p_rstd_done")
        xn_done = a.sem("p_xn_done")
        xT_done = a.sem("p_xT_done")
        xnT_done = a.sem("p_xnT_done")
        q_done = a.sem("p_q_done")
        qkv_done = a.sem("p_qkv_done")
        cos_done = a.sem("p_cos_done")
        sin_done = a.sem("p_sin_done")
        rot_done = a.sem("p_rot_done")
        vaug_done = a.sem("p_vaug_done")
        rT_done = a.sem("p_rT_done")
        part1_done = a.sem("p_part1_done")
        rest_done = a.sem("p_rest_done")
        part2_done = a.sem("p_part2_done")
        part3_done = a.sem("p_part3_done")
        block = ctx.enter_context(nc.Block())

        x_v = x.rearrange("b (g i p) d -> (b g) p i d", p=P, i=GROUP)
        flow = Flow(STEP, PASSES)

        @block.sync
        def _(sp):
            def load(it, g):
                if past(it):
                    sp.wait_ge(xn_done, it * STEP + ((g + 1) * GROUP - STEP))
                sp.dma_start(xb[:, g * GROUP:(g + 1) * GROUP],
                             x_v[bass.ds(it * GROUPS + g, 1)].rearrange("o p i d -> p (o i) d")).then_inc(x_in[g], 16)

            def store(it, s):
                done = it * STEP + (s + 1) * TILES
                sp.wait_ge(part1_done, done)
                sp.wait_ge(part2_done, done)
                sp.wait_ge(part3_done, done)
                for c in range(4):
                    kind, chunk = c // 2, c % 2
                    for part in range(PARTS):
                        sp.dma_start(
                            parts_dram[bass.ds((it * SEQS + s) * H + chunk * 8, 8), kind, part],
                            parts[:, s, c, part]).then_inc(parts_out[s], 16)
                sp.wait_ge(vaug_done, done)
                sp.dma_start(v_dram[bass.ds(it * SEQS + s, 1)].rearrange("o r p n -> p (o r) n"),
                             vaug[:, s].rearrange("p r i h e -> p r (i h e)")).then_inc(v_out[s], 16)

            def body(it):
                load(it + 1, 0)
                if past(it):
                    store(it - 1, 1)
                load(it + 1, 1)
                load(it + 1, 2)
                store(it, 0)
                load(it + 1, 3)

            load(0, 0)
            sp.dma_start(w[:], w_qkv.rearrange("(c p) n -> p c n", p=P)).then_inc(consts_in, 16)
            sp.dma_start(ident[:], ident_d).then_inc(consts_in, 16)
            sp.dma_start(cosb[:], rot_cos).then_inc(consts_in, 16)
            sp.dma_start(sinb[:], rot_sin).then_inc(consts_in, 16)
            for g in range(1, GROUPS):
                load(0, g)
            body(0)
            with sp.Fori(1, PASSES - 1) as it:
                body(it)
            store(PASSES - 2, 1)
            for s in range(SEQS):
                store(PASSES - 1, s)
            for s in range(SEQS):
                sp.wait_ge(parts_out[s], 16 * 4 * PARTS * PASSES)
                sp.wait_ge(v_out[s], 16 * PASSES)

        @block.vector
        def _(dve):
            def statistics(it, k, n):
                g = k // GROUP
                if k % GROUP == 0:
                    dve.wait_ge(x_in[g], 16 * (it + 1))
                nc.vector.bn_stats(stats[:, k], xb[:, k]).then_inc(stats_done, 1)
                if k % GROUP == GROUP - 1:
                    dve.wait_ge(stats_done, (GROUP + 1) * GROUPS * it + (GROUP + 1) * (g + 1) - 1)
                    nc.vector.memset(ahead[:], 0.0).then_inc(stats_done, 1)
                    for t in range(g * GROUP, (g + 1) * GROUP):
                        nc.vector.bn_aggr(mv[:, t], stats[:, t]).then_inc(mv_done, 1)

            def normalise(it, k, n):
                dve.wait_ge(rstd_done, it * GROUPS + (k // GROUP + 1))
                if past(n, 2):
                    dve.wait_ge(xT_done, n - 1)
                nc.vector.tensor_scalar(xn[:, k % 2], xb[:, k], mv[:, k, 0:1], rstd[:, k:k + 1],
                                        ALU.subtract, ALU.mult).then_inc(xn_done, 1)

            def cos_product(it, k, n):
                i = k % TILES
                dve.wait_ge(qkv_done, n + 1)
                if past(n, 2):
                    dve.wait_ge(rot_done, n - 1)
                nc.vector.tensor_tensor(t_cos[:, k % 2].rearrange("p (h d) -> p h d", d=DH),
                                        qkv[:, k % 2].rearrange("p (h d) -> p h d", d=DH),
                                        cosb[:, i:i + 1, :].to_broadcast([P, 2 * H, DH]),
                                        ALU.mult).then_inc(cos_done, 1)

            def rest_of(it, k, n):
                s, i = k // TILES, k % TILES
                dve.wait_ge(part1_done, n + 1)
                if past(n, 2):
                    dve.wait_ge(part3_done, n - 1)
                nc.vector.tensor_tensor(rest[:, k % 2], ps_rT[:, k % 2], parts[:, s, :, 0, i * P:(i + 1) * P],
                                        ALU.subtract).then_inc(rest_done, 1)

            def third_part(it, k, n):
                s, i = k // TILES, k % TILES
                cols = slice(i * P, (i + 1) * P)
                dve.wait_ge(part2_done, n + 1)
                nc.vector.tensor_tensor(parts[:, s, :, 2, cols], rest[:, k % 2], parts[:, s, :, 1, cols],
                                        ALU.subtract).then_inc(part3_done, 1)

            def body(it, j):
                for stage, lag in ((statistics, 0), (normalise, NORM), (cos_product, TURN), (rest_of, CUT),
                                   (third_part, LAST)):
                    tile = flow.at(it, j, lag)
                    if tile:
                        stage(*tile)

            nc.vector.memset(mhalf[:], -0.5).then_inc(ones_set, 1)
            nc.vector.memset(epsb[:], EPS).then_inc(ones_set, 1)
            nc.vector.memset(vaug[:], 1.0).then_inc(ones_set, 1)
            dve.wait_ge(consts_in, 64)
            flow.run(dve, body, LAST)

        @block.gpsimd
        def _(pool):
            def inverse_root(it, k, n):
                g = k // GROUP
                cols = slice(g * GROUP, (g + 1) * GROUP)
                pool.wait_ge(mv_done, n + 1)
                nc.gpsimd.tensor_tensor(veps[:, cols], mv[:, cols, 1], epsb[:], ALU.add).then_inc(veps_done, 1)
                pool.wait_ge(veps_done, it * GROUPS + (g + 1))
                nc.gpsimd.tensor_tensor(rstd[:, cols], veps[:, cols], mhalf[:], ALU.pow).then_inc(rstd_done, 1)

            def turn(it, k, n):
                i = k % TILES
                src = qkv[:, k % 2].rearrange("p (h d) -> p h d", d=DH)
                ts = t_sin[:].rearrange("p (h d) -> p h d", d=DH)
                pool.wait_ge(qkv_done, n + 1)
                if past(n):
                    pool.wait_ge(rot_done, n)
                for h in range(2):
                    nc.gpsimd.tensor_tensor(
                        ts[:, :, h * HALF:(h + 1) * HALF], src[:, :, (1 - h) * HALF:(2 - h) * HALF],
                        sinb[:, i:i + 1, h * HALF:(h + 1) * HALF].to_broadcast([P, 2 * H, HALF]),
                        ALU.mult).then_inc(sin_done, 1)
                pool.wait_ge(cos_done, n + 1)
                pool.wait_ge(sin_done, n * 2 + 2)
                if past(n, 2):
                    pool.wait_ge(rT_done, n - 1)
                    pool.wait_ge(vaug_done, n - 1)
                nc.gpsimd.tensor_tensor(rot[:, k % 2], t_cos[:, k % 2], t_sin[:], ALU.add).then_inc(rot_done, 1)

            def body(it, j):
                tile = flow.at(it, j, 0)
                if tile and j % GROUP == GROUP - 1:
                    inverse_root(*tile)
                tile = flow.at(it, j, TURN)
                if tile:
                    turn(*tile)

            pool.wait_ge(consts_in, 64)
            pool.wait_ge(ones_set, 3)
            flow.run(pool, body, TURN)

        @block.scalar
        def _(act):
            def turned_tokens(it, k, n):
                act.wait_ge(xT_done, n + 1)
                if past(n, 2):
                    act.wait_ge(q_done, n - 1)
                nc.scalar.copy(xnT[:, k % 2], ps_xT[:, k % 2, 0:DC]).then_inc(xnT_done, 1)

            def projected(it, k, n):
                act.wait_ge(q_done, n + 1)
                if past(n, 2):
                    act.wait_ge(rot_done, n - 1)
                nc.scalar.copy(qkv[:, k % 2], ps_q[:, k % 2]).then_inc(qkv_done, 1)

            def first_part(it, k, n):
                s, i = k // TILES, k % TILES
                if i == 0 and past(it):
                    act.wait_ge(parts_out[s], 16 * 4 * PARTS * it)
                    act.wait_ge(v_out[s], 16 * it)
                act.wait_ge(rT_done, n + 1)
                nc.scalar.copy(parts[:, s, :, 0, i * P:(i + 1) * P], ps_rT[:, k % 2]).then_inc(part1_done, 1)
                nc.scalar.copy(vaug[:, s, :, i, :, 0:DH],
                               rot[:, k % 2, D:2 * D].rearrange("p (r h d) -> p r h d", h=2, d=DH)
                               ).then_inc(vaug_done, 1)

            def second_part(it, k, n):
                s, i = k // TILES, k % TILES
                act.wait_ge(rest_done, n + 1)
                nc.scalar.copy(parts[:, s, :, 1, i * P:(i + 1) * P], rest[:, k % 2]).then_inc(part2_done, 1)

            def body(it, j):
                for stage, lag in ((turned_tokens, NORM), (projected, PROJ), (first_part, BACK), (second_part, CUT)):
                    tile = flow.at(it, j, lag)
                    if tile:
                        stage(*tile)

            act.wait_ge(ones_set, 3)
            flow.run(act, body, CUT)

        @block.tensor
        def _(pe):
            def turn_tokens(it, k, n):
                pe.wait_ge(xn_done, n + 1)
                if past(n, 2):
                    pe.wait_ge(xnT_done, n - 1)
                for c in range(DC):
                    mm = nc.tensor.transpose(ps_xT[:, k % 2, c], xn[:, k % 2, c * P:(c + 1) * P], ident[:])
                mm.then_inc(xT_done, 1)

            def products(it, k, n):
                pe.wait_ge(xnT_done, n + 1)
                if past(n, 2):
                    pe.wait_ge(qkv_done, n - 1)
                for c in range(DC):
                    mm = nc.tensor.matmul(ps_q[:, k % 2], xnT[:, k % 2, c], w[:, c], start=(c == 0), stop=(c == DC - 1))
                mm.then_inc(q_done, 1)

            def turn_back(it, k, n):
                pe.wait_ge(rot_done, n + 1)
                if past(n, 2):
                    pe.wait_ge(rest_done, n - 1)
                for c in range(4):
                    mm = nc.tensor.transpose(ps_rT[:, k % 2, c], rot[:, k % 2, c * P:(c + 1) * P], ident[:])
                mm.then_inc(rT_done, 1)

            def body(it, j):
                for stage, lag in ((turn_tokens, NORM), (products, PROJ), (turn_back, BACK)):
                    tile = flow.at(it, j, lag)
                    if tile:
                        stage(*tile)

            pe.wait_ge(consts_in, 64)
            flow.run(pe, body, BACK)


SLOTS = ((0, 0), (1, 1), (0, 1), (1, 0), (2, 0), (0, 2))
SLOT_ROW = ([0, 16, 32, 48, 64, 80], [64, 80, 96, 112, 0, 16])
MAX_ROW = (96, 32)
MAX_PARTS = 2


def slot_runs(h, kind):
    runs = []
    for row, of in zip(SLOT_ROW[h], SLOTS):
        part = of[kind]
        if runs and runs[-1][0] + runs[-1][2] * DH == row and runs[-1][1] + runs[-1][2] == part:
            runs[-1][2] += 1
        else:
            runs.append([row, part, 1])
    return runs


CHUNK = 512
QUARTER = N // 4


def attend(nc, parts_dram, v_dram, o_dram, ident_d):
    NG = 2 * TILES
    with ExitStack() as ctx:
        a = Alloc(nc, ctx)
        identb = a.sb("a_identb", [P, P], BF16)
        identf = a.sb("a_identf", [P, P])
        qb = a.sb("a_q", [P, 3, 2, N], BF16)
        kb = a.sb("a_k", [P, 3, 2, N], BF16)
        vb = a.sb("a_v", [P, 3, TILES, 2, 2 * DH])
        prob = a.sb("a_prob", [P, 4, N])
        mx = a.sb("a_mx", [P, TILES, 2, 2])
        nm = a.sb("a_nm", [P, TILES, 2])
        nsplit = a.sb("a_nsplit", [P, 2, MAX_PARTS, TILES], BF16)
        zero = a.sb("a_zero", [P, TILES, 2])
        mrow = a.sb("a_mrow", [2 * MAX_PARTS * TILES, P], BF16)
        oraw = a.sb("a_oraw", [P, 2, QUARTER])
        sm = a.ps("a_sm", [P, 2, 2, CHUNK])
        st = a.ps("a_st", [P, 3, CHUNK])
        pv = a.ps("a_pv", [P, CHUNK])

        set_up = a.sem("a_set_up")
        ident_in = a.sem("a_ident_in")
        identb_set = a.sem("a_identb_set")
        qk_in = [a.sem(f"a_qk_in{i}") for i in range(3)]
        v_in = [a.sem(f"a_v_in{i}") for i in range(3)]
        m_in = a.sem("a_m_in")
        o_out = [a.sem(f"a_o_out{i}") for i in range(2)]
        sm_done = a.sem("a_sm_done")
        max_done = a.sem("a_max_done")
        nm_done = a.sem("a_nm_done")
        n1_done = a.sem("a_n1_done")
        n2_done = a.sem("a_n2_done")
        mT_done = a.sem("a_mT_done")
        mrow_done = a.sem("a_mrow_done")
        st_done = a.sem("a_st_done")
        exp_done = a.sem("a_exp_done")
        pv_done = a.sem("a_pv_done")
        evac_done = a.sem("a_evac_done")
        block = ctx.enter_context(nc.Block())
        QK_LOADS = sum(len(slot_runs(h, kind)) for h in range(2) for kind in range(2))
        UNITS = 2 * NG
        AHEAD = NG + NG // 2
        turned = pv[0:2 * MAX_PARTS * TILES, QUARTER:QUARTER + P // 2].bitcast(BF16)

        class Pair:

            def __init__(self, k, c, p=None):
                self.k, self.c, self.p = k, c, p
                self.n = k * 3 + c
                self.buf = c % 3
                self.turn = k + c // 3

            def plus(self, d):
                return Pair(self.k, self.c + d, None if self.p is None else self.p + d)

            def exists(self):
                return self.p is None or self.p < NP

            def first(self):
                return self.p == 0

        def pairs(eng, body):
            body(Pair(0, 0, 0))
            with eng.Fori(0, (NP - 4) // 3) as k:
                for c in range(1, 4):
                    body(Pair(k, c))
            for p in range(NP - 3, NP):
                body(Pair(0, p, p))

        @block.sync
        def _(sp):
            def load(q):
                if not (q.p is not None and q.p < 3):
                    sp.wait_ge(st_done, (q.n - 2) * UNITS)
                for h in range(2):
                    for kind, buf in ((0, qb), (1, kb)):
                        for row, part, parts in slot_runs(h, kind):
                            sp.dma_start(buf[row:row + parts * DH, q.buf, h, :],
                                         parts_dram[bass.ds(q.n * 2 + h, 1), kind, part:part + parts]
                                         .rearrange("o s d n -> (o s d) n")).then_inc(qk_in[q.buf], 16)
                if not (q.p is not None and q.p < 3):
                    sp.wait_ge(pv_done, (q.n - 2) * NG)
                sp.dma_start(vb[:, q.buf].rearrange("p i h e -> p (i h e)"),
                             v_dram[bass.ds(q.n, 1)].rearrange("o p n -> (o p) n")).then_inc(v_in[q.buf], 16)

            def store(q, h):
                sp.wait_ge(evac_done, q.n * 2 + h + 1)
                sp.dma_start(o_dram[bass.ds(q.n, 1), h].rearrange("o c r n -> (o c r) n"), oraw[:, h]
                             ).then_inc(o_out[h], 16)

            def max_rows(q):
                sp.wait_ge(mrow_done, q.n + 1)
                rows = MAX_PARTS * TILES
                for h in range(2):
                    sp.dma_start(qb[MAX_ROW[h]:MAX_ROW[h] + MAX_PARTS, q.buf, h, :].rearrange("r (t c) -> r t c", c=P),
                                 mrow[h * rows:(h + 1) * rows, :]).then_inc(m_in, 16)

            def body(q):
                if not q.first() and q.plus(2).exists():
                    load(q.plus(2))
                if not q.first():
                    store(q.plus(-1), 1)
                store(q, 0)
                if q.plus(1).exists():
                    max_rows(q.plus(1))

            sp.dma_start(identf[:], ident_d).then_inc(ident_in, 16)
            sp.wait_ge(set_up, 4)
            for p in range(3):
                load(Pair(0, p, p))
            max_rows(Pair(0, 0, 0))
            pairs(sp, body)
            store(Pair(0, NP - 1, NP - 1), 1)
            for h in range(2):
                sp.wait_ge(o_out[h], 16 * NP)

        @block.tensor
        def _(pe):
            def scores(q, g, ic):
                h, jt = g // TILES, g % TILES
                u = g * 2 + ic
                slot = (q.c * UNITS + u) % 3
                if g == 0 and ic == 0:
                    pe.wait_ge(m_in, (q.n + 1) * 32)
                if not (q.first() and u < 3):
                    pe.wait_ge(exp_done, q.n * UNITS + (u - 2))
                nc.tensor.matmul(st[:, slot], kb[:, q.buf, h, jt * P:(jt + 1) * P],
                                 qb[:, q.buf, h, ic * CHUNK:(ic + 1) * CHUNK],
                                 start=True, stop=True).then_inc(st_done, 1)

            def values(q, g):
                h, jt = g // TILES, g % TILES
                if g == 0:
                    pe.wait_ge(v_in[q.buf], (q.turn + 1) * 16)
                if jt == 0 and not (q.first() and g == 0):
                    pe.wait_ge(evac_done, q.n * 2 + h)
                if jt == 0 and not (h == 1 and not q.plus(1).exists()):
                    pe.wait_ge(mrow_done, q.n + 1 + h)
                pe.wait_ge(exp_done, q.n * UNITS + 2 * g + 2)
                for c in range(4):
                    mm = nc.tensor.matmul(pv[32 * c:32 * c + 32, 0:QUARTER], vb[:, q.buf, jt, h, :],
                                          prob[:, g % 4, c * QUARTER:(c + 1) * QUARTER],
                                          start=(jt == 0), stop=(jt == TILES - 1))
                mm.then_inc(pv_done, 1)

            def maxima(q, v, slot):
                qt, kc = v // 2, v % 2
                if v == 0:
                    pe.wait_ge(qk_in[q.buf], (q.turn + 1) * 16 * QK_LOADS)
                for h in range(2):
                    rows = slice(64 * h, 64 * h + 64)
                    mm = nc.tensor.matmul(sm[:, slot, h], qb[rows, q.buf, h, qt * P:(qt + 1) * P],
                                          kb[rows, q.buf, h, kc * CHUNK:(kc + 1) * CHUNK], start=True, stop=True)
                mm.then_inc(sm_done, 1)

            def turn_maxima(q):
                pe.wait_ge(n2_done, q.n + 1)
                nc.tensor.transpose(turned, nsplit[:].rearrange("p h s t -> p (h s t)"), identb[:]).then_inc(mT_done, 1)

            def body(q):
                seen = q.n * NG + AHEAD
                for g in range(NG):
                    scores(q, g, 0)
                    if g >= 2:
                        values(q, g - 2)
                        if g - 2 == TILES - 1 and q.plus(1).exists():
                            turn_maxima(q.plus(1))
                    elif not q.first():
                        values(q.plus(-1), NG + g - 2)
                    scores(q, g, 1)
                    ahead = q.plus(1) if g < NG // 2 else q.plus(2)
                    if ahead.exists():
                        pe.wait_ge(max_done, seen + g - 1)
                        maxima(ahead, (g + NG // 2) % NG, g % 2)

            pe.wait_ge(set_up, 4)
            pe.wait_ge(identb_set, 1)
            q0, q1 = Pair(0, 0, 0), Pair(0, 1, 1)
            for v in range(NG):
                if v >= 2:
                    pe.wait_ge(max_done, v - 1)
                maxima(q0, v, v % 2)
            turn_maxima(q0)
            for v in range(NG // 2):
                pe.wait_ge(max_done, NG + v - 1)
                maxima(q1, v, v % 2)
            pairs(pe, body)
            last = Pair(0, NP - 1, NP - 1)
            values(last, NG - 2)
            values(last, NG - 1)

        @block.vector
        def _(dve):
            def reduce(q, v, s, slot):
                qt, kc = v // 2, v % 2
                if v == 0 and not q.first():
                    dve.wait_ge(nm_done, q.n)
                dve.wait_ge(sm_done, s + 1)
                nc.vector.tensor_reduce(mx[:, qt, kc, :], sm[:, slot], AX.X, ALU.max,
                                        negate=True).then_inc(max_done, 1)
                if v == NG - 1:
                    if not q.first():
                        dve.wait_ge(n2_done, q.n)
                    dve.wait_ge(max_done, (q.n + 1) * NG)
                    nc.vector.tensor_tensor(nm[:], mx[:, :, 0], mx[:, :, 1], ALU.min).then_inc(nm_done, 1)

            def body(q):
                for g in range(NG):
                    ahead = q.plus(1) if g < NG // 2 else q.plus(2)
                    if ahead.exists():
                        reduce(ahead, (g + NG // 2) % NG, q.n * NG + AHEAD + g, g % 2)

            nc.vector.memset(qb[:].bitcast(U32), 0).then_inc(set_up, 1)
            nc.vector.memset(kb[:].bitcast(U32), 0).then_inc(set_up, 1)
            nc.vector.memset(zero[:], 0.0).then_inc(set_up, 1)
            dve.wait_ge(set_up, 3)
            nc.vector.memset(kb[MAX_ROW[0]:MAX_ROW[0] + MAX_PARTS, :, 0], 1.0).then_inc(identb_set, 1)
            nc.vector.memset(kb[MAX_ROW[1]:MAX_ROW[1] + MAX_PARTS, :, 1], 1.0).then_inc(set_up, 1)
            dve.wait_ge(ident_in, 16)
            nc.vector.tensor_copy(identb[:], identf[:]).then_inc(identb_set, 1)
            for v in range(NG):
                reduce(Pair(0, 0, 0), v, v, v % 2)
            for v in range(NG // 2):
                reduce(Pair(0, 1, 1), v, NG + v, v % 2)
            pairs(dve, body)

        @block.gpsimd
        def _(pool):
            def split(q):
                part = [nsplit[:, :, s, :].rearrange("p h t -> p t h") for s in range(MAX_PARTS)]
                pool.wait_ge(nm_done, q.n + 1)
                if not q.first():
                    pool.wait_ge(mT_done, q.n)
                nc.gpsimd.tensor_tensor(part[0], nm[:], zero[:], ALU.add).then_inc(n1_done, 1)
                pool.wait_ge(n1_done, q.n + 1)
                nc.gpsimd.tensor_tensor(part[1], nm[:], part[0], ALU.subtract).then_inc(n2_done, 1)

            pool.wait_ge(set_up, 4)
            pairs(pool, split)

        @block.scalar
        def _(act):
            def exp(q, g, ic):
                u = g * 2 + ic
                act.wait_ge(st_done, q.n * UNITS + u + 1)
                if ic == 0 and not (q.first() and g < 4):
                    act.wait_ge(pv_done, q.n * NG + g - 3)
                nc.scalar.activation(prob[:, g % 4, ic * CHUNK:(ic + 1) * CHUNK], st[:, (q.c * UNITS + u) % 3],
                                     ACT.Exp, scale=DH ** -0.5).then_inc(exp_done, 1)

            def evacuate(q, h):
                act.wait_ge(pv_done, q.n * NG + (h + 1) * TILES)
                if not q.first():
                    act.wait_ge(o_out[h], q.n * 16)
                nc.scalar.copy(oraw[:, h], pv[:, 0:QUARTER]).then_inc(evac_done, 1)

            def copy_max_rows(q):
                act.wait_ge(mT_done, q.n + 1)
                if not q.first():
                    act.wait_ge(m_in, q.n * 32)
                nc.scalar.copy(mrow[:], turned).then_inc(mrow_done, 1)

            def body(q):
                for g in range(NG):
                    exp(q, g, 0)
                    if g == 1 and not q.first():
                        evacuate(q.plus(-1), 1)
                    if g == 9:
                        if q.plus(1).exists():
                            act.wait_ge(mT_done, q.n + 2)
                        evacuate(q, 0)
                        if q.plus(1).exists():
                            copy_max_rows(q.plus(1))
                    exp(q, g, 1)

            copy_max_rows(Pair(0, 0, 0))
            pairs(act, body)
            evacuate(Pair(0, NP - 1, NP - 1), 1)


def finish(nc, x, o_dram, rden_dram, w_out, b_out, w_gate, ident_d, table, out, gate):
    SEQS = 2
    STEP = SEQS * TILES
    PASSES = B // SEQS
    GROUP = 2
    PROJ, STAT, NORM, TURN, LOGITS, NORM2, BACK, CENTRE, SHARE = 3, 4, 7, 8, 9, 11, 11, 12, 13
    LGROUP = 4
    with ExitStack() as ctx:
        a = Alloc(nc, ctx)
        ident = a.sb("f_ident", [P, P])
        w = a.sb("f_w", [P, DC, D])
        wg = a.sb("f_wg", [P, DC, E])
        bo = a.sb("f_bo", [PARTS, D])
        bo_rest = a.sb("f_bo_rest", [PARTS, D])
        bo_part = a.sb("f_bo_part", [PARTS, PARTS, D], BF16)
        bo_rows = a.sb("f_bo_rows", [PARTS, D], BF16)
        ones = a.sb("f_ones", [PARTS, P], BF16)
        mhalf = a.sb("f_mhalf", [P, GROUP])
        epsb = a.sb("f_epsb", [P, GROUP])
        ahead = a.sb("f_ahead", [P, 1])
        den = a.sb("f_den", [P, B, P])
        rden = a.sb("f_rden", [P, B, P])
        num = a.sb("f_num", [P, SEQS, DC, N])
        rrep = a.sb("f_rrep", [P, SEQS, DC, N])
        o = a.sb("f_o", [P, SEQS, DC, N])
        xb = a.sb("f_x", [P, STEP, D])
        x2 = a.sb("f_x2", [P, STEP, D])
        xf = a.sb("f_xf", [P, STEP, D])
        tab = a.sb("f_tab", [P, STEP, ROW])
        stats = a.sb("f_stats", [P, 2, STEP, 6])
        mv = a.sb("f_mv", [P, 2, STEP, 2])
        veps = a.sb("f_veps", [P, 2, STEP])
        rstd = a.sb("f_rstd", [P, 2, STEP])
        xfT = a.sb("f_xfT", [P, 2, DC, P])
        lT = a.sb("f_lT", [E, 2, LGROUP * P])
        lmax = a.sb("f_lmax", [P, TILES])
        lcen = a.sb("f_lcen", [P, TILES, E])
        lexp = a.sb("f_lexp", [P, TILES, E])
        lsum = a.sb("f_lsum", [P, TILES])
        lrec = a.sb("f_lrec", [P, TILES])
        ps_y = a.ps("f_ps_y", [P, 2, 512])
        ps_xT = a.ps("f_ps_xT", [P, 2, 4, P])
        ps_lT = a.ps("f_ps_lT", [P, 2, LGROUP * P])
        ps_l = a.ps("f_ps_l", [P, 2, 512])

        consts_in = a.sem("f_consts_in")
        set_up = a.sem("f_set_up")
        den_in = [a.sem("f_den_in_first"), a.sem("f_den_in_others")]
        rden_out = [a.sem("f_rden_out_first"), a.sem("f_rden_out_others")]
        num_in = [a.sem(f"f_num_in{s}") for s in range(SEQS)]
        x_in = [a.sem(f"f_x_in{s}") for s in range(SEQS)]
        out_out = [a.sem(f"f_out_out{s}") for s in range(SEQS)]
        tab_out = [a.sem(f"f_tab_out{s}") for s in range(SEQS)]
        bias_done = a.sem("f_bias_done")
        rden_done = a.sem("f_rden_done")
        o_done = a.sem("f_o_done")
        y_done = a.sem("f_y_done")
        x2_done = a.sem("f_x2_done")
        stats_done = [a.sem(f"f_stats_done{v}") for v in range(2)]
        mv_done = [a.sem(f"f_mv_done{v}") for v in range(2)]
        veps_done = [a.sem(f"f_veps_done{v}") for v in range(2)]
        rstd_done = [a.sem(f"f_rstd_done{v}") for v in range(2)]
        xf_done = a.sem("f_xf_done")
        xT_done = a.sem("f_xT_done")
        xfT_done = a.sem("f_xfT_done")
        logits_done = a.sem("f_logits_done")
        lT_done = a.sem("f_lT_done")
        back_done = a.sem("f_back_done")
        yn_done = a.sem("f_yn_done")
        base_done = a.sem("f_base_done")
        lmax_done = a.sem("f_lmax_done")
        lcen_done = a.sem("f_lcen_done")
        lexp_done = a.sem("f_lexp_done")
        lsum_done = a.sem("f_lsum_done")
        lrec_done = a.sem("f_lrec_done")
        gate_done = a.sem("f_gate_done")
        scores_done = a.sem("f_scores_done")
        block = ctx.enter_context(nc.Block())

        x_v = x.rearrange("b (i p) d -> b p i d", p=P)
        out_v = out.rearrange("b (i p) d -> b p i d", p=P)
        table_v = table.rearrange("(b i p) e -> b p i e", p=P, i=TILES)
        HC = PAIRS // DC
        NUM_LOADS = DC * 4 + DC
        flow = Flow(STEP, PASSES)

        def one(v):
            return bass.ds(v, 1)

        def tiles_of(s):
            return slice(s * TILES, (s + 1) * TILES)

        @block.sync
        def _(sp):
            def load_num(it, s):
                b = it * SEQS + s
                if past(it):
                    sp.wait_ge(o_done, DC * SEQS * it + DC * (s + 1 - SEQS))
                for ch in range(DC):
                    for c in range(4):
                        sp.dma_start(num[:, s, ch, c * QUARTER:(c + 1) * QUARTER],
                                     o_dram[bass.ds(b * PAIRS + ch * HC, HC), :, c, 0:DH, :]
                                     .rearrange("n h r x -> (n h) r x")).then_inc(num_in[s], 16)

            def load_rrep(it, s):
                b = it * SEQS + s
                for ch in range(DC):
                    sp.dma_start(rrep[:, s, ch],
                                 rden_dram[one(b), ch * 64:(ch + 1) * 64].rearrange("o (k q) n -> (o k) (q n)", q=TILES)
                                 .unsqueeze(1).to_broadcast([2 * HC, DH, N])).then_inc(num_in[s], 16)

            def load_x(it, s):
                if past(it):
                    sp.wait_ge(x2_done, it * STEP + (s + 1 - SEQS) * TILES)
                sp.dma_start(xb[:, tiles_of(s)], x_v[one(it * SEQS + s)].rearrange("o p i d -> p (o i) d")
                             ).then_inc(x_in[s], 16)

            def load_den(b):
                sp.dma_start(den[:, b], o_dram[bass.ds(b * PAIRS, PAIRS), :, :, DH, :]
                             .rearrange("n h c (f x) -> (n h c) f x", f=2)).then_inc(den_in[b > 0], 16)

            def store_rden(b):
                sp.dma_start(rden_dram[b], rden[:, b]).then_inc(rden_out[b > 0], 16)

            def store_out(it, s):
                sp.wait_ge(base_done, it * STEP + (s + 1) * TILES)
                sp.dma_start(out_v[one(it * SEQS + s)].rearrange("o p i d -> p (o i) d"), x2[:, tiles_of(s)]
                             ).then_inc(out_out[s], 16)

            def store_tab(it, s):
                done = it * STEP + (s + 1) * TILES
                sp.wait_ge(yn_done, done)
                sp.wait_ge(scores_done, done)
                sp.dma_start(table_v[one(it * SEQS + s)].rearrange("o p i e -> p (o i) e"), tab[:, tiles_of(s)]
                             ).then_inc(tab_out[s], 16)

            def body(it):
                load_num(it + 1, 0)
                load_rrep(it + 1, 0)
                if past(it):
                    store_tab(it - 1, 0)
                    store_out(it - 1, 1)
                load_x(it + 1, 0)
                load_num(it + 1, 1)
                load_rrep(it + 1, 1)
                if past(it):
                    store_tab(it - 1, 1)
                store_out(it, 0)
                load_x(it + 1, 1)

            load_den(0)
            load_num(0, 0)
            sp.wait_ge(rden_done, 1)
            store_rden(0)
            sp.dma_start(bo[:], b_out.rearrange("(o n) -> o n", o=1).to_broadcast([PARTS, D])).then_inc(consts_in, 16)
            sp.dma_start(ident[:], ident_d).then_inc(consts_in, 16)
            sp.dma_start(w[:], w_out.rearrange("(c p) n -> p c n", p=P)).then_inc(consts_in, 16)
            sp.dma_start(wg[:], w_gate).then_inc(consts_in, 16)
            sp.wait_ge(rden_out[0], 16)
            load_rrep(0, 0)
            load_x(0, 0)
            for b in range(1, B):
                load_den(b)
            load_num(0, 1)
            load_x(0, 1)
            for b in range(1, B):
                sp.wait_ge(rden_done, b + 1)
                store_rden(b)
            sp.wait_ge(rden_out[1], 16 * (B - 1))
            load_rrep(0, 1)
            body(0)
            with sp.Fori(1, PASSES - 1) as it:
                body(it)
            last = PASSES - 1
            store_tab(last - 1, 0)
            store_out(last - 1, 1)
            store_tab(last - 1, 1)
            for s in range(SEQS):
                store_out(last, s)
                store_tab(last, s)
            for s in range(SEQS):
                sp.wait_ge(out_out[s], 16 * PASSES)
                sp.wait_ge(tab_out[s], 16 * PASSES)

        @block.gpsimd
        def _(pool):
            def divide(it, k, n):
                s = k // TILES
                pool.wait_ge(num_in[s], 16 * NUM_LOADS * (it + 1))
                if past(n, STEP):
                    pool.wait_ge(y_done, n - TILES)
                for ch in range(DC):
                    nc.gpsimd.tensor_tensor(o[:, s, ch], num[:, s, ch], rrep[:, s, ch], ALU.mult).then_inc(o_done, 1)

            def inverse_root(v, it, k, n):
                cols = slice(k + 1 - GROUP, k + 1)
                count = it * (STEP // GROUP) + (k // GROUP + 1)
                pool.wait_ge(mv_done[v], n + 1)
                nc.gpsimd.tensor_tensor(veps[:, v, cols], mv[:, v, cols, 1], epsb[:], ALU.add).then_inc(veps_done[v], 1)
                pool.wait_ge(veps_done[v], count)
                nc.gpsimd.tensor_tensor(rstd[:, v, cols], veps[:, v, cols], mhalf[:], ALU.pow
                                        ).then_inc(rstd_done[v], 1)

            def base(it, k, n):
                pool.wait_ge(xf_done, n + 1)
                nc.gpsimd.tensor_tensor(x2[:, k], x2[:, k], xf[:, k], ALU.add).then_inc(base_done, 1)

            def body(it, j):
                for v, lag in ((0, STAT), (1, TURN)):
                    tile = flow.at(it, j, lag)
                    if tile and tile[1] % GROUP == GROUP - 1:
                        inverse_root(v, *tile)
                tile = flow.at(it, j, TURN)
                if tile:
                    base(*tile)
                tile = flow.at(it, j, 0)
                if tile and j % TILES == 0:
                    divide(*tile)

            pool.wait_ge(set_up, 3)
            flow.run(pool, body, TURN)

        @block.vector
        def _(dve):
            def residual(it, k, n):
                s = k // TILES
                if k % TILES == 0:
                    dve.wait_ge(x_in[s], 16 * (it + 1))
                    if past(it):
                        dve.wait_ge(out_out[s], 16 * it)
                dve.wait_ge(y_done, n + 1)
                nc.vector.tensor_tensor(x2[:, k], ps_y[:, k % 2, 0:D], xb[:, k], ALU.add).then_inc(x2_done, 1)

            def statistics(v, buf, made, it, k, n):
                dve.wait_ge(made, n + 1)
                nc.vector.bn_stats(stats[:, v, k], buf[:, k]).then_inc(stats_done[v], 1)
                if k % GROUP == GROUP - 1:
                    groups = it * (STEP // GROUP) * (GROUP + 1)
                    dve.wait_ge(stats_done[v], groups + (k // GROUP + 1) * (GROUP + 1) - 1)
                    nc.vector.memset(ahead[:], 0.0).then_inc(stats_done[v], 1)
                    for t in range(k + 1 - GROUP, k + 1):
                        nc.vector.bn_aggr(mv[:, v, t], stats[:, v, t]).then_inc(mv_done[v], 1)

            def normalise(it, k, n):
                dve.wait_ge(rstd_done[0], it * (STEP // GROUP) + (k // GROUP + 1))
                nc.vector.tensor_scalar(xf[:, k], x2[:, k], mv[:, 0, k, 0:1], rstd[:, 0, k:k + 1],
                                        ALU.subtract, ALU.mult).then_inc(xf_done, 1)

            def normalise_again(it, k, n):
                s = k // TILES
                if k % TILES == 0 and past(it):
                    dve.wait_ge(tab_out[s], 16 * it)
                dve.wait_ge(rstd_done[1], it * (STEP // GROUP) + (k // GROUP + 1))
                nc.vector.tensor_scalar(tab[:, k, 0:D], xf[:, k], mv[:, 1, k, 0:1], rstd[:, 1, k:k + 1],
                                        ALU.subtract, ALU.mult).then_inc(yn_done, 1)

            def centre(it, k, n):
                s = k // TILES
                count = it * SEQS + (s + 1)
                lg = ps_l[:, s, 0:TILES * E].rearrange("p (i e) -> p i e", e=E)
                dve.wait_ge(back_done, it * (STEP // LGROUP) + (k + 1) // LGROUP)
                nc.vector.tensor_reduce(lmax[:], lg, AX.X, ALU.max).then_inc(lmax_done, 1)
                dve.wait_ge(lmax_done, count)
                nc.vector.tensor_tensor(lcen[:], lg, lmax[:].unsqueeze(2).to_broadcast([P, TILES, E]),
                                        ALU.subtract).then_inc(lcen_done, 1)

            def share(it, k, n):
                s = k // TILES
                count = it * SEQS + (s + 1)
                dve.wait_ge(lexp_done, count)
                nc.vector.tensor_reduce(lsum[:], lexp[:], AX.X, ALU.add).then_inc(lsum_done, 1)
                dve.wait_ge(lsum_done, count)
                nc.vector.reciprocal(lrec[:], lsum[:]).then_inc(lrec_done, 1)
                dve.wait_ge(lrec_done, count)
                nc.vector.tensor_tensor(gate[:, bass.ds(it * STEP + s * TILES, TILES), :], lexp[:],
                                        lrec[:].unsqueeze(2).to_broadcast([P, TILES, E]), ALU.mult).then_inc(gate_done, 1)

            def split_bias():
                dve.wait_ge(consts_in, 64)
                left = bo
                for v in range(PARTS):
                    if v > 0:
                        dve.wait_ge(bias_done, 3 * v)
                    nc.vector.tensor_copy(bo_part[:, v], left[:]).then_inc(bias_done, 1)
                    dve.wait_ge(bias_done, 3 * v + 1)
                    nc.vector.tensor_tensor(bo_rest[:], left[:], bo_part[:, v], ALU.subtract).then_inc(bias_done, 1)
                    if v == 0:
                        nc.vector.tensor_scalar(bo_rows[:], bo_part[:, 0], ident[0:PARTS, 0:1], None, ALU.mult
                                                ).then_inc(bias_done, 1)
                    else:
                        nc.vector.scalar_tensor_tensor(out=bo_rows[:], in0=bo_part[:, v], scalar=ident[0:PARTS, v:v + 1],
                                                       in1=bo_rows[:], op0=ALU.mult, op1=ALU.add).then_inc(bias_done, 1)
                    left = bo_rest

            def body(it, j):
                if isinstance(it, int) and it == 0 and 1 <= j < B:
                    dve.wait_ge(den_in[1], 16 * (B - 1))
                    nc.vector.reciprocal(rden[:, j], den[:, j]).then_inc(rden_done, 1)
                tile = flow.at(it, j, PROJ)
                if tile:
                    residual(*tile)
                tile = flow.at(it, j, STAT)
                if tile:
                    statistics(0, x2, x2_done, *tile)
                tile = flow.at(it, j, NORM)
                if tile:
                    normalise(*tile)
                tile = flow.at(it, j, TURN)
                if tile:
                    statistics(1, xf, xf_done, *tile)
                tile = flow.at(it, j, CENTRE)
                if tile and tile[1] % TILES == TILES - 1:
                    centre(*tile)
                tile = flow.at(it, j, NORM2)
                if tile:
                    normalise_again(*tile)
                tile = flow.at(it, j, SHARE)
                if tile and tile[1] % TILES == TILES - 1:
                    share(*tile)

            nc.vector.memset(mhalf[:], -0.5).then_inc(set_up, 1)
            nc.vector.memset(epsb[:], EPS).then_inc(set_up, 1)
            nc.vector.memset(ones[:], 1.0).then_inc(set_up, 1)
            dve.wait_ge(den_in[0], 16)
            nc.vector.reciprocal(rden[:, 0], den[:, 0]).then_inc(rden_done, 1)
            split_bias()
            flow.run(dve, body, SHARE)

        @block.scalar
        def _(act):
            def turned(it, k, n):
                act.wait_ge(xT_done, n + 1)
                if past(n, 2):
                    act.wait_ge(logits_done, n - 1)
                nc.scalar.copy(xfT[:, k % 2], ps_xT[:, k % 2, 0:DC]).then_inc(xfT_done, 1)

            def turned_logits(it, k, n):
                group = it * (STEP // LGROUP) + k // LGROUP
                act.wait_ge(logits_done, n + 1)
                if past(group, 2):
                    act.wait_ge(back_done, group - 1)
                nc.scalar.copy(lT[:, (k // LGROUP) % 2], ps_lT[0:E, (k // LGROUP) % 2]).then_inc(lT_done, 1)

            def exponential(it, k, n):
                s = k // TILES
                act.wait_ge(lcen_done, it * SEQS + (s + 1))
                if past(n, TILES):
                    act.wait_ge(gate_done, it * SEQS + s)
                nc.scalar.activation(lexp[:], lcen[:], ACT.Exp).then_inc(lexp_done, 1)

            def scores(it, k, n):
                s = k // TILES
                act.wait_ge(gate_done, it * SEQS + (s + 1))
                if past(it):
                    act.wait_ge(tab_out[s], 16 * it)
                nc.scalar.copy(tab[:, tiles_of(s), D:ROW], gate[:, bass.ds(it * STEP + s * TILES, TILES), :]
                               ).then_inc(scores_done, TILES)

            def body(it, j):
                tile = flow.at(it, j, TURN)
                if tile:
                    turned(*tile)
                tile = flow.at(it, j, LOGITS)
                if tile and tile[1] % LGROUP == LGROUP - 1:
                    turned_logits(*tile)
                for stage, lag in ((exponential, CENTRE), (scores, SHARE)):
                    tile = flow.at(it, j, lag)
                    if tile and tile[1] % TILES == TILES - 1:
                        stage(*tile)

            flow.run(act, body, SHARE)

        @block.tensor
        def _(pe):
            def project_tile(it, k, n):
                s, i = k // TILES, k % TILES
                if i == 0:
                    pe.wait_ge(o_done, DC * SEQS * it + DC * (s + 1))
                if past(n, 2):
                    pe.wait_ge(x2_done, n - 1)
                for ch in range(DC):
                    nc.tensor.matmul(ps_y[:, k % 2, 0:D], o[:, s, ch, i * P:(i + 1) * P], w[:, ch],
                                     start=(ch == 0), stop=False)
                nc.tensor.matmul(ps_y[:, k % 2, 0:D], ones[:], bo_rows[:], start=False, stop=True).then_inc(y_done, 1)

            def turn(it, k, n):
                pe.wait_ge(xf_done, n + 1)
                if past(n, 2):
                    pe.wait_ge(xfT_done, n - 1)
                for c in range(DC):
                    mm = nc.tensor.transpose(ps_xT[:, k % 2, c], xf[:, k, c * P:(c + 1) * P], ident[:])
                mm.then_inc(xT_done, 1)

            def logits(it, k, n):
                group = it * (STEP // LGROUP) + k // LGROUP
                i = k % LGROUP
                pe.wait_ge(xfT_done, n + 1)
                if i == 0 and past(group, 2):
                    pe.wait_ge(lT_done, group - 1)
                for c in range(DC):
                    mm = nc.tensor.matmul(ps_lT[0:E, (k // LGROUP) % 2, i * P:(i + 1) * P], wg[:, c], xfT[:, k % 2, c],
                                          start=(c == 0), stop=(c == DC - 1))
                mm.then_inc(logits_done, 1)

            def turn_back(it, k, n):
                s = k // TILES
                pe.wait_ge(lT_done, it * (STEP // LGROUP) + (k // LGROUP + 1))
                if k % TILES < LGROUP and past(it):
                    pe.wait_ge(lcen_done, it * SEQS + (s + 1 - SEQS))
                for t in range(LGROUP):
                    i = k % TILES + 1 - LGROUP + t
                    mm = nc.tensor.matmul(ps_l[:, s, i * E:(i + 1) * E], lT[:, (k // LGROUP) % 2, t * P:(t + 1) * P],
                                          ident[0:E, 0:E], start=True, stop=True)
                mm.then_inc(back_done, 1)

            def body(it, j):
                for stage, lag in ((project_tile, PROJ), (turn, TURN), (logits, LOGITS)):
                    tile = flow.at(it, j, lag)
                    if tile:
                        stage(*tile)
                tile = flow.at(it, j, BACK)
                if tile and tile[1] % LGROUP == LGROUP - 1:
                    turn_back(*tile)

            pe.wait_ge(consts_in, 64)
            pe.wait_ge(set_up, 3)
            pe.wait_ge(bias_done, 3 * PARTS)
            flow.run(pe, body, BACK)


ROUNDS = 15
LEVELS = 4


def choose(nc, gate, consts, places_hi, places_lo):
    GROUP = TOK // 16
    GC = GROUP // P
    with ExitStack() as ctx:
        a = Alloc(nc, ctx)
        ident = a.sb("c_ident", [P, P])
        same = a.sb("c_same", [P, P])
        before = a.sb("c_before", [P, P])
        bits = a.sb("c_bits", [P, ROUNDS, LEVELS], I32)
        by_group = a.sb("c_by_group", [P, GC, E, 16])
        score = a.sb("c_score", [P, GROUP])
        mark = a.sb("c_mark", [P, LEVELS, GROUP], BF16)
        zeros = a.sb("c_zeros", [P, GROUP])
        best = a.sb("c_best", [P, 1])
        cand = a.sb("c_cand", [P, LEVELS])
        held = a.sb("c_held", [P, LEVELS])
        count = a.sb("c_count", [P, LEVELS])
        above = a.sb("c_above", [P, GROUP])
        n_above = a.sb("c_n_above", [P, 1])
        equal = a.sb("c_equal", [P, GROUP])
        rank = a.sb("c_rank", [P, GROUP])
        need = a.sb("c_need", [P, 1])
        limit = a.sb("c_limit", [P, 1])
        taken = a.sb("c_taken", [P, GROUP])
        chosen = a.sb("c_chosen", [P, GROUP])
        place = a.sb("c_place", [P, GROUP])
        offset = a.sb("c_offset", [P, 1])
        marked = a.sb("c_marked", [P, GROUP])
        place_i = a.sb("c_place_i", [P, GROUP], I32)
        hi_i = a.sb("c_hi_i", [P, GROUP], I32)
        lo_i = a.sb("c_lo_i", [P, GROUP], I32)
        ps_t = a.ps("c_ps_t", [P, GC, P])
        ps_c = a.ps("c_ps_c", [P, 512])
        ps_p = a.ps("c_ps_p", [P, GC, P])

        consts_in = a.sem("c_consts_in")
        grouped = a.sem("c_grouped")
        turned = a.sem("c_turned")
        counted = a.sem("c_counted")
        totals = a.sem("c_totals")
        step = a.sem("c_step")
        block = ctx.enter_context(nc.Block())

        @block.sync
        def _(sp):
            for buf, name in ((ident, "ident"), (same, "same"), (before, "before"), (bits, "bits")):
                sp.dma_start(buf[:], consts[name]).then_inc(consts_in, 16)

        @block.tensor
        def _(pe):
            pe.wait_ge(consts_in, 64)
            pe.wait_ge(grouped, GC)
            for c in range(GC):
                mm = nc.tensor.transpose(ps_t[:, c], by_group[:, c].rearrange("p e g -> p (e g)"), ident[:])
            mm.then_inc(turned, 1)
            with pe.Fori(0, ROUNDS) as r:
                pe.wait_ge(counted, r + 1)
                nc.tensor.matmul(ps_c[:, 0:LEVELS], same[:], count[:], start=True, stop=True).then_inc(totals, 1)
            pe.wait_ge(counted, ROUNDS + 1)
            nc.tensor.matmul(ps_c[:, 0:1], same[:], n_above[:], start=True, stop=True).then_inc(totals, 1)
            pe.wait_ge(counted, ROUNDS + 2)
            nc.tensor.matmul(ps_c[:, 0:1], before[:], rank[:, GROUP - 1:GROUP], start=True, stop=True
                             ).then_inc(totals, 1)
            pe.wait_ge(counted, ROUNDS + 3)
            nc.tensor.matmul(ps_c[:, 0:1], before[:], place[:, GROUP - 1:GROUP], start=True, stop=True
                             ).then_inc(totals, 1)
            pe.wait_ge(counted, ROUNDS + 4)
            for c in range(GC):
                mm = nc.tensor.transpose(ps_p[:, c], marked[:, c * P:(c + 1) * P], ident[:])
            mm.then_inc(turned, 1)

        @block.vector
        def _(dve):
            for c in range(GC):
                nc.vector.tensor_copy(by_group[:, c], gate[:].rearrange("p (g c) e -> p c e g", c=GC)[:, c]
                                      ).then_inc(grouped, 1)
            nc.vector.memset(zeros[:], 0.0).then_inc(step, 1)
            nc.vector.memset(best[:], 0.0).then_inc(step, 1)
            dve.wait_ge(consts_in, 64)
            dve.wait_ge(turned, 1)
            nc.vector.tensor_copy(score[:], ps_t[:].rearrange("p c n -> p (c n)")).then_inc(step, 1)
            SET_UP, EACH = 3, LEVELS + 3
            with dve.Fori(0, ROUNDS) as r:
                done = r * EACH + SET_UP
                dve.wait_ge(step, done)
                nc.vector.tensor_tensor(cand[:].bitcast(I32), bits[:, bass.ds(r, 1), :].rearrange("p o l -> p (o l)"),
                                        best[:].bitcast(I32).to_broadcast([P, LEVELS]), ALU.bitwise_or).then_inc(step, 1)
                dve.wait_ge(step, done + 1)
                for v in range(LEVELS):
                    nc.vector.tensor_scalar(mark[:, v], score[:], cand[:, v:v + 1], 0.0, ALU.is_ge, ALU.add,
                                            accum_out=count[:, v:v + 1]).then_inc(step if v < LEVELS - 1 else counted, 1)
                dve.wait_ge(totals, r + 1)
                nc.vector.scalar_tensor_tensor(out=held[:], in0=ps_c[:, 0:LEVELS], scalar=float(K), in1=cand[:],
                                               op0=ALU.is_ge, op1=ALU.mult).then_inc(step, 1)
                dve.wait_ge(step, done + LEVELS + 1)
                nc.vector.tensor_reduce(best[:], held[:], AX.X, ALU.max).then_inc(step, 2)
            done = ROUNDS * EACH + SET_UP
            dve.wait_ge(step, done)
            nc.vector.tensor_scalar(above[:], score[:], best[:], 0.0, ALU.is_gt, ALU.add, accum_out=n_above[:]
                                    ).then_inc(counted, 1)
            nc.vector.tensor_scalar(equal[:], score[:], best[:], None, ALU.is_equal).then_inc(step, 1)
            dve.wait_ge(step, done + 1)
            nc.vector.tensor_tensor_scan(rank[:], equal[:], zeros[:], 0.0, ALU.add, ALU.add).then_inc(step, 1)
            dve.wait_ge(totals, ROUNDS + 1)
            nc.vector.tensor_scalar(need[:], ps_c[:, 0:1], -1.0, float(K), ALU.mult, ALU.add).then_inc(step, 1)
            dve.wait_ge(step, done + 3)
            nc.vector.tensor_copy(offset[:], need[:]).then_inc(counted, 1)
            dve.wait_ge(totals, ROUNDS + 2)
            nc.vector.tensor_tensor(limit[:], need[:], ps_c[:, 0:1], ALU.subtract).then_inc(step, 1)
            dve.wait_ge(step, done + 4)
            nc.vector.scalar_tensor_tensor(out=taken[:], in0=rank[:], scalar=limit[:], in1=equal[:],
                                           op0=ALU.is_le, op1=ALU.mult).then_inc(step, 1)
            dve.wait_ge(step, done + 5)
            dve.wait_ge(counted, ROUNDS + 2)
            nc.vector.tensor_tensor(chosen[:], taken[:], above[:], ALU.add).then_inc(step, 1)
            dve.wait_ge(step, done + 6)
            nc.vector.tensor_tensor_scan(place[:], chosen[:], zeros[:], 0.0, ALU.add, ALU.add).then_inc(counted, 1)
            dve.wait_ge(totals, ROUNDS + 3)
            nc.vector.tensor_copy(offset[:], ps_c[:, 0:1]).then_inc(step, 1)
            dve.wait_ge(step, done + 7)
            dve.wait_ge(counted, ROUNDS + 3)
            nc.vector.scalar_tensor_tensor(out=marked[:], in0=place[:], scalar=offset[:], in1=chosen[:],
                                           op0=ALU.add, op1=ALU.mult).then_inc(counted, 1)
            dve.wait_ge(turned, 2)
            nc.vector.tensor_scalar(place_i[:], ps_p[:].rearrange("p c n -> p (c n)"), -1.0, None, ALU.add
                                    ).then_inc(step, 1)
            dve.wait_ge(step, done + 8)
            nc.vector.tensor_scalar(hi_i[:], place_i[:], 7, None, ALU.arith_shift_right).then_inc(step, 1)
            nc.vector.tensor_scalar(lo_i[:], place_i[:], P - 1, None, ALU.bitwise_and).then_inc(step, 1)
            dve.wait_ge(step, done + 10)
            for to, of in ((places_hi, hi_i), (places_lo, lo_i)):
                for c in range(GC):
                    nc.vector.tensor_copy(to[:].rearrange("p e (g c) -> p c e g", c=GC)[:, c],
                                          of[:].rearrange("p (c e g) -> p c e g", c=GC, e=E)[:, c]).then_inc(step, 1)
            dve.wait_ge(step, done + 10 + 2 * GC)


def experts(nc, table, consts, fc1, fc2, b1, b2, ln_w, ln_b, places_hi, places_lo, out):
    TT = TOK // P
    KT = K // P
    HK = KT // 2
    WIDE = HK * P
    with ExitStack() as ctx:
        a = Alloc(nc, ctx)
        ident = a.sb("e_ident", [P, P])
        iota = a.sb("e_iota", [P, P])
        iota16 = a.sb("e_iota16", [P, P], BF16)
        tile_no = a.sb("e_tile_no", [P, TT, KT])
        row_no = a.sb("e_row_no", [P, 1])
        lnw = a.sb("e_lnw", [P, DC])
        lnb = a.sb("e_lnb", [P, DC])
        hi = a.sb("e_hi", [P, TT])
        lo = a.sb("e_lo", [P, TT])
        at_lo = a.sb("e_at_lo", [P, TT, P], BF16)
        at_hi = a.sb("e_at_hi", [P, TT, KT])
        number = a.sb("e_number", [P, TT, 2, KT], BF16)
        rows_p = a.sb("e_rows_p", [P, KT])
        idx = a.sb("e_idx", [P, 2, KT], U32)
        y = a.sb("e_y", [P, 2, KT, ROW])
        wk = a.sb("e_wk", [P, 2, KT])
        yT = a.sb("e_yT", [P, DC, K])
        w1 = a.sb("e_w1", [P, 2, DC, FF])
        w2 = a.sb("e_w2", [P, 2, FC, D])
        b1b = a.sb("e_b1b", [P, 2, FC])
        b2b = a.sb("e_b2b", [P, 2, D])
        hT = a.sb("e_hT", [P, FC, K])
        biased = a.sb("e_biased", [P, 2, D])
        ob = a.sb("e_ob", [P, KT, D])
        ahead = a.sb("e_ahead", [P, 1])
        ps_h = a.ps("e_ps_h", [P, 3, WIDE])
        ps_o = a.ps("e_ps_o", [P, 2, 512])
        ps_y = a.ps("e_ps_y", [P, 2, WIDE])
        ps_i = a.ps("e_ps_i", [P, 512])

        consts_in = a.sem("e_consts_in")
        w1_in = [a.sem(f"e_w1_in{k}") for k in range(2)]
        w2_in = [a.sem(f"e_w2_in{k}") for k in range(2)]
        gathered = [a.sem(f"e_gathered{k}") for k in range(2)]
        scattered = a.sem("e_scattered")
        iota_done = a.sem("e_iota_done")
        cur_done = a.sem("e_cur_done")
        at_hi_done = a.sem("e_at_hi_done")
        onehots_done = a.sem("e_onehots_done")
        listed = a.sem("e_listed")
        rows_p_done = a.sem("e_rows_p_done")
        idx_done = a.sem("e_idx_done")
        wk_done = a.sem("e_wk_done")
        turned = a.sem("e_turned")
        yT_done = a.sem("e_yT_done")
        h_done = a.sem("e_h_done")
        gelu_done = a.sem("e_gelu_done")
        o_done = a.sem("e_o_done")
        biased_done = a.sem("e_biased_done")
        ob_done = a.sem("e_ob_done")
        ahead_done = a.sem("e_ahead_done")
        block = ctx.enter_context(nc.Block())

        ONEHOTS = TT + 2
        GROUPS = 2 * DC
        HG = 2 * FC
        out_rows = out.rearrange("b n d -> (b n) d")

        def each(eng, step):
            with eng.Fori(0, E // 2 - 1) as it:
                for k in range(2):
                    step(it * 2 + k, k, True)
            step(E - 2, 0, True)
            step(E - 1, 1, False)

        @block.sync
        def _(sp):
            def load(e, k):
                sp.dma_start(w1[:, k], fc1[bass.ds(e, 1)].rearrange("o (c p) f -> p (o c) f", p=P)).then_inc(w1_in[k], 16)
                sp.dma_start(b1b[:, k], b1[bass.ds(e, 1)].rearrange("o p f -> (o p) f")).then_inc(w1_in[k], 16)
                if not isinstance(e, int):
                    sp.wait_ge(o_done, KT * (e - 1))
                    sp.wait_ge(biased_done, KT * (e - 1))
                sp.dma_start(w2[:, k], fc2[bass.ds(e, 1)].rearrange("o (c p) d -> p (o c) d", p=P)).then_inc(w2_in[k], 16)
                sp.dma_start(b2b[:, k], b2[bass.ds(e, 1)].to_broadcast([P, D])).then_inc(w2_in[k], 16)

            for buf, src in ((ident, consts["ident"]), (iota, consts["iota"]), (tile_no, consts["tile_no"]),
                             (row_no, consts["row_no"]), (lnw, ln_w), (lnb, ln_b)):
                sp.dma_start(buf[:], src).then_inc(consts_in, 16)
            for k in range(2):
                load(k, k)
            with sp.Fori(0, E // 2 - 1) as it:
                for k in range(2):
                    sp.wait_ge(h_done, HG * (it * 2 + k + 1))
                    sp.wait_ge(gelu_done, HG * (it * 2 + k + 1))
                    load(it * 2 + k + 2, k)
            sp.wait_ge(scattered, 16 * KT * E)

        @block.vector
        def _(dve):
            def onehots(e):
                dve.wait_ge(onehots_done, ONEHOTS * e)
                nc.vector.tensor_copy(hi[:], places_hi[:, bass.ds(e, 1)].rearrange("p o t -> p (o t)")).then_inc(cur_done, 1)
                nc.vector.tensor_copy(lo[:], places_lo[:, bass.ds(e, 1)].rearrange("p o t -> p (o t)")).then_inc(cur_done, 1)
                dve.wait_ge(cur_done, 2 * (e + 1))
                dve.wait_ge(listed, e)
                nc.vector.tensor_tensor(at_hi[:], hi[:].unsqueeze(2).to_broadcast([P, TT, KT]),
                                        iota[:, 0:KT].unsqueeze(1).to_broadcast([P, TT, KT]), ALU.is_equal
                                        ).then_inc(at_hi_done, 1)
                for t in range(TT):
                    nc.vector.tensor_scalar(at_lo[:, t], iota16[:], lo[:, t:t + 1], None, ALU.is_equal
                                            ).then_inc(onehots_done, 1)
                dve.wait_ge(at_hi_done, e + 1)
                nc.vector.tensor_tensor(number[:, :, 0], at_hi[:], tile_no[:], ALU.mult).then_inc(onehots_done, 1)
                nc.vector.tensor_scalar(number[:, :, 1], at_hi[:], row_no[:], None, ALU.mult).then_inc(onehots_done, 1)

            def indices(e, k):
                dve.wait_ge(listed, e + 1)
                dve.wait_ge(idx_done, e)
                nc.vector.tensor_copy(rows_p[:], ps_i[:, KT:2 * KT]).then_inc(rows_p_done, 1)
                dve.wait_ge(rows_p_done, e + 1)
                if not isinstance(e, int) or e >= 2:
                    dve.wait_ge(scattered, 16 * KT * (e - 1))
                nc.vector.scalar_tensor_tensor(out=idx[:, k], in0=ps_i[:, 0:KT], scalar=float(P), in1=rows_p[:],
                                               op0=ALU.mult, op1=ALU.add).then_inc(idx_done, 1)

            def affine(e, k):
                for h in range(2):
                    for c in range(DC):
                        g = h * DC + c
                        dve.wait_ge(turned, GROUPS * e + g + 1)
                        nc.vector.tensor_scalar(yT[:, c, h * WIDE:(h + 1) * WIDE], ps_y[:, g % 2],
                                                lnw[:, c:c + 1], lnb[:, c:c + 1], ALU.mult, ALU.add).then_inc(yT_done, 1)
                for h in range(2):
                    dve.wait_ge(gathered[h], 16 * HK * (e + 1))
                nc.vector.tensor_copy(wk[:, k], y[:, k, :, bass.ds(e + D, 1)].rearrange("p t o -> p (t o)")
                                      ).then_inc(wk_done, 1)

            def weigh(e, k):
                dve.wait_ge(w2_in[k], 32 * (e // 2 + 1) if isinstance(e, int) else (e - k) * 16 + 32)
                dve.wait_ge(wk_done, e + 1)
                for i in range(KT + 1):
                    if i < KT:
                        dve.wait_ge(o_done, KT * e + i + 1)
                        dve.wait_ge(ob_done, KT * e + max(i - 1, 0))
                        nc.vector.tensor_tensor(biased[:, i % 2], ps_o[:, i % 2, 0:D], b2b[:, k], ALU.add
                                                ).then_inc(biased_done, 1)
                    if i > 0:
                        dve.wait_ge(biased_done, KT * e + i)
                        dve.wait_ge(scattered, 16 * KT * e)
                        nc.vector.tensor_scalar(ob[:, i - 1], biased[:, (i - 1) % 2], wk[:, k, i - 1:i], None, ALU.mult
                                                ).then_inc(ob_done, 1)

            def step(e, k, more):
                if more:
                    onehots(e + 1)
                    indices(e + 1, 1 - k)
                weigh(e, k)
                if more:
                    affine(e + 1, 1 - k)

            dve.wait_ge(consts_in, 16 * 6)
            nc.vector.tensor_copy(iota16[:], iota[:]).then_inc(iota_done, 1)
            dve.wait_ge(iota_done, 1)
            onehots(0)
            indices(0, 0)
            affine(0, 0)
            each(dve, step)

        @block.gpsimd
        def _(pool):
            def carry_waits(n):
                pool.wait_ge(ahead_done, n)
                nc.gpsimd.tensor_tensor(ahead[:], row_no[:], row_no[:], ALU.add).then_inc(ahead_done, 1)

            def gather(e, k, first):
                pool.wait_ge(idx_done, e + 1)
                if not isinstance(e, int) or e >= 2:
                    pool.wait_ge(turned, GROUPS * (e - 1))
                    pool.wait_ge(wk_done, e - 1)
                carry_waits(first)
                for i in range(KT):
                    nc.gpsimd.indirect_dma_start(
                        out=y[:, k, i], out_offset=None, in_=table,
                        in_offset=bass.IndirectOffsetOnAxis(ap=idx[:, k, i:i + 1], axis=0)).then_inc(gathered[i // HK], 16)

            def step(e, k, more):
                if more:
                    gather(e + 1, 1 - k, (KT + 1) * e + 1)
                pool.wait_ge(scattered, 16 * KT * e)
                for i in range(KT):
                    pool.wait_ge(ob_done, KT * e + i + 1)
                    carry_waits((KT + 1) * e + 1 + more + i)
                    nc.gpsimd.indirect_dma_start(
                        out=out_rows, out_offset=bass.IndirectOffsetOnAxis(ap=idx[:, k, i:i + 1], axis=0),
                        in_=ob[:, i], in_offset=None, compute_op=ALU.add).then_inc(scattered, 16)

            pool.wait_ge(consts_in, 16 * 6)
            gather(0, 0, 0)
            each(pool, step)

        @block.scalar
        def _(act):
            def step(e, k, more):
                for g in range(HG):
                    h, f = g // FC, g % FC
                    act.wait_ge(h_done, HG * e + g + 1)
                    act.wait_ge(o_done, KT * e)
                    nc.scalar.activation(hT[:, f, h * WIDE:(h + 1) * WIDE], ps_h[:, g % 3], ACT.Gelu_apprx_tanh,
                                         bias=b1b[:, k, f:f + 1]).then_inc(gelu_done, 1)

            each(act, step)

        @block.tensor
        def _(pe):
            def list_tokens(e):
                pe.wait_ge(onehots_done, ONEHOTS * (e + 1))
                pe.wait_ge(idx_done, e)
                for t in range(TT):
                    mm = nc.tensor.matmul(ps_i[:, 0:2 * KT], at_lo[:, t], number[:, t].rearrange("p v k -> p (v k)"),
                                          start=(t == 0), stop=(t == TT - 1))
                mm.then_inc(listed, 1)

            def turn(e, k):
                for h in range(2):
                    pe.wait_ge(gathered[h], 16 * HK * (e + 1))
                    for c in range(DC):
                        g = h * DC + c
                        pe.wait_ge(yT_done, GROUPS * e + max(g - 1, 0))
                        for i in range(HK):
                            mm = nc.tensor.transpose(ps_y[:, g % 2, i * P:(i + 1) * P],
                                                     y[:, k, h * HK + i, c * P:(c + 1) * P], ident[:])
                        mm.then_inc(turned, 1)

            def step(e, k, more):
                pe.wait_ge(w1_in[k], 32 * (e // 2 + 1) if isinstance(e, int) else (e - k) * 16 + 32)
                for g in range(HG):
                    h, f = g // FC, g % FC
                    if f == 0:
                        pe.wait_ge(yT_done, GROUPS * e + DC * (h + 1))
                    pe.wait_ge(gelu_done, HG * e + max(g - 2, 0))
                    for c in range(DC):
                        mm = nc.tensor.matmul(ps_h[:, g % 3], w1[:, k, c, f * P:(f + 1) * P],
                                              yT[:, c, h * WIDE:(h + 1) * WIDE], start=(c == 0), stop=(c == DC - 1))
                    mm.then_inc(h_done, 1)
                if more:
                    list_tokens(e + 1)
                pe.wait_ge(w2_in[k], 32 * (e // 2 + 1) if isinstance(e, int) else (e - k) * 16 + 32)
                pe.wait_ge(gelu_done, HG * (e + 1))
                for i in range(KT):
                    pe.wait_ge(biased_done, KT * e + max(i - 1, 0))
                    for f in range(FC):
                        mm = nc.tensor.matmul(ps_o[:, i % 2, 0:D], hT[:, f, i * P:(i + 1) * P], w2[:, k, f],
                                              start=(f == 0), stop=(f == FC - 1))
                    mm.then_inc(o_done, 1)
                if more:
                    turn(e + 1, 1 - k)

            pe.wait_ge(consts_in, 16 * 6)
            list_tokens(0)
            turn(0, 0)
            each(pe, step)


def block_kernel(nc, t, out):
    parts = nc.dram_tensor("qkv_parts", (B * H, 2, PARTS, DH, N), BF16).ap()
    values = nc.dram_tensor("values", (B, PAIRS, P, TILES * 2 * 2 * DH), F32).ap()
    o = nc.dram_tensor("attended", (NP, 2, 4, 2 * DH, N // 4), F32).ap()
    rden = nc.dram_tensor("reciprocal_denominators", (B, P, P), F32).ap()
    table = nc.dram_tensor("token_table", (TOK, ROW), F32).ap()
    with ExitStack() as ctx:
        a = Alloc(nc, ctx)
        gate = a.sb("gate", [P, TOK // P, E])
        places_hi = a.sb("places_hi", [P, E, TOK // P])
        places_lo = a.sb("places_lo", [P, E, TOK // P])
        project(nc, t["x"], t["w_qkv"], t["rot_cos"], t["rot_sin"], t["ident"], parts, values)
        attend(nc, parts, values.rearrange("b r p n -> (b r) p n"), o, t["ident"])
        finish(nc, t["x"], o, rden, t["w_out"], t["b_out"], t["w_gate"], t["ident"], table, out, gate)
        choose(nc, gate, t, places_hi, places_lo)
        experts(nc, table, t, t["fc1"], t["fc2"], t["b1"], t["b2"], t["ln_w"], t["ln_b"], places_hi, places_lo, out)


def constants():
    i = np.arange(P)
    inv_freq = (1.0 / 10000.0 ** (np.arange(0, DH, 2, dtype=np.float32) / DH)).astype(np.float32)
    angle = np.outer(np.arange(N, dtype=np.float32), inv_freq).astype(np.float32)
    cos, sin = np.cos(angle), np.sin(angle)

    def by_tile(v):
        return v.reshape(TILES, P, DH).transpose(1, 0, 2)

    group = i // DH
    return {
        "ident": np.eye(P, dtype=np.float32),
        "rot_cos": by_tile(np.concatenate([cos, cos], -1)),
        "rot_sin": by_tile(np.concatenate([-sin, sin], -1)),
        "same": (group[:, None] == group[None]).astype(np.float32),
        "before": ((group[:, None] == group[None]) & (i[:, None] < i[None])).astype(np.float32),
        "bits": np.broadcast_to(np.array([[v << (2 * (ROUNDS - 1 - r)) for v in range(LEVELS)]
                                          for r in range(ROUNDS)], np.int32), (P, ROUNDS, LEVELS)),
        "iota": np.broadcast_to(i.astype(np.float32), (P, P)),
        "tile_no": np.broadcast_to(np.arange(TOK // P, dtype=np.float32)[None, :, None], (P, TOK // P, K // P)),
        "row_no": i.astype(np.float32)[:, None],
    }


def layout(L0_attn_x, L0_attn_Wq, L0_attn_Wkv, L0_attn_Wout, L0_attn_bout, L0_ffn_gate_w, L0_ffn_ln_w, L0_ffn_ln_b,
           L0_ffn_fc1s, L0_ffn_b1s, L0_ffn_fc2s, L0_ffn_b2s):
    return {
        "x": L0_attn_x,
        "w_qkv": np.concatenate([L0_attn_Wq, L0_attn_Wkv], axis=1),
        "w_out": L0_attn_Wout,
        "b_out": L0_attn_bout,
        "w_gate": L0_ffn_gate_w.T.reshape(DC, P, E).transpose(1, 0, 2),
        "ln_w": L0_ffn_ln_w.reshape(DC, P).T,
        "ln_b": L0_ffn_ln_b.reshape(DC, P).T,
        "fc1": L0_ffn_fc1s.transpose(0, 2, 1),
        "b1": L0_ffn_b1s.reshape(E, FC, P).transpose(0, 2, 1),
        "fc2": L0_ffn_fc2s.transpose(0, 2, 1),
        "b2": L0_ffn_b2s,
    }


def kernel(**inputs):
    import concourse.bacc as bacc
    from concourse.bass_utils import run_bass_kernel_spmd

    nc = bacc.Bacc("TRN2", target_bir_lowering=False, num_devices=1)
    arrays, aps = {}, {}
    for name, value in {**constants(), **layout(**{n: np.asarray(v) for n, v in inputs.items()})}.items():
        value = np.ascontiguousarray(value)
        arrays[f"in_{name}_dram"] = value
        aps[name] = nc.dram_tensor(f"in_{name}_dram", value.shape, mybir.dt.from_np(value.dtype),
                                   kind="ExternalInput").ap()
    out = nc.dram_tensor("out_0_dram", (B, N, D), F32, kind="ExternalOutput").ap()
    block_kernel(nc, aps, out)
    result = run_bass_kernel_spmd(nc, [arrays], core_ids=[0])
    return result.results[0]["out_0_dram"]
```

```python
from contextlib import ExitStack

import numpy as np

import concourse.bass as bass
from concourse import mybir

F32 = mybir.dt.float32
BF16 = mybir.dt.bfloat16
I32 = mybir.dt.int32
U32 = mybir.dt.uint32
F32R = mybir.dt.float32r
ALU = mybir.AluOpType
ACT = mybir.ActivationFunctionType
AX = mybir.AxisListType

P = 128
B, N, D = 8, 1024, 256
H, DH = 16, 16
TILES = N // P
TOK = B * N
DC = D // P
HALF = DH // 2
PAIRS = H // 2
NP = B * PAIRS
PARTS = 3
EPS = 1e-5
E, FF = 8, 1024
K = TOK // E
FC = FF // P
ROW = D + E


class Alloc:

    def __init__(self, nc, ctx):
        self.nc, self.ctx = nc, ctx

    def sb(self, name, shape, dt=F32):
        return self.ctx.enter_context(self.nc.sbuf_tensor(name, shape, dt))

    def ps(self, name, shape, dt=F32):
        return self.ctx.enter_context(self.nc.psum_tensor(name, shape, dt))

    def sem(self, name):
        return self.ctx.enter_context(self.nc.semaphore(name))


def past(count, least=1):
    return not isinstance(count, int) or count >= least


class Flow:

    def __init__(self, step, passes):
        self.step, self.passes = step, passes

    def at(self, it, j, lag):
        turn = it if j >= lag else it - 1
        k = (j - lag) % self.step
        if isinstance(turn, int) and not 0 <= turn < self.passes:
            return None
        return turn, k, turn * self.step + k

    def run(self, eng, body, last_lag):
        for it in range(2):
            for j in range(self.step):
                body(it, j)
        with eng.Fori(2, self.passes) as it:
            for j in range(self.step):
                body(it, j)
        for j in range(last_lag):
            body(self.passes, j)


def project(nc, x, w_qkv, rot_cos, rot_sin, ident_d, parts_dram, v_dram):
    SEQS = 2
    STEP = SEQS * TILES
    PASSES = B // SEQS
    GROUP = 4
    GROUPS = STEP // GROUP
    NORM, PROJ, TURN, SUM, BACK, CUT, LAST = 6, 7, 8, 9, 10, 11, 12
    FIRST = P
    with ExitStack() as ctx:
        a = Alloc(nc, ctx)
        ident = a.sb("p_ident", [P, P])
        w = a.sb("p_w", [P, DC, 2 * D])
        cosb = a.sb("p_cos", [P, TILES, DH])
        sinb = a.sb("p_sin", [P, TILES, DH])
        xb = a.sb("p_x", [P, STEP, D])
        stats = a.sb("p_stats", [P, STEP, 6])
        mv = a.sb("p_mv", [P, STEP, 2])
        veps = a.sb("p_veps", [P, STEP])
        rstd = a.sb("p_rstd", [P, STEP])
        mhalf = a.sb("p_mhalf", [P, GROUP])
        epsb = a.sb("p_epsb", [P, GROUP])
        ahead = a.sb("p_ahead", [P, 1])
        xn = a.sb("p_xn", [P, 2, D])
        xnT = a.sb("p_xnT", [P, 2, DC, P])
        qkv = a.sb("p_qkv", [P, 2, 2 * D])
        t_cos = a.sb("p_tcos", [P, 2, 2 * D])
        t_sin = a.sb("p_tsin", [P, 2, 2 * D])
        rot = a.sb("p_rot", [P, 2, 2 * D])
        values = a.sb("p_values", [P, SEQS, PAIRS, TILES, 2, DH])
        parts = a.sb("p_parts", [P, SEQS, 4, PARTS, N], BF16)
        rest = a.sb("p_rest", [P, 2, 4, P])
        ps_xT = a.ps("p_ps_xT", [P, 2, 4, P])
        ps_q = a.ps("p_ps_q", [P, 2, 4 * P])
        ps_rT = a.ps("p_ps_rT", [P, 2, 4, P])

        consts_in = a.sem("p_consts_in")
        x_in = [a.sem(f"p_x_in{g}") for g in range(GROUPS)]
        parts_out = [a.sem(f"p_parts_out{s}") for s in range(SEQS)]
        v_out = [a.sem(f"p_v_out{s}") for s in range(SEQS)]
        halves_set = a.sem("p_halves_set")
        stats_done = a.sem("p_stats_done")
        mv_done = a.sem("p_mv_done")
        veps_done = a.sem("p_veps_done")
        rstd_done = a.sem("p_rstd_done")
        xn_done = a.sem("p_xn_done")
        xT_done = a.sem("p_xT_done")
        xnT_done = a.sem("p_xnT_done")
        q_done = a.sem("p_q_done")
        qkv_done = a.sem("p_qkv_done")
        cos_done = a.sem("p_cos_done")
        sin_done = a.sem("p_sin_done")
        rot_done = a.sem("p_rot_done")
        rot_first_done = a.sem("p_rot_first_done")
        values_done = a.sem("p_values_done")
        rT_done = a.sem("p_rT_done")
        part1_done = a.sem("p_part1_done")
        rest_done = a.sem("p_rest_done")
        part2_done = a.sem("p_part2_done")
        part3_done = a.sem("p_part3_done")
        block = ctx.enter_context(nc.Block())

        x_v = x.rearrange("b (g i p) d -> (b g) p i d", p=P, i=GROUP)
        flow = Flow(STEP, PASSES)

        @block.sync
        def _(sp):
            def load(it, g):
                if past(it):
                    sp.wait_ge(xn_done, it * STEP + ((g + 1) * GROUP - STEP))
                sp.dma_start(xb[:, g * GROUP:(g + 1) * GROUP],
                             x_v[bass.ds(it * GROUPS + g, 1)].rearrange("o p i d -> p (o i) d")).then_inc(x_in[g], 16)

            def store(it, s):
                done = it * STEP + (s + 1) * TILES
                sp.wait_ge(part1_done, done)
                sp.wait_ge(part2_done, done)
                sp.wait_ge(part3_done, done)
                for c in range(4):
                    kind, chunk = c // 2, c % 2
                    for part in range(PARTS):
                        sp.dma_start(
                            parts_dram[bass.ds((it * SEQS + s) * H + chunk * 8, 8), kind, part],
                            parts[:, s, c, part]).then_inc(parts_out[s], 16)
                sp.wait_ge(values_done, done)
                sp.dma_start(v_dram[bass.ds(it * SEQS + s, 1)].rearrange("o r p n -> p (o r) n"),
                             values[:, s].rearrange("p r i h e -> p r (i h e)")).then_inc(v_out[s], 16)

            def body(it):
                load(it + 1, 0)
                if past(it):
                    store(it - 1, 1)
                load(it + 1, 1)
                load(it + 1, 2)
                store(it, 0)
                load(it + 1, 3)

            load(0, 0)
            sp.dma_start(w[:], w_qkv.rearrange("(c p) n -> p c n", p=P)).then_inc(consts_in, 16)
            sp.dma_start(ident[:], ident_d).then_inc(consts_in, 16)
            sp.dma_start(cosb[:], rot_cos).then_inc(consts_in, 16)
            sp.dma_start(sinb[:], rot_sin).then_inc(consts_in, 16)
            for g in range(1, GROUPS):
                load(0, g)
            body(0)
            with sp.Fori(1, PASSES - 1) as it:
                body(it)
            store(PASSES - 2, 1)
            for s in range(SEQS):
                store(PASSES - 1, s)
            for s in range(SEQS):
                sp.wait_ge(parts_out[s], 16 * 4 * PARTS * PASSES)
                sp.wait_ge(v_out[s], 16 * PASSES)

        @block.vector
        def _(dve):
            def statistics(it, k, n):
                g = k // GROUP
                if k % GROUP == 0:
                    dve.wait_ge(x_in[g], 16 * (it + 1))
                nc.vector.bn_stats(stats[:, k], xb[:, k]).then_inc(stats_done, 1)
                if k % GROUP == GROUP - 1:
                    dve.wait_ge(stats_done, (GROUP + 1) * GROUPS * it + (GROUP + 1) * (g + 1) - 1)
                    nc.vector.memset(ahead[:], 0.0).then_inc(stats_done, 1)
                    for t in range(g * GROUP, (g + 1) * GROUP):
                        nc.vector.bn_aggr(mv[:, t], stats[:, t]).then_inc(mv_done, 1)

            def normalise(it, k, n):
                dve.wait_ge(rstd_done, it * GROUPS + (k // GROUP + 1))
                if past(n, 2):
                    dve.wait_ge(xT_done, n - 1)
                nc.vector.tensor_scalar(xn[:, k % 2], xb[:, k], mv[:, k, 0:1], rstd[:, k:k + 1],
                                        ALU.subtract, ALU.mult).then_inc(xn_done, 1)

            def cos_product(it, k, n):
                i = k % TILES
                dve.wait_ge(qkv_done, n + 1)
                if past(n, 2):
                    dve.wait_ge(rot_done, n - 1)
                    dve.wait_ge(rot_first_done, n - 1)
                nc.vector.tensor_tensor(t_cos[:, k % 2].rearrange("p (h d) -> p h d", d=DH),
                                        qkv[:, k % 2].rearrange("p (h d) -> p h d", d=DH),
                                        cosb[:, i:i + 1, :].to_broadcast([P, 2 * H, DH]),
                                        ALU.mult).then_inc(cos_done, 1)

            def first_sum(it, k, n):
                dve.wait_ge(sin_done, n * 2 + 2)
                dve.wait_ge(cos_done, n + 1)
                if past(n, 2):
                    dve.wait_ge(rT_done, n - 1)
                nc.vector.tensor_tensor(rot[:, k % 2, 0:FIRST], t_cos[:, k % 2, 0:FIRST], t_sin[:, k % 2, 0:FIRST],
                                        ALU.add).then_inc(rot_first_done, 1)

            def rest_of(it, k, n):
                s, i = k // TILES, k % TILES
                dve.wait_ge(part1_done, n + 1)
                if past(n, 2):
                    dve.wait_ge(part3_done, n - 1)
                nc.vector.tensor_tensor(rest[:, k % 2], ps_rT[:, k % 2], parts[:, s, :, 0, i * P:(i + 1) * P],
                                        ALU.subtract).then_inc(rest_done, 1)

            def third_part(it, k, n):
                s, i = k // TILES, k % TILES
                cols = slice(i * P, (i + 1) * P)
                dve.wait_ge(part2_done, n + 1)
                nc.vector.tensor_tensor(parts[:, s, :, 2, cols], rest[:, k % 2], parts[:, s, :, 1, cols],
                                        ALU.subtract).then_inc(part3_done, 1)

            def body(it, j):
                for stage, lag in ((statistics, 0), (normalise, NORM), (cos_product, TURN), (rest_of, CUT),
                                   (third_part, LAST), (first_sum, SUM)):
                    tile = flow.at(it, j, lag)
                    if tile:
                        stage(*tile)

            nc.vector.memset(mhalf[:], -0.5).then_inc(halves_set, 1)
            nc.vector.memset(epsb[:], EPS).then_inc(halves_set, 1)
            dve.wait_ge(consts_in, 64)
            flow.run(dve, body, LAST)

        @block.gpsimd
        def _(pool):
            def inverse_root(it, k, n):
                g = k // GROUP
                cols = slice(g * GROUP, (g + 1) * GROUP)
                pool.wait_ge(mv_done, n + 1)
                nc.gpsimd.tensor_tensor(veps[:, cols], mv[:, cols, 1], epsb[:], ALU.add).then_inc(veps_done, 1)
                pool.wait_ge(veps_done, it * GROUPS + (g + 1))
                nc.gpsimd.tensor_tensor(rstd[:, cols], veps[:, cols], mhalf[:], ALU.pow).then_inc(rstd_done, 1)

            def turn(it, k, n):
                i = k % TILES
                src = qkv[:, k % 2].rearrange("p (h d) -> p h d", d=DH)
                ts = t_sin[:, k % 2].rearrange("p (h d) -> p h d", d=DH)
                pool.wait_ge(qkv_done, n + 1)
                if past(n, 2):
                    pool.wait_ge(rot_done, n - 1)
                    pool.wait_ge(rot_first_done, n - 1)
                for h in range(2):
                    nc.gpsimd.tensor_tensor(
                        ts[:, :, h * HALF:(h + 1) * HALF], src[:, :, (1 - h) * HALF:(2 - h) * HALF],
                        sinb[:, i:i + 1, h * HALF:(h + 1) * HALF].to_broadcast([P, 2 * H, HALF]),
                        ALU.mult).then_inc(sin_done, 1)
                pool.wait_ge(cos_done, n + 1)
                pool.wait_ge(sin_done, n * 2 + 2)
                if past(n, 2):
                    pool.wait_ge(rT_done, n - 1)
                    pool.wait_ge(values_done, n - 1)
                nc.gpsimd.tensor_tensor(rot[:, k % 2, FIRST:], t_cos[:, k % 2, FIRST:], t_sin[:, k % 2, FIRST:], ALU.add
                                        ).then_inc(rot_done, 1)

            def body(it, j):
                tile = flow.at(it, j, 0)
                if tile and j % GROUP == GROUP - 1:
                    inverse_root(*tile)
                tile = flow.at(it, j, TURN)
                if tile:
                    turn(*tile)

            pool.wait_ge(consts_in, 64)
            pool.wait_ge(halves_set, 2)
            flow.run(pool, body, TURN)

        @block.scalar
        def _(act):
            def turned_tokens(it, k, n):
                act.wait_ge(xT_done, n + 1)
                if past(n, 2):
                    act.wait_ge(q_done, n - 1)
                nc.scalar.copy(xnT[:, k % 2], ps_xT[:, k % 2, 0:DC]).then_inc(xnT_done, 1)

            def projected(it, k, n):
                act.wait_ge(q_done, n + 1)
                if past(n, 2):
                    act.wait_ge(rot_done, n - 1)
                nc.scalar.copy(qkv[:, k % 2], ps_q[:, k % 2]).then_inc(qkv_done, 1)

            def first_part(it, k, n):
                s, i = k // TILES, k % TILES
                if i == 0 and past(it):
                    act.wait_ge(parts_out[s], 16 * 4 * PARTS * it)
                    act.wait_ge(v_out[s], 16 * it)
                act.wait_ge(rT_done, n + 1)
                nc.scalar.copy(parts[:, s, :, 0, i * P:(i + 1) * P], ps_rT[:, k % 2]).then_inc(part1_done, 1)
                nc.scalar.copy(values[:, s, :, i],
                               rot[:, k % 2, D:2 * D].rearrange("p (r h d) -> p r h d", h=2, d=DH)
                               ).then_inc(values_done, 1)

            def second_part(it, k, n):
                s, i = k // TILES, k % TILES
                act.wait_ge(rest_done, n + 1)
                nc.scalar.copy(parts[:, s, :, 1, i * P:(i + 1) * P], rest[:, k % 2]).then_inc(part2_done, 1)

            def body(it, j):
                for stage, lag in ((turned_tokens, NORM), (projected, PROJ), (first_part, BACK), (second_part, CUT)):
                    tile = flow.at(it, j, lag)
                    if tile:
                        stage(*tile)

            flow.run(act, body, CUT)

        @block.tensor
        def _(pe):
            def turn_tokens(it, k, n):
                pe.wait_ge(xn_done, n + 1)
                if past(n, 2):
                    pe.wait_ge(xnT_done, n - 1)
                for c in range(DC):
                    mm = nc.tensor.transpose(ps_xT[:, k % 2, c], xn[:, k % 2, c * P:(c + 1) * P], ident[:])
                mm.then_inc(xT_done, 1)

            def products(it, k, n):
                pe.wait_ge(xnT_done, n + 1)
                if past(n, 2):
                    pe.wait_ge(qkv_done, n - 1)
                for c in range(DC):
                    mm = nc.tensor.matmul(ps_q[:, k % 2], xnT[:, k % 2, c], w[:, c], start=(c == 0), stop=(c == DC - 1))
                mm.then_inc(q_done, 1)

            def turn_back(it, k, n):
                pe.wait_ge(rot_done, n + 1)
                pe.wait_ge(rot_first_done, n + 1)
                if past(n, 2):
                    pe.wait_ge(rest_done, n - 1)
                for c in range(4):
                    mm = nc.tensor.transpose(ps_rT[:, k % 2, c], rot[:, k % 2, c * P:(c + 1) * P], ident[:])
                mm.then_inc(rT_done, 1)

            def body(it, j):
                for stage, lag in ((turn_tokens, NORM), (products, PROJ), (turn_back, BACK)):
                    tile = flow.at(it, j, lag)
                    if tile:
                        stage(*tile)

            pe.wait_ge(consts_in, 64)
            flow.run(pe, body, BACK)


SLOTS = ((0, 0), (1, 1), (0, 1), (1, 0), (2, 0), (0, 2))
SLOT_ROW = ([0, 16, 32, 48, 64, 80], [64, 80, 96, 112, 0, 16])
MAX_ROW = (96, 32)
MAX_PARTS = 2


def slot_runs(h, kind):
    runs = []
    for row, of in zip(SLOT_ROW[h], SLOTS):
        part = of[kind]
        if runs and runs[-1][0] + runs[-1][2] * DH == row and runs[-1][1] + runs[-1][2] == part:
            runs[-1][2] += 1
        else:
            runs.append([row, part, 1])
    return runs


CHUNK = 512
HALVES = N // CHUNK


def attend(nc, parts_dram, v_dram, o_dram, ident_d):
    NG = 2 * TILES
    TURN_AT = 12
    with ExitStack() as ctx:
        a = Alloc(nc, ctx)
        identb = a.sb("a_identb", [P, P], BF16)
        identf = a.sb("a_identf", [P, P])
        qb = a.sb("a_q", [P, 3, 2, N], BF16)
        kb = a.sb("a_k", [P, 3, 2, N], BF16)
        v_raw = a.sb("a_v_raw", [P, 3, TILES, 2, DH])
        vb = a.sb("a_v", [P, 3, TILES, 2, 2 * DH])
        prob = a.sb("a_prob", [P, 4, N])
        mx = a.sb("a_mx", [P, TILES, 2, 2])
        nm = a.sb("a_nm", [P, TILES, 2])
        nsplit = a.sb("a_nsplit", [P, 2, MAX_PARTS, TILES], BF16)
        zero = a.sb("a_zero", [P, TILES, 2])
        mrow = a.sb("a_mrow", [2 * MAX_PARTS * TILES, P], BF16)
        oraw = a.sb("a_oraw", [P, CHUNK])
        sm = a.ps("a_sm", [P, 2, 2, CHUNK])
        st = a.ps("a_st", [P, 3, CHUNK])
        pv = a.ps("a_pv", [P, CHUNK])

        set_up = a.sem("a_set_up")
        ident_in = a.sem("a_ident_in")
        identb_set = a.sem("a_identb_set")
        qk_in = [a.sem(f"a_qk_in{i}") for i in range(3)]
        v_in = [a.sem(f"a_v_in{i}") for i in range(3)]
        v_placed = a.sem("a_v_placed")
        m_in = a.sem("a_m_in")
        o_out = a.sem("a_o_out")
        sm_done = a.sem("a_sm_done")
        max_done = a.sem("a_max_done")
        nm_done = a.sem("a_nm_done")
        n1_done = a.sem("a_n1_done")
        n2_done = a.sem("a_n2_done")
        mT_done = a.sem("a_mT_done")
        mrow_done = a.sem("a_mrow_done")
        st_done = a.sem("a_st_done")
        exp_done = a.sem("a_exp_done")
        pv_done = a.sem("a_pv_done")
        evac_done = a.sem("a_evac_done")
        block = ctx.enter_context(nc.Block())
        QK_LOADS = sum(len(slot_runs(h, kind)) for h in range(2) for kind in range(2))
        UNITS = 2 * NG
        AHEAD = NG + NG // 2
        turned = sm[0:2 * MAX_PARTS * TILES, 0, 0, 0:P // 2].bitcast(BF16)

        class Pair:

            def __init__(self, k, c, p=None):
                self.k, self.c, self.p = k, c, p
                self.n = k * 3 + c
                self.buf = c % 3
                self.turn = k + c // 3

            def plus(self, d):
                return Pair(self.k, self.c + d, None if self.p is None else self.p + d)

            def exists(self):
                return self.p is None or self.p < NP

            def first(self):
                return self.p == 0

        def pairs(eng, body):
            body(Pair(0, 0, 0))
            with eng.Fori(0, (NP - 4) // 3) as k:
                for c in range(1, 4):
                    body(Pair(k, c))
            for p in range(NP - 3, NP):
                body(Pair(0, p, p))

        @block.sync
        def _(sp):
            def load(q):
                if not (q.p is not None and q.p < 3):
                    sp.wait_ge(st_done, (q.n - 2) * UNITS)
                for h in range(2):
                    for kind, buf in ((0, qb), (1, kb)):
                        for row, part, parts in slot_runs(h, kind):
                            sp.dma_start(buf[row:row + parts * DH, q.buf, h, :],
                                         parts_dram[bass.ds(q.n * 2 + h, 1), kind, part:part + parts]
                                         .rearrange("o s d n -> (o s d) n")).then_inc(qk_in[q.buf], 16)
                if not (q.p is not None and q.p < 3):
                    sp.wait_ge(v_placed, q.n - 2)
                sp.dma_start(v_raw[:, q.buf].rearrange("p i h e -> p (i h e)"),
                             v_dram[bass.ds(q.n, 1)].rearrange("o p n -> (o p) n")).then_inc(v_in[q.buf], 16)

            def store(q):
                sp.wait_ge(evac_done, q.n + 1)
                sp.dma_start(o_dram[bass.ds(q.n, 1)].rearrange("o h c r n -> (o h c r) n"), oraw[:]).then_inc(o_out, 16)

            def max_rows(q):
                sp.wait_ge(mrow_done, q.n + 1)
                rows = MAX_PARTS * TILES
                for h in range(2):
                    sp.dma_start(qb[MAX_ROW[h]:MAX_ROW[h] + MAX_PARTS, q.buf, h, :].rearrange("r (t c) -> r t c", c=P),
                                 mrow[h * rows:(h + 1) * rows, :]).then_inc(m_in, 16)

            def body(q):
                if not q.first() and q.plus(2).exists():
                    load(q.plus(2))
                if not q.first():
                    store(q.plus(-1))
                if q.plus(1).exists():
                    max_rows(q.plus(1))

            sp.dma_start(identf[:], ident_d).then_inc(ident_in, 16)
            for p in range(3):
                load(Pair(0, p, p))
            sp.wait_ge(set_up, 8)
            max_rows(Pair(0, 0, 0))
            pairs(sp, body)
            store(Pair(0, NP - 1, NP - 1))
            sp.wait_ge(o_out, 16 * NP)

        @block.tensor
        def _(pe):
            def scores(q, g, ic):
                jt, h = g // 2, g % 2
                u = g * 2 + ic
                slot = (q.c * UNITS + u) % 3
                if g == 0 and ic == 0:
                    pe.wait_ge(m_in, (q.n + 1) * 32)
                if not (q.first() and u < 3):
                    pe.wait_ge(exp_done, q.n * UNITS + (u - 2))
                nc.tensor.matmul(st[:, slot], kb[:, q.buf, h, jt * P:(jt + 1) * P],
                                 qb[:, q.buf, h, ic * CHUNK:(ic + 1) * CHUNK],
                                 start=True, stop=True).then_inc(st_done, 1)

            def values(q, jt):
                if jt == 0:
                    pe.wait_ge(v_placed, q.n + 1)
                    if not q.first():
                        pe.wait_ge(evac_done, q.n)
                pe.wait_ge(exp_done, q.n * UNITS + 4 * jt + 4)
                for h in range(2):
                    for ic in range(HALVES):
                        row = 2 * DH * (h * HALVES + ic)
                        mm = nc.tensor.matmul(pv[row:row + 2 * DH, :], vb[:, q.buf, jt, h, :],
                                              prob[:, (2 * jt + h) % 4, ic * CHUNK:(ic + 1) * CHUNK],
                                              start=(jt == 0), stop=(jt == TILES - 1))
                mm.then_inc(pv_done, 1)

            def maxima(q, v, slot):
                qt, kc = v // 2, v % 2
                if v == 0:
                    pe.wait_ge(qk_in[q.buf], (q.turn + 1) * 16 * QK_LOADS)
                for h in range(2):
                    rows = slice(64 * h, 64 * h + 64)
                    mm = nc.tensor.matmul(sm[:, slot, h], qb[rows, q.buf, h, qt * P:(qt + 1) * P],
                                          kb[rows, q.buf, h, kc * CHUNK:(kc + 1) * CHUNK], start=True, stop=True)
                mm.then_inc(sm_done, 1)

            def turn_maxima(q):
                pe.wait_ge(n2_done, q.n + 1)
                nc.tensor.transpose(turned, nsplit[:].rearrange("p h s t -> p (h s t)"), identb[:]).then_inc(mT_done, 1)

            def body(q):
                seen = q.n * NG + AHEAD

                def unit(g):
                    ahead = q.plus(1) if g < NG // 2 else q.plus(2)
                    if ahead.exists():
                        pe.wait_ge(max_done, seen + g - 1)
                        if g == TURN_AT:
                            pe.wait_ge(mrow_done, q.n + 2)
                        maxima(ahead, (g + NG // 2) % NG, g % 2)

                for g in range(NG):
                    scores(q, g, 0)
                    if g == TURN_AT + 1:
                        unit(TURN_AT)
                    if g % 2 == 1 and g >= 3:
                        values(q, (g - 3) // 2)
                    elif g == 1 and not q.first():
                        values(q.plus(-1), TILES - 1)
                    if g == TURN_AT and q.plus(1).exists():
                        if q.plus(2).exists():
                            pe.wait_ge(max_done, seen + g - 1)
                        turn_maxima(q.plus(1))
                    scores(q, g, 1)
                    if g != TURN_AT:
                        unit(g)

            q0, q1 = Pair(0, 0, 0), Pair(0, 1, 1)
            for v in range(NG):
                if v >= 2:
                    pe.wait_ge(max_done, v - 1)
                maxima(q0, v, v % 2)
            pe.wait_ge(identb_set, 1)
            turn_maxima(q0)
            for v in range(NG // 2):
                pe.wait_ge(max_done, NG + v - 1)
                if v == 0:
                    pe.wait_ge(mrow_done, 1)
                maxima(q1, v, v % 2)
            pe.wait_ge(set_up, 8)
            pairs(pe, body)
            values(Pair(0, NP - 1, NP - 1), TILES - 1)

        @block.vector
        def _(dve):
            def reduce(q, v, s, slot):
                qt, kc = v // 2, v % 2
                if v == 0 and not q.first():
                    dve.wait_ge(nm_done, q.n)
                dve.wait_ge(sm_done, s + 1)
                nc.vector.tensor_reduce(mx[:, qt, kc, :], sm[:, slot], AX.X, ALU.max,
                                        negate=True).then_inc(max_done, 1)
                if v == NG - 1:
                    if not q.first():
                        dve.wait_ge(n2_done, q.n)
                    dve.wait_ge(max_done, (q.n + 1) * NG)
                    nc.vector.tensor_tensor(nm[:], mx[:, :, 0], mx[:, :, 1], ALU.min).then_inc(nm_done, 1)

            def body(q):
                for g in range(NG):
                    ahead = q.plus(1) if g < NG // 2 else q.plus(2)
                    if ahead.exists():
                        reduce(ahead, (g + NG // 2) % NG, q.n * NG + AHEAD + g, g % 2)

            dve.wait_ge(ident_in, 16)
            nc.vector.tensor_copy(identb[:], identf[:]).then_inc(identb_set, 1)
            for v in range(NG):
                reduce(Pair(0, 0, 0), v, v, v % 2)
            for v in range(NG // 2):
                reduce(Pair(0, 1, 1), v, NG + v, v % 2)
            pairs(dve, body)

        @block.gpsimd
        def _(pool):
            def split(q):
                part = [nsplit[:, :, s, :].rearrange("p h t -> p t h") for s in range(MAX_PARTS)]
                pool.wait_ge(nm_done, q.n + 1)
                if not q.first():
                    pool.wait_ge(mT_done, q.n)
                nc.gpsimd.tensor_tensor(part[0], nm[:], zero[:], ALU.add).then_inc(n1_done, 1)
                pool.wait_ge(n1_done, q.n + 1)
                nc.gpsimd.tensor_tensor(part[1], nm[:], part[0], ALU.subtract).then_inc(n2_done, 1)

            def place(q):
                pool.wait_ge(v_in[q.buf], (q.turn + 1) * 16)
                if not (q.p is not None and q.p < 3):
                    pool.wait_ge(pv_done, (q.n - 2) * TILES)
                nc.gpsimd.tensor_tensor(vb[:, q.buf, :, :, 0:DH], v_raw[:, q.buf],
                                        zero[:].unsqueeze(3).to_broadcast([P, TILES, 2, DH]), ALU.add
                                        ).then_inc(v_placed, 1)

            def body(q):
                split(q)
                if not q.first() and q.plus(2).exists():
                    place(q.plus(2))

            nc.gpsimd.memset(zero[:], 0.0).then_inc(set_up, 1)
            nc.gpsimd.memset(vb[:], 1.0).then_inc(set_up, 1)
            pool.wait_ge(set_up, 2)
            for p in range(3):
                place(Pair(0, p, p))
            pairs(pool, body)

        @block.scalar
        def _(act):
            def exp(q, g, ic):
                u = g * 2 + ic
                act.wait_ge(st_done, q.n * UNITS + u + 1)
                if ic == 0 and not (q.first() and g < 4):
                    act.wait_ge(pv_done, q.n * TILES + (g // 2 - 1))
                nc.scalar.activation(prob[:, g % 4, ic * CHUNK:(ic + 1) * CHUNK], st[:, (q.c * UNITS + u) % 3],
                                     ACT.Exp, scale=DH ** -0.5).then_inc(exp_done, 1)

            def evacuate(q):
                act.wait_ge(pv_done, (q.n + 1) * TILES)
                if not q.first():
                    act.wait_ge(o_out, q.n * 16)
                nc.scalar.copy(oraw[:], pv[:]).then_inc(evac_done, 1)

            def copy_max_rows(q):
                act.wait_ge(mT_done, q.n + 1)
                if not q.first():
                    act.wait_ge(m_in, q.n * 32)
                nc.scalar.copy(mrow[:], turned).then_inc(mrow_done, 1)

            def body(q):
                for g in range(NG):
                    if g == 2 and not q.first():
                        evacuate(q.plus(-1))
                    if g == TURN_AT and q.plus(1).exists():
                        copy_max_rows(q.plus(1))
                    exp(q, g, 0)
                    exp(q, g, 1)

            act.wait_ge(set_up, 2)
            for buf in (kb, qb):
                for h in range(2):
                    rows = slice(MAX_ROW[h], MAX_ROW[h] + 32)
                    nc.scalar.copy(buf[rows, :, h], zero[rows, 0:1, 0:1].to_broadcast([32, 3, N])).then_inc(set_up, 1)
            act.wait_ge(set_up, 6)
            for h in range(2):
                rows = slice(MAX_ROW[h], MAX_ROW[h] + MAX_PARTS)
                nc.scalar.copy(kb[rows, :, h], vb[rows, 0, 0, 0:1, DH:DH + 1].to_broadcast([MAX_PARTS, 3, N])
                               ).then_inc(set_up, 1)
            copy_max_rows(Pair(0, 0, 0))
            pairs(act, body)
            evacuate(Pair(0, NP - 1, NP - 1))


def finish(nc, x, o_dram, rden_dram, w_out, b_out, w_gate, ident_d, table, out, gate):
    SEQS = 2
    STEP = SEQS * TILES
    PASSES = B // SEQS
    GROUP = 2
    PROJ, STAT, NORM, TURN, LOGITS, SHIFT, NORM2, BACK, CENTRE, SHARE = 3, 4, 7, 8, 9, 10, 11, 11, 12, 13
    LGROUP = 4
    with ExitStack() as ctx:
        a = Alloc(nc, ctx)
        ident = a.sb("f_ident", [P, P])
        w = a.sb("f_w", [P, DC, D])
        wg = a.sb("f_wg", [P, DC, E])
        bo = a.sb("f_bo", [PARTS, D])
        bo_rest = a.sb("f_bo_rest", [PARTS, D])
        bo_part = a.sb("f_bo_part", [PARTS, PARTS, D], BF16)
        bo_rows = a.sb("f_bo_rows", [PARTS, D], BF16)
        ones = a.sb("f_ones", [PARTS, P], BF16)
        mhalf = a.sb("f_mhalf", [P, GROUP])
        epsb = a.sb("f_epsb", [P, GROUP])
        ahead = a.sb("f_ahead", [P, 1])
        den = a.sb("f_den", [P, B, P])
        rden = a.sb("f_rden", [P, B, P])
        num = a.sb("f_num", [P, SEQS, DC, N])
        rrep = a.sb("f_rrep", [P, SEQS, DC, N])
        o = a.sb("f_o", [P, SEQS, DC, N])
        xb = a.sb("f_x", [P, STEP, D])
        x2 = a.sb("f_x2", [P, STEP, D])
        xf = a.sb("f_xf", [P, STEP, D])
        tab = a.sb("f_tab", [P, STEP, ROW])
        stats = a.sb("f_stats", [P, 2, STEP, 6])
        mv = a.sb("f_mv", [P, 2, STEP, 2])
        veps = a.sb("f_veps", [P, 2, STEP])
        rstd = a.sb("f_rstd", [P, 2, STEP])
        shift = a.sb("f_shift", [P, STEP])
        xfT = a.sb("f_xfT", [P, 2, DC, P])
        lT = a.sb("f_lT", [E, 2, LGROUP * P])
        lmax = a.sb("f_lmax", [P, TILES])
        lcen = a.sb("f_lcen", [P, TILES, E])
        lexp = a.sb("f_lexp", [P, TILES, E])
        lsum = a.sb("f_lsum", [P, TILES])
        lrec = a.sb("f_lrec", [P, TILES])
        ps_y = a.ps("f_ps_y", [P, 2, 512])
        ps_xT = a.ps("f_ps_xT", [P, 2, 4, P])
        ps_lT = a.ps("f_ps_lT", [P, 2, LGROUP * P])
        ps_l = a.ps("f_ps_l", [P, 2, 512])

        consts_in = a.sem("f_consts_in")
        set_up = a.sem("f_set_up")
        den_in = [a.sem("f_den_in_first"), a.sem("f_den_in_others")]
        rden_out = [a.sem(f"f_rden_out_{name}") for name in ("first", "second", "others")]
        num_in = [a.sem(f"f_num_in{s}") for s in range(SEQS)]
        x_in = [a.sem(f"f_x_in{s}") for s in range(SEQS)]
        out_out = [a.sem(f"f_out_out{s}") for s in range(SEQS)]
        tab_out = [a.sem(f"f_tab_out{s}") for s in range(SEQS)]
        bias_done = a.sem("f_bias_done")
        rden_done = a.sem("f_rden_done")
        o_done = a.sem("f_o_done")
        y_done = a.sem("f_y_done")
        x2_done = a.sem("f_x2_done")
        stats_done = [a.sem(f"f_stats_done{v}") for v in range(2)]
        mv_done = [a.sem(f"f_mv_done{v}") for v in range(2)]
        veps_done = [a.sem(f"f_veps_done{v}") for v in range(2)]
        rstd_done = [a.sem(f"f_rstd_done{v}") for v in range(2)]
        xf_done = a.sem("f_xf_done")
        xT_done = a.sem("f_xT_done")
        xfT_done = a.sem("f_xfT_done")
        logits_done = a.sem("f_logits_done")
        lT_done = a.sem("f_lT_done")
        back_done = a.sem("f_back_done")
        shift_done = a.sem("f_shift_done")
        yn_done = a.sem("f_yn_done")
        base_done = a.sem("f_base_done")
        base4_done = a.sem("f_base4_done")
        lmax_done = a.sem("f_lmax_done")
        lcen_done = a.sem("f_lcen_done")
        lexp_done = a.sem("f_lexp_done")
        lsum_done = a.sem("f_lsum_done")
        lrec_done = a.sem("f_lrec_done")
        gate_done = a.sem("f_gate_done")
        scores_done = a.sem("f_scores_done")
        block = ctx.enter_context(nc.Block())

        x_v = x.rearrange("b (i p) d -> b p i d", p=P)
        out_v = out.rearrange("b (i p) d -> b p i d", p=P)
        table_v = table.rearrange("(b i p) e -> b p i e", p=P, i=TILES)
        HC = PAIRS // DC
        NUM_LOADS = DC * HALVES + DC
        flow = Flow(STEP, PASSES)

        def one(v):
            return bass.ds(v, 1)

        def tiles_of(s):
            return slice(s * TILES, (s + 1) * TILES)

        @block.sync
        def _(sp):
            def load_num(it, s):
                b = it * SEQS + s
                if past(it):
                    sp.wait_ge(o_done, 2 * DC * SEQS * it + 2 * DC * (s + 1 - SEQS))
                for ch in range(DC):
                    for c in range(HALVES):
                        sp.dma_start(num[:, s, ch, c * CHUNK:(c + 1) * CHUNK],
                                     o_dram[bass.ds(b * PAIRS + ch * HC, HC), :, c, 0:DH, :]
                                     .rearrange("n h r x -> (n h) r x")).then_inc(num_in[s], 16)

            def load_rrep(it, s):
                b = it * SEQS + s
                for ch in range(DC):
                    sp.dma_start(rrep[:, s, ch],
                                 rden_dram[one(b), ch * 64:(ch + 1) * 64].rearrange("o (k q) n -> (o k) (q n)", q=TILES)
                                 .unsqueeze(1).to_broadcast([2 * HC, DH, N])).then_inc(num_in[s], 16)

            def load_x(it, s):
                if past(it):
                    sp.wait_ge(x2_done, it * STEP + (s + 1 - SEQS) * TILES)
                sp.dma_start(xb[:, tiles_of(s)], x_v[one(it * SEQS + s)].rearrange("o p i d -> p (o i) d")
                             ).then_inc(x_in[s], 16)

            def load_den(b):
                sp.dma_start(den[:, b], o_dram[bass.ds(b * PAIRS, PAIRS), :, :, DH, :]
                             .rearrange("n h c (f x) -> (n h c) f x", x=P)).then_inc(den_in[b > 0], 16)

            def store_rden(b):
                sp.dma_start(rden_dram[b], rden[:, b]).then_inc(rden_out[min(b, 2)], 16)

            def store_out(it, s):
                sp.wait_ge(base4_done, it * (STEP // 4) + (s + 1) * (TILES // 4))
                sp.wait_ge(base_done, it * (STEP - STEP // 4) + (s + 1) * (TILES - TILES // 4))
                sp.dma_start(out_v[one(it * SEQS + s)].rearrange("o p i d -> p (o i) d"), x2[:, tiles_of(s)]
                             ).then_inc(out_out[s], 16)

            def store_tab(it, s):
                done = it * STEP + (s + 1) * TILES
                sp.wait_ge(yn_done, done)
                sp.wait_ge(scores_done, done)
                sp.dma_start(table_v[one(it * SEQS + s)].rearrange("o p i e -> p (o i) e"), tab[:, tiles_of(s)]
                             ).then_inc(tab_out[s], 16)

            def body(it):
                load_num(it + 1, 0)
                load_rrep(it + 1, 0)
                if past(it):
                    store_tab(it - 1, 0)
                    store_out(it - 1, 1)
                load_x(it + 1, 0)
                load_num(it + 1, 1)
                load_rrep(it + 1, 1)
                if past(it):
                    store_tab(it - 1, 1)
                store_out(it, 0)
                load_x(it + 1, 1)

            load_den(0)
            load_num(0, 0)
            sp.wait_ge(rden_done, 1)
            store_rden(0)
            sp.dma_start(bo[:], b_out.rearrange("(o n) -> o n", o=1).to_broadcast([PARTS, D])).then_inc(consts_in, 16)
            sp.dma_start(ident[:], ident_d).then_inc(consts_in, 16)
            sp.dma_start(w[:], w_out.rearrange("(c p) n -> p c n", p=P)).then_inc(consts_in, 16)
            sp.dma_start(wg[:], w_gate).then_inc(consts_in, 16)
            sp.wait_ge(rden_out[0], 16)
            load_rrep(0, 0)
            load_x(0, 0)
            for b in range(1, B):
                load_den(b)
            load_num(0, 1)
            load_x(0, 1)
            sp.wait_ge(rden_done, 2)
            store_rden(1)
            sp.wait_ge(rden_out[1], 16)
            load_rrep(0, 1)
            for b in range(2, B):
                sp.wait_ge(rden_done, b + 1)
                store_rden(b)
            sp.wait_ge(rden_out[2], 16 * (B - 2))
            body(0)
            with sp.Fori(1, PASSES - 1) as it:
                body(it)
            last = PASSES - 1
            store_tab(last - 1, 0)
            store_out(last - 1, 1)
            store_tab(last - 1, 1)
            for s in range(SEQS):
                store_out(last, s)
                store_tab(last, s)
            for s in range(SEQS):
                sp.wait_ge(out_out[s], 16 * PASSES)
                sp.wait_ge(tab_out[s], 16 * PASSES)

        @block.gpsimd
        def _(pool):
            def divide(it, k, n):
                s, half = k // TILES, k % TILES // 2
                cols = slice(half * CHUNK, (half + 1) * CHUNK)
                if half == 0:
                    pool.wait_ge(num_in[s], 16 * NUM_LOADS * (it + 1))
                    if past(n, STEP):
                        pool.wait_ge(y_done, n - TILES)
                for ch in range(DC):
                    nc.gpsimd.tensor_tensor(o[:, s, ch, cols], num[:, s, ch, cols], rrep[:, s, ch, cols], ALU.mult
                                            ).then_inc(o_done, 1)

            def inverse_root(v, it, k, n):
                cols = slice(k + 1 - GROUP, k + 1)
                count = it * (STEP // GROUP) + (k // GROUP + 1)
                pool.wait_ge(mv_done[v], n + 1)
                if v == 1 and past(it):
                    pool.wait_ge(yn_done, n + 1 - STEP)
                nc.gpsimd.tensor_tensor(veps[:, v, cols], mv[:, v, cols, 1], epsb[:], ALU.add).then_inc(veps_done[v], 1)
                pool.wait_ge(veps_done[v], count)
                nc.gpsimd.tensor_tensor(rstd[:, v, cols], veps[:, v, cols], mhalf[:], ALU.pow
                                        ).then_inc(rstd_done[v], 1)

            def base(it, k, n):
                pool.wait_ge(xf_done, n + 1)
                nc.gpsimd.tensor_tensor(x2[:, k], x2[:, k], xf[:, k], ALU.add).then_inc(base_done, 1)

            def body(it, j):
                for v, lag in ((0, STAT), (1, TURN)):
                    tile = flow.at(it, j, lag)
                    if tile and tile[1] % GROUP == GROUP - 1:
                        inverse_root(v, *tile)
                tile = flow.at(it, j, TURN)
                if tile and tile[1] % 4 < 3:
                    base(*tile)
                tile = flow.at(it, j, 0)
                if tile and j % TILES in (0, 2):
                    divide(*tile)

            pool.wait_ge(set_up, 3)
            flow.run(pool, body, TURN)

        @block.vector
        def _(dve):
            def residual(it, k, n):
                s = k // TILES
                if k % TILES == 0:
                    dve.wait_ge(x_in[s], 16 * (it + 1))
                    if past(it):
                        dve.wait_ge(out_out[s], 16 * it)
                dve.wait_ge(y_done, n + 1)
                nc.vector.tensor_tensor(x2[:, k], ps_y[:, k % 2, 0:D], xb[:, k], ALU.add).then_inc(x2_done, 1)

            def statistics(v, buf, made, it, k, n):
                dve.wait_ge(made, n + 1)
                nc.vector.bn_stats(stats[:, v, k], buf[:, k]).then_inc(stats_done[v], 1)
                if k % GROUP == GROUP - 1:
                    groups = it * (STEP // GROUP) * (GROUP + 1)
                    dve.wait_ge(stats_done[v], groups + (k // GROUP + 1) * (GROUP + 1) - 1)
                    nc.vector.memset(ahead[:], 0.0).then_inc(stats_done[v], 1)
                    for t in range(k + 1 - GROUP, k + 1):
                        nc.vector.bn_aggr(mv[:, v, t], stats[:, v, t]).then_inc(mv_done[v], 1)

            def normalise(it, k, n):
                dve.wait_ge(rstd_done[0], it * (STEP // GROUP) + (k // GROUP + 1))
                if past(it):
                    dve.wait_ge(yn_done, n + 1 - STEP)
                nc.vector.tensor_scalar(xf[:, k], x2[:, k], mv[:, 0, k, 0:1], rstd[:, 0, k:k + 1],
                                        ALU.subtract, ALU.mult).then_inc(xf_done, 1)

            def base(it, k, n):
                dve.wait_ge(xf_done, n + 1)
                nc.vector.tensor_tensor(x2[:, k], x2[:, k], xf[:, k], ALU.add).then_inc(base4_done, 1)

            def shift_of(it, k, n):
                cols = slice(k + 1 - GROUP, k + 1)
                dve.wait_ge(rstd_done[1], it * (STEP // GROUP) + (k // GROUP + 1))
                nc.vector.scalar_tensor_tensor(out=shift[:, cols], in0=mv[:, 1, cols, 0], scalar=-1.0,
                                               in1=rstd[:, 1, cols], op0=ALU.mult, op1=ALU.mult).then_inc(shift_done, 1)

            def centre(it, k, n):
                s = k // TILES
                count = it * SEQS + (s + 1)
                lg = ps_l[:, s, 0:TILES * E].rearrange("p (i e) -> p i e", e=E)
                dve.wait_ge(back_done, it * (STEP // LGROUP) + (k + 1) // LGROUP)
                nc.vector.tensor_reduce(lmax[:], lg, AX.X, ALU.max).then_inc(lmax_done, 1)
                dve.wait_ge(lmax_done, count)
                nc.vector.tensor_tensor(lcen[:], lg, lmax[:].unsqueeze(2).to_broadcast([P, TILES, E]),
                                        ALU.subtract).then_inc(lcen_done, 1)

            def share(it, k, n):
                s = k // TILES
                count = it * SEQS + (s + 1)
                dve.wait_ge(lexp_done, count)
                nc.vector.tensor_reduce(lsum[:], lexp[:], AX.X, ALU.add).then_inc(lsum_done, 1)
                dve.wait_ge(lsum_done, count)
                nc.vector.reciprocal(lrec[:], lsum[:]).then_inc(lrec_done, 1)
                dve.wait_ge(lrec_done, count)
                nc.vector.tensor_tensor(gate[:, bass.ds(it * STEP + s * TILES, TILES), :], lexp[:],
                                        lrec[:].unsqueeze(2).to_broadcast([P, TILES, E]), ALU.mult).then_inc(gate_done, 1)

            def split_bias():
                dve.wait_ge(consts_in, 64)
                left = bo
                for v in range(PARTS):
                    if v > 0:
                        dve.wait_ge(bias_done, 3 * v)
                    nc.vector.tensor_copy(bo_part[:, v], left[:]).then_inc(bias_done, 1)
                    dve.wait_ge(bias_done, 3 * v + 1)
                    nc.vector.tensor_tensor(bo_rest[:], left[:], bo_part[:, v], ALU.subtract).then_inc(bias_done, 1)
                    if v == 0:
                        nc.vector.tensor_scalar(bo_rows[:], bo_part[:, 0], ident[0:PARTS, 0:1], None, ALU.mult
                                                ).then_inc(bias_done, 1)
                    else:
                        nc.vector.scalar_tensor_tensor(out=bo_rows[:], in0=bo_part[:, v], scalar=ident[0:PARTS, v:v + 1],
                                                       in1=bo_rows[:], op0=ALU.mult, op1=ALU.add).then_inc(bias_done, 1)
                    left = bo_rest

            def body(it, j):
                if isinstance(it, int) and it == 0 and 1 <= j < B:
                    dve.wait_ge(den_in[1], 16 * (B - 1))
                    nc.vector.reciprocal(rden[:, j], den[:, j]).then_inc(rden_done, 1)
                tile = flow.at(it, j, PROJ)
                if tile:
                    residual(*tile)
                tile = flow.at(it, j, STAT)
                if tile:
                    statistics(0, x2, x2_done, *tile)
                tile = flow.at(it, j, NORM)
                if tile:
                    normalise(*tile)
                tile = flow.at(it, j, TURN)
                if tile:
                    statistics(1, xf, xf_done, *tile)
                    if tile[1] % 4 == 3:
                        base(*tile)
                tile = flow.at(it, j, CENTRE)
                if tile and tile[1] % TILES == TILES - 1:
                    centre(*tile)
                tile = flow.at(it, j, SHIFT)
                if tile and tile[1] % GROUP == GROUP - 1:
                    shift_of(*tile)
                tile = flow.at(it, j, SHARE)
                if tile and tile[1] % TILES == TILES - 1:
                    share(*tile)

            nc.vector.memset(mhalf[:], -0.5).then_inc(set_up, 1)
            nc.vector.memset(epsb[:], EPS).then_inc(set_up, 1)
            nc.vector.memset(ones[:], 1.0).then_inc(set_up, 1)
            dve.wait_ge(den_in[0], 16)
            nc.vector.reciprocal(rden[:, 0], den[:, 0]).then_inc(rden_done, 1)
            split_bias()
            flow.run(dve, body, SHARE)

        @block.scalar
        def _(act):
            def turned(it, k, n):
                act.wait_ge(xT_done, n + 1)
                if past(n, 2):
                    act.wait_ge(logits_done, n - 1)
                nc.scalar.copy(xfT[:, k % 2], ps_xT[:, k % 2, 0:DC]).then_inc(xfT_done, 1)

            def normalise_again(it, k, n):
                s = k // TILES
                if k % TILES == 0 and past(it):
                    act.wait_ge(tab_out[s], 16 * it)
                act.wait_ge(shift_done, it * (STEP // GROUP) + (k // GROUP + 1))
                nc.scalar.activation(tab[:, k, 0:D], xf[:, k], ACT.Identity, bias=shift[:, k:k + 1],
                                     scale=rstd[:, 1, k:k + 1]).then_inc(yn_done, 1)

            def turned_logits(it, k, n):
                group = it * (STEP // LGROUP) + k // LGROUP
                act.wait_ge(logits_done, n + 1)
                if past(group, 2):
                    act.wait_ge(back_done, group - 1)
                nc.scalar.copy(lT[:, (k // LGROUP) % 2], ps_lT[0:E, (k // LGROUP) % 2]).then_inc(lT_done, 1)

            def exponential(it, k, n):
                s = k // TILES
                act.wait_ge(lcen_done, it * SEQS + (s + 1))
                if past(n, TILES):
                    act.wait_ge(gate_done, it * SEQS + s)
                nc.scalar.activation(lexp[:], lcen[:], ACT.Exp).then_inc(lexp_done, 1)

            def scores(it, k, n):
                s = k // TILES
                act.wait_ge(gate_done, it * SEQS + (s + 1))
                if past(it):
                    act.wait_ge(tab_out[s], 16 * it)
                nc.scalar.copy(tab[:, tiles_of(s), D:ROW], gate[:, bass.ds(it * STEP + s * TILES, TILES), :]
                               ).then_inc(scores_done, TILES)

            def body(it, j):
                tile = flow.at(it, j, TURN)
                if tile:
                    turned(*tile)
                tile = flow.at(it, j, LOGITS)
                if tile and tile[1] % LGROUP == LGROUP - 1:
                    turned_logits(*tile)
                tile = flow.at(it, j, NORM2)
                if tile:
                    normalise_again(*tile)
                for stage, lag in ((exponential, CENTRE), (scores, SHARE)):
                    tile = flow.at(it, j, lag)
                    if tile and tile[1] % TILES == TILES - 1:
                        stage(*tile)

            flow.run(act, body, SHARE)

        @block.tensor
        def _(pe):
            def project_tile(it, k, n):
                s, i = k // TILES, k % TILES
                if i % (TILES // 2) == 0:
                    pe.wait_ge(o_done, 2 * DC * SEQS * it + DC * (2 * s + i // (TILES // 2) + 1))
                if past(n, 2):
                    pe.wait_ge(x2_done, n - 1)
                for ch in range(DC):
                    nc.tensor.matmul(ps_y[:, k % 2, 0:D], o[:, s, ch, i * P:(i + 1) * P], w[:, ch],
                                     start=(ch == 0), stop=False)
                nc.tensor.matmul(ps_y[:, k % 2, 0:D], ones[:], bo_rows[:], start=False, stop=True).then_inc(y_done, 1)

            def turn(it, k, n):
                pe.wait_ge(xf_done, n + 1)
                if past(n, 2):
                    pe.wait_ge(xfT_done, n - 1)
                for c in range(DC):
                    mm = nc.tensor.transpose(ps_xT[:, k % 2, c], xf[:, k, c * P:(c + 1) * P], ident[:])
                mm.then_inc(xT_done, 1)

            def logits(it, k, n):
                group = it * (STEP // LGROUP) + k // LGROUP
                i = k % LGROUP
                pe.wait_ge(xfT_done, n + 1)
                if i == 0 and past(group, 2):
                    pe.wait_ge(lT_done, group - 1)
                for c in range(DC):
                    mm = nc.tensor.matmul(ps_lT[0:E, (k // LGROUP) % 2, i * P:(i + 1) * P], wg[:, c], xfT[:, k % 2, c],
                                          start=(c == 0), stop=(c == DC - 1))
                mm.then_inc(logits_done, 1)

            def turn_back(it, k, n):
                s = k // TILES
                pe.wait_ge(lT_done, it * (STEP // LGROUP) + (k // LGROUP + 1))
                if k % TILES < LGROUP and past(it):
                    pe.wait_ge(lcen_done, it * SEQS + (s + 1 - SEQS))
                for t in range(LGROUP):
                    i = k % TILES + 1 - LGROUP + t
                    mm = nc.tensor.matmul(ps_l[:, s, i * E:(i + 1) * E], lT[:, (k // LGROUP) % 2, t * P:(t + 1) * P],
                                          ident[0:E, 0:E], start=True, stop=True)
                mm.then_inc(back_done, 1)

            def body(it, j):
                for stage, lag in ((project_tile, PROJ), (turn, TURN), (logits, LOGITS)):
                    tile = flow.at(it, j, lag)
                    if tile:
                        stage(*tile)
                tile = flow.at(it, j, BACK)
                if tile and tile[1] % LGROUP == LGROUP - 1:
                    turn_back(*tile)

            pe.wait_ge(consts_in, 64)
            pe.wait_ge(set_up, 3)
            pe.wait_ge(bias_done, 3 * PARTS)
            flow.run(pe, body, BACK)


ROUNDS = 15
LEVELS = 4
UNROLL = 5


def choose(nc, gate, consts, places_hi, places_lo):
    GROUP = TOK // 16
    GC = GROUP // P
    with ExitStack() as ctx:
        a = Alloc(nc, ctx)
        ident = a.sb("c_ident", [P, P])
        same = a.sb("c_same", [P, P])
        before = a.sb("c_before", [P, P])
        bits = a.sb("c_bits", [P, ROUNDS, LEVELS], I32)
        by_group = a.sb("c_by_group", [P, GC, E, 16])
        score = a.sb("c_score", [P, GROUP])
        mark = a.sb("c_mark", [P, LEVELS - 1, GROUP], BF16)
        zeros = a.sb("c_zeros", [P, GROUP])
        best = a.sb("c_best", [P, 1])
        cand = a.sb("c_cand", [P, LEVELS])
        count = a.sb("c_count", [P, LEVELS - 1])
        above = a.sb("c_above", [P, GROUP])
        n_above = a.sb("c_n_above", [P, 1])
        equal = a.sb("c_equal", [P, GROUP])
        rank = a.sb("c_rank", [P, GROUP])
        need = a.sb("c_need", [P, 1])
        limit = a.sb("c_limit", [P, 1])
        taken = a.sb("c_taken", [P, GROUP])
        chosen = a.sb("c_chosen", [P, GROUP])
        place = a.sb("c_place", [P, GROUP])
        offset = a.sb("c_offset", [P, 1])
        marked = a.sb("c_marked", [P, GROUP])
        place_i = a.sb("c_place_i", [P, GROUP], I32)
        hi_i = a.sb("c_hi_i", [P, GROUP], I32)
        lo_i = a.sb("c_lo_i", [P, GROUP], I32)
        ps_t = a.ps("c_ps_t", [P, GC, P])
        ps_c = a.ps("c_ps_c", [P, 512])
        ps_p = a.ps("c_ps_p", [P, GC, P])

        consts_in = a.sem("c_consts_in")
        grouped = a.sem("c_grouped")
        turned = a.sem("c_turned")
        counted = a.sem("c_counted")
        totals = a.sem("c_totals")
        step = a.sem("c_step")
        block = ctx.enter_context(nc.Block())

        @block.sync
        def _(sp):
            for buf, name in ((ident, "ident"), (same, "same"), (before, "before"), (bits, "bits")):
                sp.dma_start(buf[:], consts[name]).then_inc(consts_in, 16)

        @block.tensor
        def _(pe):
            pe.wait_ge(consts_in, 64)
            pe.wait_ge(grouped, GC)
            for c in range(GC):
                mm = nc.tensor.transpose(ps_t[:, c], by_group[:, c].rearrange("p e g -> p (e g)"), ident[:])
            mm.then_inc(turned, 1)
            with pe.Fori(0, ROUNDS // UNROLL) as k:
                for u in range(UNROLL):
                    pe.wait_ge(counted, k * UNROLL + (u + 1))
                    nc.tensor.matmul(ps_c[:, 0:LEVELS - 1], same[:], count[:], start=True, stop=True
                                     ).then_inc(totals, 1)
            pe.wait_ge(counted, ROUNDS + 1)
            nc.tensor.matmul(ps_c[:, 0:1], same[:], n_above[:], start=True, stop=True).then_inc(totals, 1)
            pe.wait_ge(counted, ROUNDS + 2)
            nc.tensor.matmul(ps_c[:, 0:1], before[:], rank[:, GROUP - 1:GROUP], start=True, stop=True
                             ).then_inc(totals, 1)
            pe.wait_ge(counted, ROUNDS + 3)
            nc.tensor.matmul(ps_c[:, 0:1], before[:], place[:, GROUP - 1:GROUP], start=True, stop=True
                             ).then_inc(totals, 1)
            pe.wait_ge(counted, ROUNDS + 4)
            for c in range(GC):
                mm = nc.tensor.transpose(ps_p[:, c], marked[:, c * P:(c + 1) * P], ident[:])
            mm.then_inc(turned, 1)

        @block.vector
        def _(dve):
            for c in range(GC):
                nc.vector.tensor_copy(by_group[:, c], gate[:].rearrange("p (g c) e -> p c e g", c=GC)[:, c]
                                      ).then_inc(grouped, 1)
            nc.vector.memset(zeros[:], 0.0).then_inc(step, 1)
            nc.vector.memset(best[:], 0.0).then_inc(step, 1)
            dve.wait_ge(consts_in, 64)
            dve.wait_ge(turned, 1)
            nc.vector.tensor_copy(score[:], ps_t[:].rearrange("p c n -> p (c n)")).then_inc(step, 1)
            SET_UP, EACH = 3, LEVELS + 2
            def search(r):
                done = r * EACH + SET_UP
                dve.wait_ge(step, done)
                nc.vector.tensor_tensor(cand[:].bitcast(I32), bits[:, bass.ds(r, 1), :].rearrange("p o l -> p (o l)"),
                                        best[:].bitcast(I32).to_broadcast([P, LEVELS]), ALU.bitwise_or).then_inc(step, 1)
                dve.wait_ge(step, done + 1)
                for v in range(1, LEVELS):
                    nc.vector.tensor_scalar(mark[:, v - 1], score[:], cand[:, v:v + 1], 0.0, ALU.is_ge, ALU.add,
                                            accum_out=count[:, v - 1:v]).then_inc(step if v < LEVELS - 1 else counted, 1)
                dve.wait_ge(totals, r + 1)
                nc.vector.scalar_tensor_tensor(out=cand[:, 1:], in0=ps_c[:, 0:LEVELS - 1], scalar=float(K),
                                               in1=cand[:, 1:], op0=ALU.is_ge, op1=ALU.mult).then_inc(step, 1)
                dve.wait_ge(step, done + LEVELS)
                nc.vector.tensor_reduce(best[:], cand[:], AX.X, ALU.max).then_inc(step, 2)

            with dve.Fori(0, ROUNDS // UNROLL) as k:
                for u in range(UNROLL):
                    search(k * UNROLL + u)
            done = ROUNDS * EACH + SET_UP
            dve.wait_ge(step, done)
            nc.vector.tensor_scalar(above[:], score[:], best[:], 0.0, ALU.is_gt, ALU.add, accum_out=n_above[:]
                                    ).then_inc(counted, 1)
            nc.vector.tensor_scalar(equal[:], score[:], best[:], None, ALU.is_equal).then_inc(step, 1)
            dve.wait_ge(step, done + 1)
            nc.vector.tensor_tensor_scan(rank[:], equal[:], zeros[:], 0.0, ALU.add, ALU.add).then_inc(step, 1)
            dve.wait_ge(totals, ROUNDS + 1)
            nc.vector.tensor_scalar(need[:], ps_c[:, 0:1], -1.0, float(K), ALU.mult, ALU.add).then_inc(step, 1)
            dve.wait_ge(step, done + 3)
            nc.vector.tensor_copy(offset[:], need[:]).then_inc(counted, 1)
            dve.wait_ge(totals, ROUNDS + 2)
            nc.vector.tensor_tensor(limit[:], need[:], ps_c[:, 0:1], ALU.subtract).then_inc(step, 1)
            dve.wait_ge(step, done + 4)
            nc.vector.scalar_tensor_tensor(out=taken[:], in0=rank[:], scalar=limit[:], in1=equal[:],
                                           op0=ALU.is_le, op1=ALU.mult).then_inc(step, 1)
            dve.wait_ge(step, done + 5)
            dve.wait_ge(counted, ROUNDS + 2)
            nc.vector.tensor_tensor(chosen[:], taken[:], above[:], ALU.add).then_inc(step, 1)
            dve.wait_ge(step, done + 6)
            nc.vector.tensor_tensor_scan(place[:], chosen[:], zeros[:], 0.0, ALU.add, ALU.add).then_inc(counted, 1)
            dve.wait_ge(totals, ROUNDS + 3)
            nc.vector.tensor_copy(offset[:], ps_c[:, 0:1]).then_inc(step, 1)
            dve.wait_ge(step, done + 7)
            dve.wait_ge(counted, ROUNDS + 3)
            nc.vector.scalar_tensor_tensor(out=marked[:], in0=place[:], scalar=offset[:], in1=chosen[:],
                                           op0=ALU.add, op1=ALU.mult).then_inc(counted, 1)
            dve.wait_ge(turned, 2)
            nc.vector.tensor_scalar(place_i[:], ps_p[:].rearrange("p c n -> p (c n)"), -1.0, None, ALU.add
                                    ).then_inc(step, 1)
            dve.wait_ge(step, done + 8)
            nc.vector.tensor_scalar(hi_i[:], place_i[:], 7, None, ALU.arith_shift_right).then_inc(step, 1)
            nc.vector.tensor_scalar(lo_i[:], place_i[:], P - 1, None, ALU.bitwise_and).then_inc(step, 1)
            dve.wait_ge(step, done + 10)
            for to, of in ((places_hi, hi_i), (places_lo, lo_i)):
                for c in range(GC):
                    nc.vector.tensor_copy(to[:].rearrange("p e (g c) -> p c e g", c=GC)[:, c],
                                          of[:].rearrange("p (c e g) -> p c e g", c=GC, e=E)[:, c]).then_inc(step, 1)
            dve.wait_ge(step, done + 10 + 2 * GC)


def experts(nc, table, consts, fc1, fc2, b1, b2, ln_w, ln_b, places_hi, places_lo, out):
    TT = TOK // P
    KT = K // P
    HK = KT // 2
    WIDE = HK * P
    with ExitStack() as ctx:
        a = Alloc(nc, ctx)
        ident = a.sb("e_ident", [P, P])
        iota = a.sb("e_iota", [P, P])
        iota16 = a.sb("e_iota16", [P, P], BF16)
        tile_no = a.sb("e_tile_no", [P, TT, KT])
        row_no = a.sb("e_row_no", [P, 1])
        lnw = a.sb("e_lnw", [P, DC])
        lnb = a.sb("e_lnb", [P, DC])
        hi = a.sb("e_hi", [P, TT])
        lo = a.sb("e_lo", [P, TT])
        at_lo = a.sb("e_at_lo", [P, TT, P], BF16)
        at_hi = a.sb("e_at_hi", [P, TT, KT])
        number = a.sb("e_number", [P, TT, 2, KT], BF16)
        rows_p = a.sb("e_rows_p", [P, KT])
        idx = a.sb("e_idx", [P, 2, KT], U32)
        y = a.sb("e_y", [P, KT, ROW])
        wk = a.sb("e_wk", [P, 2, KT])
        yT = a.sb("e_yT", [P, 2, WIDE])
        yT_high = a.sb("e_yT_high", [P, DC, K], F32R)
        yT_low = a.sb("e_yT_low", [P, DC, K], F32R)
        w1 = a.sb("e_w1", [P, DC, FF])
        w1_high = a.sb("e_w1_high", [P, DC, FF], F32R)
        w1_low = a.sb("e_w1_low", [P, DC, FF], F32R)
        w2 = a.sb("e_w2", [P, FC, D])
        w2_high = a.sb("e_w2_high", [P, FC, D], F32R)
        w2_low = a.sb("e_w2_low", [P, FC, D], F32R)
        hT = a.sb("e_hT", [P, 4, WIDE])
        hT_high = a.sb("e_hT_high", [P, FC, K], F32R)
        hT_low = a.sb("e_hT_low", [P, FC, K], F32R)
        b1b = a.sb("e_b1b", [P, 2, FC])
        b2b = a.sb("e_b2b", [P, 2, D])
        biased = a.sb("e_biased", [P, 2, D])
        ob = a.sb("e_ob", [P, KT, D])
        ahead = a.sb("e_ahead", [P, 1])
        ps_h = a.ps("e_ps_h", [P, 3, WIDE])
        ps_o = a.ps("e_ps_o", [P, 2, 512])
        ps_y = a.ps("e_ps_y", [P, 2, WIDE])
        ps_i = a.ps("e_ps_i", [P, 512])

        consts_in = a.sem("e_consts_in")
        w1_in = a.sem("e_w1_in")
        w2_in = a.sem("e_w2_in")
        gathered = [a.sem(f"e_gathered{k}") for k in range(2)]
        scattered = a.sem("e_scattered")
        iota_done = a.sem("e_iota_done")
        cur_done = a.sem("e_cur_done")
        at_hi_done = a.sem("e_at_hi_done")
        onehots_done = a.sem("e_onehots_done")
        listed = a.sem("e_listed")
        rows_p_done = a.sem("e_rows_p_done")
        idx_done = a.sem("e_idx_done")
        wk_done = a.sem("e_wk_done")
        turned = a.sem("e_turned")
        yT_done = a.sem("e_yT_done")
        yT_high_done = a.sem("e_yT_high_done")
        yT_low_done = a.sem("e_yT_low_done")
        w1_high_done = a.sem("e_w1_high_done")
        w1_low_done = a.sem("e_w1_low_done")
        w2_high_done = a.sem("e_w2_high_done")
        w2_low_done = a.sem("e_w2_low_done")
        hT_high_done = a.sem("e_hT_high_done")
        hT_low_done = a.sem("e_hT_low_done")
        h_done = a.sem("e_h_done")
        gelu_done = a.sem("e_gelu_done")
        o_done = a.sem("e_o_done")
        biased_done = a.sem("e_biased_done")
        ob_done = a.sem("e_ob_done")
        ahead_done = a.sem("e_ahead_done")
        block = ctx.enter_context(nc.Block())

        ONEHOTS = TT + 2
        LISTED_AT = 6
        GROUPS = 2 * DC
        HG = 2 * FC
        out_rows = out.rearrange("b n d -> (b n) d")

        def group_of(buf, g):
            return buf[:, g % FC, (g // FC) * WIDE:(g // FC + 1) * WIDE]

        def each(eng, step):
            for k in range(2):
                step(k, k, 2)
            with eng.Fori(1, E // 2 - 1) as it:
                for k in range(2):
                    step(it * 2 + k, k, 2)
            step(E - 2, 0, 1)
            step(E - 1, 1, 0)

        @block.sync
        def _(sp):
            def load(e, k):
                if past(e):
                    sp.wait_ge(w1_low_done, e)
                sp.dma_start(w1[:], fc1[bass.ds(e, 1)].rearrange("o (c p) f -> p (o c) f", p=P)).then_inc(w1_in, 16)
                if past(e, 2):
                    sp.wait_ge(gelu_done, HG * (e - 1))
                sp.dma_start(b1b[:, k], b1[bass.ds(e, 1)].rearrange("o p f -> (o p) f")).then_inc(w1_in, 16)
                if past(e):
                    sp.wait_ge(w2_low_done, e)
                sp.dma_start(w2[:], fc2[bass.ds(e, 1)].rearrange("o (c p) d -> p (o c) d", p=P)).then_inc(w2_in, 16)
                if past(e, 2):
                    sp.wait_ge(biased_done, KT * (e - 1))
                sp.dma_start(b2b[:, k], b2[bass.ds(e, 1)].to_broadcast([P, D])).then_inc(w2_in, 16)

            for buf, src in ((ident, consts["ident"]), (iota, consts["iota"]), (tile_no, consts["tile_no"]),
                             (row_no, consts["row_no"]), (lnw, ln_w), (lnb, ln_b)):
                sp.dma_start(buf[:], src).then_inc(consts_in, 16)
            for k in range(2):
                load(k, k)
            with sp.Fori(1, E // 2) as it:
                for k in range(2):
                    load(it * 2 + k, k)
            sp.wait_ge(scattered, 16 * KT * E)

        @block.vector
        def _(dve):
            def begin_list(e):
                if past(e):
                    dve.wait_ge(onehots_done, ONEHOTS * e)
                nc.vector.tensor_copy(hi[:], places_hi[:, bass.ds(e, 1)].rearrange("p o t -> p (o t)")).then_inc(cur_done, 1)
                nc.vector.tensor_copy(lo[:], places_lo[:, bass.ds(e, 1)].rearrange("p o t -> p (o t)")).then_inc(cur_done, 1)
                dve.wait_ge(cur_done, 2 * (e + 1))
                if past(e):
                    dve.wait_ge(listed, e)
                nc.vector.tensor_tensor(at_hi[:], hi[:].unsqueeze(2).to_broadcast([P, TT, KT]),
                                        iota[:, 0:KT].unsqueeze(1).to_broadcast([P, TT, KT]), ALU.is_equal
                                        ).then_inc(at_hi_done, 1)
                dve.wait_ge(at_hi_done, e + 1)
                nc.vector.tensor_tensor(number[:, :, 0], at_hi[:], tile_no[:], ALU.mult).then_inc(onehots_done, 1)
                nc.vector.tensor_scalar(number[:, :, 1], at_hi[:], row_no[:], None, ALU.mult).then_inc(onehots_done, 1)

            def onehots(tiles):
                for t in tiles:
                    nc.vector.tensor_scalar(at_lo[:, t], iota16[:], lo[:, t:t + 1], None, ALU.is_equal
                                            ).then_inc(onehots_done, 1)

            def indices(e, k):
                dve.wait_ge(listed, e + 1)
                if past(e):
                    dve.wait_ge(idx_done, e)
                nc.vector.tensor_copy(rows_p[:], ps_i[:, KT:2 * KT]).then_inc(rows_p_done, 1)
                dve.wait_ge(rows_p_done, e + 1)
                if past(e, 2):
                    dve.wait_ge(scattered, 16 * KT * (e - 1))
                nc.vector.scalar_tensor_tensor(out=idx[:, k], in0=ps_i[:, 0:KT], scalar=float(P), in1=rows_p[:],
                                               op0=ALU.mult, op1=ALU.add).then_inc(idx_done, 1)

            def affine(e, k, h):
                if past(e) and h == 0:
                    dve.wait_ge(h_done, HG * e)
                half = [(c, GROUPS * e + h * DC + c, (slice(None), c, slice(h * WIDE, (h + 1) * WIDE))) for c in range(DC)]
                for c, n, part in half:
                    dve.wait_ge(turned, n + 1)
                    if past(e) or h > 0:
                        dve.wait_ge(yT_low_done, n - 1)
                    nc.vector.tensor_scalar(yT[:, c], ps_y[:, c], lnw[:, c:c + 1], lnb[:, c:c + 1],
                                            ALU.mult, ALU.add).then_inc(yT_done, 1)
                for c, n, part in half:
                    dve.wait_ge(yT_done, n + 1)
                    nc.vector.tensor_copy(yT_high[part], yT[:, c]).then_inc(yT_high_done, 1)
                for c, n, part in half:
                    dve.wait_ge(yT_high_done, n + 1)
                    nc.vector.tensor_tensor(yT_low[part], yT[:, c], yT_high[part], ALU.subtract
                                            ).then_inc(yT_low_done, 1)
                if h == 1:
                    for g in range(2):
                        dve.wait_ge(gathered[g], 16 * HK * (e + 1))
                    nc.vector.tensor_copy(wk[:, k], y[:, :, bass.ds(e + D, 1)].rearrange("p t o -> p (t o)")
                                          ).then_inc(wk_done, 1)

            def cut_w1(e):
                dve.wait_ge(w1_in, 32 * (e + 1))
                if past(e):
                    dve.wait_ge(h_done, HG * e)
                nc.vector.tensor_copy(w1_high[:], w1[:]).then_inc(w1_high_done, 1)

            def cut_w2(e):
                dve.wait_ge(w2_in, 32 * (e + 1))
                if past(e):
                    dve.wait_ge(o_done, KT * e)
                nc.vector.tensor_copy(w2_high[:], w2[:]).then_inc(w2_high_done, 1)

            def low_hidden(e, g):
                dve.wait_ge(hT_high_done, HG * e + g + 1)
                nc.vector.tensor_tensor(group_of(hT_low, g), hT[:, g % 4], group_of(hT_high, g), ALU.subtract
                                        ).then_inc(hT_low_done, 1)

            def weigh(e, k, i):
                if i == 0:
                    dve.wait_ge(wk_done, e + 1)
                if i < KT:
                    dve.wait_ge(o_done, KT * e + i + 1)
                    if past(e) or i >= 2:
                        dve.wait_ge(ob_done, KT * e + i - 1)
                    nc.vector.tensor_tensor(biased[:, i % 2], ps_o[:, i % 2, 0:D], b2b[:, k], ALU.add
                                            ).then_inc(biased_done, 1)
                if i > 0:
                    dve.wait_ge(biased_done, KT * e + i)
                    if past(e):
                        dve.wait_ge(scattered, 16 * KT * e)
                    nc.vector.tensor_scalar(ob[:, i - 1], biased[:, (i - 1) % 2], wk[:, k, i - 1:i], None, ALU.mult
                                            ).then_inc(ob_done, 1)

            def step(e, k, follow):
                cut_w2(e)
                for g in range(HG):
                    low_hidden(e, g)
                    if g == LISTED_AT and follow > 0:
                        indices(e + 1, 1 - k)
                if follow > 0:
                    cut_w1(e + 1)
                if follow > 1:
                    begin_list(e + 2)
                for i in range(KT + 1):
                    weigh(e, k, i)
                    if i in (HK - 1, HK + 1) and follow > 0:
                        affine(e + 1, 1 - k, (i - HK + 1) // 2)
                    if i < KT and follow > 1:
                        onehots(range(i * TT // KT, (i + 1) * TT // KT))

            dve.wait_ge(consts_in, 16 * 6)
            nc.vector.tensor_copy(iota16[:], iota[:]).then_inc(iota_done, 1)
            dve.wait_ge(iota_done, 1)
            begin_list(0)
            onehots(range(TT))
            indices(0, 0)
            cut_w1(0)
            begin_list(1)
            onehots(range(TT))
            for h in range(2):
                affine(0, 0, h)
            each(dve, step)

        @block.gpsimd
        def _(pool):
            def carry_waits(n):
                if past(n):
                    pool.wait_ge(ahead_done, n)
                nc.gpsimd.tensor_tensor(ahead[:], row_no[:], row_no[:], ALU.add).then_inc(ahead_done, 1)

            def gather(e, k, first):
                pool.wait_ge(idx_done, e + 1)
                if past(e):
                    pool.wait_ge(turned, GROUPS * e)
                    pool.wait_ge(wk_done, e)
                carry_waits(first)
                for i in range(KT):
                    nc.gpsimd.indirect_dma_start(
                        out=y[:, i], out_offset=None, in_=table,
                        in_offset=bass.IndirectOffsetOnAxis(ap=idx[:, k, i:i + 1], axis=0)).then_inc(gathered[i // HK], 16)

            def low_w1(e):
                pool.wait_ge(w1_high_done, e + 1)
                nc.gpsimd.tensor_tensor(w1_low[:], w1[:], w1_high[:], ALU.subtract).then_inc(w1_low_done, 1)

            def step(e, k, follow):
                pool.wait_ge(w2_high_done, e + 1)
                nc.gpsimd.tensor_tensor(w2_low[:], w2[:], w2_high[:], ALU.subtract).then_inc(w2_low_done, 1)
                if follow > 0:
                    gather(e + 1, 1 - k, (KT + 1) * e + 1)
                if follow > 0:
                    low_w1(e + 1)
                if past(e):
                    pool.wait_ge(scattered, 16 * KT * e)
                for i in range(KT):
                    pool.wait_ge(ob_done, KT * e + i + 1)
                    carry_waits((KT + 1) * e + 1 + min(follow, 1) + i)
                    nc.gpsimd.indirect_dma_start(
                        out=out_rows, out_offset=bass.IndirectOffsetOnAxis(ap=idx[:, k, i:i + 1], axis=0),
                        in_=ob[:, i], in_offset=None, compute_op=ALU.add).then_inc(scattered, 16)

            pool.wait_ge(consts_in, 16 * 6)
            gather(0, 0, 0)
            low_w1(0)
            each(pool, step)

        @block.scalar
        def _(act):
            def step(e, k, follow):
                for g in range(HG):
                    n = HG * e + g
                    act.wait_ge(h_done, n + 1)
                    if past(e) or g >= 4:
                        act.wait_ge(hT_low_done, n - 3)
                    nc.scalar.activation(hT[:, g % 4], ps_h[:, g % 3], ACT.Gelu_apprx_tanh,
                                         bias=b1b[:, k, g % FC:g % FC + 1]).then_inc(gelu_done, 1)
                    act.wait_ge(gelu_done, n + 1)
                    if past(e):
                        act.wait_ge(o_done, KT * e)
                    nc.scalar.copy(group_of(hT_high, g), hT[:, g % 4]).then_inc(hT_high_done, 1)

            each(act, step)

        @block.tensor
        def _(pe):
            def list_tokens(e):
                pe.wait_ge(onehots_done, ONEHOTS * (e + 1))
                if past(e):
                    pe.wait_ge(idx_done, e)
                for t in range(TT):
                    mm = nc.tensor.matmul(ps_i[:, 0:2 * KT], at_lo[:, t], number[:, t].rearrange("p v k -> p (v k)"),
                                          start=(t == 0), stop=(t == TT - 1))
                mm.then_inc(listed, 1)

            def turn(e, h):
                pe.wait_ge(gathered[h], 16 * HK * (e + 1))
                for c in range(DC):
                    if past(e) or h > 0:
                        pe.wait_ge(yT_done, GROUPS * e + h * DC + c - 1)
                    for i in range(HK):
                        mm = nc.tensor.transpose(ps_y[:, c, i * P:(i + 1) * P],
                                                 y[:, h * HK + i, c * P:(c + 1) * P], ident[:])
                    mm.then_inc(turned, 1)

            def one_pass(to, weights, moving, first, last):
                return nc.tensor.matmul(to, weights, moving, start=first, stop=last)

            def hidden(e, k, groups):
                for g in groups:
                    h, f = g // FC, g % FC
                    cols, fs = slice(h * WIDE, (h + 1) * WIDE), slice(f * P, (f + 1) * P)
                    if f == 0:
                        pe.wait_ge(yT_low_done, GROUPS * e + DC * (h + 1))
                    if past(e) or g >= 3:
                        pe.wait_ge(gelu_done, HG * e + g - 2)
                    for c in range(DC):
                        one_pass(ps_h[:, g % 3], w1_high[:, c, fs], yT_high[:, c, cols], c == 0, False)
                        one_pass(ps_h[:, g % 3], w1_high[:, c, fs], yT_low[:, c, cols], False, False)
                        mm = one_pass(ps_h[:, g % 3], w1_low[:, c, fs], yT_high[:, c, cols], False, c == DC - 1)
                    mm.then_inc(h_done, 1)

            def outputs(e, k, tiles):
                for i in tiles:
                    cols = slice(i * P, (i + 1) * P)
                    if past(e) or i >= 2:
                        pe.wait_ge(biased_done, KT * e + i - 1)
                    for f in range(FC):
                        one_pass(ps_o[:, i % 2, 0:D], hT_high[:, f, cols], w2_high[:, f], f == 0, False)
                        one_pass(ps_o[:, i % 2, 0:D], hT_high[:, f, cols], w2_low[:, f], False, False)
                        mm = one_pass(ps_o[:, i % 2, 0:D], hT_low[:, f, cols], w2_high[:, f], False, f == FC - 1)
                    mm.then_inc(o_done, 1)

            def step(e, k, follow):
                pe.wait_ge(w1_low_done, e + 1)
                hidden(e, k, range(0, LISTED_AT))
                if follow > 0:
                    list_tokens(e + 1)
                hidden(e, k, range(LISTED_AT, HG))
                pe.wait_ge(w2_low_done, e + 1)
                pe.wait_ge(hT_low_done, HG * e + FC)
                outputs(e, k, range(0, HK))
                pe.wait_ge(hT_low_done, HG * (e + 1))
                for h, tiles in ((0, range(HK, HK + 2)), (1, range(HK + 2, KT))):
                    if follow > 0:
                        turn(e + 1, h)
                    outputs(e, k, tiles)

            pe.wait_ge(consts_in, 16 * 6)
            list_tokens(0)
            for h in range(2):
                turn(0, h)
            each(pe, step)


def block_kernel(nc, t, out):
    parts = nc.dram_tensor("qkv_parts", (B * H, 2, PARTS, DH, N), BF16).ap()
    values = nc.dram_tensor("values", (B, PAIRS, P, TILES * 2 * DH), F32).ap()
    o = nc.dram_tensor("attended", (NP, 2, HALVES, 2 * DH, CHUNK), F32).ap()
    rden = nc.dram_tensor("reciprocal_denominators", (B, P, P), F32).ap()
    table = nc.dram_tensor("token_table", (TOK, ROW), F32).ap()
    with ExitStack() as ctx:
        a = Alloc(nc, ctx)
        gate = a.sb("gate", [P, TOK // P, E])
        places_hi = a.sb("places_hi", [P, E, TOK // P])
        places_lo = a.sb("places_lo", [P, E, TOK // P])
        project(nc, t["x"], t["w_qkv"], t["rot_cos"], t["rot_sin"], t["ident"], parts, values)
        attend(nc, parts, values.rearrange("b r p n -> (b r) p n"), o, t["ident"])
        finish(nc, t["x"], o, rden, t["w_out"], t["b_out"], t["w_gate"], t["ident"], table, out, gate)
        choose(nc, gate, t, places_hi, places_lo)
        experts(nc, table, t, t["fc1"], t["fc2"], t["b1"], t["b2"], t["ln_w"], t["ln_b"], places_hi, places_lo, out)


def constants():
    i = np.arange(P)
    inv_freq = (1.0 / 10000.0 ** (np.arange(0, DH, 2, dtype=np.float32) / DH)).astype(np.float32)
    angle = np.outer(np.arange(N, dtype=np.float32), inv_freq).astype(np.float32)
    cos, sin = np.cos(angle), np.sin(angle)

    def by_tile(v):
        return v.reshape(TILES, P, DH).transpose(1, 0, 2)

    group = i // DH
    return {
        "ident": np.eye(P, dtype=np.float32),
        "rot_cos": by_tile(np.concatenate([cos, cos], -1)),
        "rot_sin": by_tile(np.concatenate([-sin, sin], -1)),
        "same": (group[:, None] == group[None]).astype(np.float32),
        "before": ((group[:, None] == group[None]) & (i[:, None] < i[None])).astype(np.float32),
        "bits": np.broadcast_to(np.array([[v << (2 * (ROUNDS - 1 - r)) for v in range(LEVELS)]
                                          for r in range(ROUNDS)], np.int32), (P, ROUNDS, LEVELS)),
        "iota": np.broadcast_to(i.astype(np.float32), (P, P)),
        "tile_no": np.broadcast_to(np.arange(TOK // P, dtype=np.float32)[None, :, None], (P, TOK // P, K // P)),
        "row_no": i.astype(np.float32)[:, None],
    }


def layout(L0_attn_x, L0_attn_Wq, L0_attn_Wkv, L0_attn_Wout, L0_attn_bout, L0_ffn_gate_w, L0_ffn_ln_w, L0_ffn_ln_b,
           L0_ffn_fc1s, L0_ffn_b1s, L0_ffn_fc2s, L0_ffn_b2s):
    return {
        "x": L0_attn_x,
        "w_qkv": np.concatenate([L0_attn_Wq, L0_attn_Wkv], axis=1),
        "w_out": L0_attn_Wout,
        "b_out": L0_attn_bout,
        "w_gate": L0_ffn_gate_w.T.reshape(DC, P, E).transpose(1, 0, 2),
        "ln_w": L0_ffn_ln_w.reshape(DC, P).T,
        "ln_b": L0_ffn_ln_b.reshape(DC, P).T,
        "fc1": L0_ffn_fc1s.transpose(0, 2, 1),
        "b1": L0_ffn_b1s.reshape(E, FC, P).transpose(0, 2, 1),
        "fc2": L0_ffn_fc2s.transpose(0, 2, 1),
        "b2": L0_ffn_b2s,
    }


def kernel(**inputs):
    import concourse.bacc as bacc
    from concourse.bass_utils import run_bass_kernel_spmd

    nc = bacc.Bacc("TRN2", target_bir_lowering=False, num_devices=1)
    arrays, aps = {}, {}
    for name, value in {**constants(), **layout(**{n: np.asarray(v) for n, v in inputs.items()})}.items():
        value = np.ascontiguousarray(value)
        arrays[f"in_{name}_dram"] = value
        aps[name] = nc.dram_tensor(f"in_{name}_dram", value.shape, mybir.dt.from_np(value.dtype),
                                   kind="ExternalInput").ap()
    out = nc.dram_tensor("out_0_dram", (B, N, D), F32, kind="ExternalOutput").ap()
    block_kernel(nc, aps, out)
    result = run_bass_kernel_spmd(nc, [arrays], core_ids=[0])
    return result.results[0]["out_0_dram"]
```
